# Optimizing a Trainium2 kernel written in Bass

```python
import numpy as np
import jax
import jax.numpy as jnp

def _softmax(x, axis=-1):
    return jax.nn.softmax(x, axis=axis)

def _gelu(x):
    return jax.nn.gelu(x, approximate=True)

def _silu(x):
    return jax.nn.silu(x)

def _sigmoid(x):
    return jax.nn.sigmoid(x)

def _layernorm(x, axis=-1, eps=1e-05):
    m = jnp.mean(x, axis=axis, keepdims=True)
    v = jnp.var(x, axis=axis, keepdims=True)
    return (x - m) / jnp.sqrt(v + eps)

def _scatter_add(tgt, idx, src, axis=0):
    return tgt.at[idx].add(src)

def _segment_sum(src, seg, n):
    return jax.ops.segment_sum(src, seg, n)
kernel_name = 'mk_seq_postln_d1_jaxref_r4_468aad'

def setup_inputs(seed: int=0):
    np.random.seed(seed)
    _w = jnp.asarray

    def _L0_attn_setup():
        import jax, jax.numpy as jnp
        import numpy as np
        DIM = 512
        HEADS = 16
        HEAD_DIM = DIM // HEADS
        RANK = 16
        ALPHA = 8.0
        SCALING = ALPHA / RANK
        SCALE = HEAD_DIM ** (-0.5)

        def lora_linear(x, W, b, Bm, Am):
            out = jnp.einsum('bld,od->blo', x, W) + b
            upd = jnp.einsum('blr,or->blo', jnp.einsum('bld,rd->blr', x, Bm), Am)
            return out + SCALING * upd

        def _split(t):
            B, L, D = t.shape
            return t.reshape(B, L, HEADS, HEAD_DIM).transpose(0, 2, 1, 3)
        key = jax.random.key(seed)
        ks = jax.random.split(key, 20)
        B, L = (4, 512)
        x = jax.random.normal(ks[0], (B, L, DIM), dtype=jnp.float32)
        s = 0.02
        inp = {'x': x}
        for i, name in enumerate(['q', 'k', 'v', 'o']):
            inp[f'W{name}'] = jax.random.normal(ks[1 + 4 * i], (DIM, DIM), jnp.float32) * s
            inp[f'b{name}'] = jax.random.normal(ks[2 + 4 * i], (DIM,), jnp.float32) * s
            inp[f'B{name}'] = jax.random.normal(ks[3 + 4 * i], (RANK, DIM), jnp.float32) * s
            inp[f'A{name}'] = jax.random.uniform(ks[4 + 4 * i], (DIM, RANK), jnp.float32, -0.1, 0.1)
        return inp
    _L0_attn_in = _L0_attn_setup()

    def _L0_ffn_setup():
        import jax, jax.numpy as jnp
        import numpy as np
        B, S, D = (4, 512, 512)
        E = 8
        H = 704
        CAP_F = 1.0

        def _moe(x, Wg, W1, W3, W2, sw1, sw3, sw2):
            b, sl, d = x.shape
            T = b * sl
            C = int(CAP_F * T / E)
            xt = x.reshape(T, d)
            probs = jax.nn.softmax(xt @ Wg, axis=-1)
            eidx = jnp.argmax(probs, axis=-1)
            gate = jnp.take_along_axis(probs, eidx[:, None], 1)[:, 0]
            oh = jax.nn.one_hot(eidx, E, dtype=jnp.int32)
            pos = (jnp.cumsum(oh, axis=0) * oh).sum(-1) - 1
            keep = pos < C
            flat = jnp.where(keep, eidx * C + pos, E * C)
            xd = jnp.zeros((E * C, d), x.dtype).at[flat].set(xt, mode='drop')
            xd = xd.reshape(E, C, d)
            h = jax.nn.silu(jnp.einsum('ecd,edh->ech', xd, W1)) * jnp.einsum('ecd,edh->ech', xd, W3)
            oe = jnp.einsum('ech,ehd->ecd', h, W2).reshape(E * C, d)
            out = jnp.take(oe, jnp.minimum(flat, E * C - 1), axis=0)
            out = out * (gate * keep.astype(x.dtype))[:, None]
            shared = jax.nn.silu(xt @ sw1) * (xt @ sw3) @ sw2
            return (out + shared).reshape(b, sl, d)
        key = jax.random.key(seed)
        ks = jax.random.split(key, 8)
        s = lambda fan: 1.0 / np.sqrt(fan)
        return {'x': jax.random.normal(ks[0], (B, S, D), jnp.float32), 'Wg': jax.random.normal(ks[1], (D, E), jnp.float32) * s(D), 'W1': jax.random.normal(ks[2], (E, D, H), jnp.float32) * s(D), 'W3': jax.random.normal(ks[3], (E, D, H), jnp.float32) * s(D), 'W2': jax.random.normal(ks[4], (E, H, D), jnp.float32) * s(H), 'sw1': jax.random.normal(ks[5], (D, H), jnp.float32) * s(D), 'sw3': jax.random.normal(ks[6], (D, H), jnp.float32) * s(D), 'sw2': jax.random.normal(ks[7], (H, D), jnp.float32) * s(H)}
    _L0_ffn_in = _L0_ffn_setup()
    _d = {'L0_attn_x': _L0_attn_in['x'], 'L0_attn_Wq': _L0_attn_in['Wq'], 'L0_attn_bq': _L0_attn_in['bq'], 'L0_attn_Bq': _L0_attn_in['Bq'], 'L0_attn_Aq': _L0_attn_in['Aq'], 'L0_attn_Wk': _L0_attn_in['Wk'], 'L0_attn_bk': _L0_attn_in['bk'], 'L0_attn_Bk': _L0_attn_in['Bk'], 'L0_attn_Ak': _L0_attn_in['Ak'], 'L0_attn_Wv': _L0_attn_in['Wv'], 'L0_attn_bv': _L0_attn_in['bv'], 'L0_attn_Bv': _L0_attn_in['Bv'], 'L0_attn_Av': _L0_attn_in['Av'], 'L0_attn_Wo': _L0_attn_in['Wo'], 'L0_attn_bo': _L0_attn_in['bo'], 'L0_attn_Bo': _L0_attn_in['Bo'], 'L0_attn_Ao': _L0_attn_in['Ao'], 'L0_ffn_Wg': _L0_ffn_in['Wg'], 'L0_ffn_W1': _L0_ffn_in['W1'], 'L0_ffn_W3': _L0_ffn_in['W3'], 'L0_ffn_W2': _L0_ffn_in['W2'], 'L0_ffn_sw1': _L0_ffn_in['sw1'], 'L0_ffn_sw3': _L0_ffn_in['sw3'], 'L0_ffn_sw2': _L0_ffn_in['sw2']}
    _x0 = _d['L0_attn_x']
    _d['L0_attn_x'] = jax.random.normal(jax.random.fold_in(jax.random.key(seed), 1), (2, 1024, 512), dtype=_x0.dtype)
    del _x0
    return _d

def reference(L0_attn_x, L0_attn_Wq, L0_attn_bq, L0_attn_Bq, L0_attn_Aq, L0_attn_Wk, L0_attn_bk, L0_attn_Bk, L0_attn_Ak, L0_attn_Wv, L0_attn_bv, L0_attn_Bv, L0_attn_Av, L0_attn_Wo, L0_attn_bo, L0_attn_Bo, L0_attn_Ao, L0_ffn_Wg, L0_ffn_W1, L0_ffn_W3, L0_ffn_W2, L0_ffn_sw1, L0_ffn_sw3, L0_ffn_sw2):

    def _L0_attn_ref(x, Wq, bq, Bq, Aq, Wk, bk, Bk, Ak, Wv, bv, Bv, Av, Wo, bo, Bo, Ao):
        import jax, jax.numpy as jnp
        import numpy as np
        DIM = 512
        HEADS = 16
        HEAD_DIM = DIM // HEADS
        RANK = 16
        ALPHA = 8.0
        SCALING = ALPHA / RANK
        SCALE = HEAD_DIM ** (-0.5)

        def lora_linear(x, W, b, Bm, Am):
            out = jnp.einsum('bld,od->blo', x, W) + b
            upd = jnp.einsum('blr,or->blo', jnp.einsum('bld,rd->blr', x, Bm), Am)
            return out + SCALING * upd

        def _split(t):
            B, L, D = t.shape
            return t.reshape(B, L, HEADS, HEAD_DIM).transpose(0, 2, 1, 3)
        q = _split(lora_linear(x, Wq, bq, Bq, Aq))
        k = _split(lora_linear(x, Wk, bk, Bk, Ak))
        v = _split(lora_linear(x, Wv, bv, Bv, Av))
        scores = jnp.einsum('bhqd,bhkd->bhqk', q, k) * SCALE
        attn = jax.nn.softmax(scores, axis=-1)
        out = jnp.einsum('bhqk,bhkd->bhqd', attn, v)
        B, H, L, hd = out.shape
        out = out.transpose(0, 2, 1, 3).reshape(B, L, H * hd)
        return lora_linear(out, Wo, bo, Bo, Ao)

    def _L0_ffn_ref(x, Wg, W1, W3, W2, sw1, sw3, sw2):
        import jax, jax.numpy as jnp
        import numpy as np
        B, S, D = (4, 512, 512)
        E = 8
        H = 704
        CAP_F = 1.0

        def _moe(x, Wg, W1, W3, W2, sw1, sw3, sw2):
            b, sl, d = x.shape
            T = b * sl
            C = int(CAP_F * T / E)
            xt = x.reshape(T, d)
            probs = jax.nn.softmax(xt @ Wg, axis=-1)
            eidx = jnp.argmax(probs, axis=-1)
            gate = jnp.take_along_axis(probs, eidx[:, None], 1)[:, 0]
            oh = jax.nn.one_hot(eidx, E, dtype=jnp.int32)
            pos = (jnp.cumsum(oh, axis=0) * oh).sum(-1) - 1
            keep = pos < C
            flat = jnp.where(keep, eidx * C + pos, E * C)
            xd = jnp.zeros((E * C, d), x.dtype).at[flat].set(xt, mode='drop')
            xd = xd.reshape(E, C, d)
            h = jax.nn.silu(jnp.einsum('ecd,edh->ech', xd, W1)) * jnp.einsum('ecd,edh->ech', xd, W3)
            oe = jnp.einsum('ech,ehd->ecd', h, W2).reshape(E * C, d)
            out = jnp.take(oe, jnp.minimum(flat, E * C - 1), axis=0)
            out = out * (gate * keep.astype(x.dtype))[:, None]
            shared = jax.nn.silu(xt @ sw1) * (xt @ sw3) @ sw2
            return (out + shared).reshape(b, sl, d)
        return _moe(x, Wg, W1, W3, W2, sw1, sw3, sw2)
    x = L0_attn_x
    x = _layernorm(x + _L0_attn_ref(x, L0_attn_Wq, L0_attn_bq, L0_attn_Bq, L0_attn_Aq, L0_attn_Wk, L0_attn_bk, L0_attn_Bk, L0_attn_Ak, L0_attn_Wv, L0_attn_bv, L0_attn_Bv, L0_attn_Av, L0_attn_Wo, L0_attn_bo, L0_attn_Bo, L0_attn_Ao), axis=-1)
    x = _layernorm(x + _L0_ffn_ref(x, L0_ffn_Wg, L0_ffn_W1, L0_ffn_W3, L0_ffn_W2, L0_ffn_sw1, L0_ffn_sw3, L0_ffn_sw2), axis=-1)
    return x

_drawn_inputs = setup_inputs


def setup_inputs(seed=0):
    import zlib

    import numpy as np

    out = dict(_drawn_inputs(seed))
    spreads = {}
    factors = {'L0_attn_Wq': 7.821,
     'L0_attn_bq': 8.0,
     'L0_attn_Bq': 8.0,
     'L0_attn_Aq': 8.0,
     'L0_attn_Wk': 7.75,
     'L0_attn_bk': 64.0,
     'L0_attn_Bk': 8.0,
     'L0_attn_Ak': 8.0,
     'L0_attn_Wv': 3.818,
     'L0_attn_bv': 3.614,
     'L0_attn_Bv': 8.0,
     'L0_attn_Av': 8.0,
     'L0_attn_Bo': 8.0,
     'L0_attn_Ao': 8.0,
     'L0_attn_bo': 4.918}
    for name, (base, spread) in spreads.items():
        noise = np.random.default_rng([zlib.crc32(name.encode()), seed]).standard_normal(out[name].shape)
        drawn = base * np.exp(spread * noise) if base else spread * noise
        out[name] = jnp.asarray(drawn.astype(out[name].dtype))
    for name, factor in factors.items():
        out[name] = (out[name] * factor).astype(out[name].dtype)
    return out
```

```python
from contextlib import ExitStack

import concourse.bass as bass
from concourse import mybir

F32 = mybir.dt.float32
FR = mybir.dt.float32r
BF16 = mybir.dt.bfloat16
U32 = mybir.dt.uint32
ACT = mybir.ActivationFunctionType
ALU = mybir.AluOpType
AX = mybir.AxisListType

P = 128
B, L, D = 2, 1024, 512
T = B * L
NT = T // P
DC = D // P
HEADS = 16
HD = D // HEADS
HG = P // HD
NG = HEADS // HG
RANK = 16
LORA = 8.0 / RANK
SCALE = float(HD) ** -0.5
HALF = 512
KC = L // P
E = 8
CAP = T // E
F = 704
FC = 6
FTAIL = F - 5 * P
EPS = 1e-5
SPLIT = ((0, 0), (0, 1), (1, 0))


class Arena:

    def __init__(self, nc, start, end):
        self.nc, self.at, self.end = nc, start, end

    def __call__(self, name, shape, dt):
        size = mybir.dt.size(dt)
        for n in shape[1:]:
            size *= n
        t = self.nc.alloc_sbuf_tensor_at(name, shape, dt, offset=self.at)
        self.at += (size + 31) // 32 * 32
        assert self.at <= self.end, (name, self.at, self.end)
        return t


class Chain:

    def __init__(self, eng, sem, base=0):
        self.eng, self.sem, self.base, self.k = eng, sem, base, 0

    def __call__(self, ins):
        ins.then_inc(self.sem, 1)
        self.k += 1
        self.eng.wait_ge(self.sem, self.base + self.k)


def proj_uses():
    return [("proj", m, hf) for m in range(3) for hf in range(2)] + [("vturn", 0), ("vturn", 1)]


def smax_uses():
    return [("smax", hh, qt, n) for hh in range(HG) for qt in range(HALF // P) for n in range(2)]


LAST_SMAX = smax_uses()[-1]
PRO_USES = proj_uses() + smax_uses() + [("mrow",)]


def slot_uses(slot, last):
    plan = [([], []) for _ in range(KC)]
    if not (last and slot == 3):
        uses = smax_uses()
        for kc, n in enumerate((5, 5, 5, 5, 5, 5, 2, 0)):
            mine = [uses.pop(0) for _ in range(n)]
            plan[kc][0].extend(mine[:2])
            plan[kc][1].extend(mine[2:])
        plan[7][0].append(("mrow",))
    if slot == 0 or (slot == 2 and not last):
        for kc, use in enumerate(proj_uses()):
            plan[kc][1].insert(0, use)
    return plan


def numbered(last):
    where, k = {}, 0
    for slot in range(4):
        for parts in slot_uses(slot, last):
            for part in parts:
                for use in part:
                    where[slot, use] = k
                    k += 1
    return where, k


G_USES = numbered(False)[1]
CONV_BEFORE = {1: ((13, 0),), 2: ((13, 1), (2, 0)), 3: ((13, 2), (2, 1)), 4: ((13, 3), (2, 2)), 5: ((13, 4), (2, 3))}
CONV_OWN = {0: ((13, 5), (2, 4)), 1: ((2, 5),)}


def tail(c):
    return 0 if c < FC - 1 else P - FTAIL


def emit(nc, ctx, x, W, bias, bo, Bm, Am, Wg, W1, W3, W2, sw1, sw3, sw2, out):
    sems = {}

    def sem(name):
        if name not in sems:
            sems[name] = ctx.enter_context(nc.semaphore(name))
        return sems[name]

    work = [ctx.enter_context(nc.psum_tensor(f"work{i}", [P, 512], F32)) for i in range(2)]
    pair = [ctx.enter_context(nc.psum_tensor(f"pair{i}", [P, 2, 512], F32)) for i in range(2)]
    ov = ctx.enter_context(nc.psum_tensor("ov", [P, 512], F32))
    dn = ctx.enter_context(nc.psum_tensor("dn", [P, 512], F32))
    bank = [work[0][:], work[1][:], pair[0][:, 0], pair[0][:, 1], pair[1][:, 0], pair[1][:, 1], ov[:], dn[:]]

    wt_d = nc.dram_tensor("wt_d", [4, 2, P, DC, D], F32).ap()
    attn_d = nc.dram_tensor("attn_d", [D, T], F32).ap()
    xd_d = nc.dram_tensor("xd_d", [E * CAP, D], F32).ap()
    oe_d = nc.dram_tensor("oe_d", [E * CAP, D], F32).ap()
    x_rows = x.rearrange("b l d -> (b l) d")
    out_rows = out.rearrange("b l d -> (b l) d")
    attn_cols = attn_d.rearrange("(c p) t -> p c t", p=P)

    keep = Arena(nc, (nc.sbuf_base + 31) // 32 * 32, nc.sbuf_usable_end)
    xT = [keep(f"xT{s}", [P, DC, T], FR) for s in ("hi", "lo")]
    ident = keep("ident", [P, P], F32)
    ones32 = keep("ones32", [P, HD], F32)
    tri = keep("tri", [P, P], BF16)
    allone = keep("allone", [P, P], BF16)
    zeros = keep("zeros", [P, D], F32)
    wg_raw = keep("wg_raw", [P, DC, E], F32)
    region = keep.at

    att = Arena(nc, region, nc.sbuf_usable_end)
    Qs = [att("Qs0", [P, HG, L], FR)]
    Ks = [att("Ks0", [P, HG, L], FR)]
    plane = [[att(f"plane_{m}{s}", [P, L], FR) for s in ("hi", "lo")] for m in "qk"]
    vT = att("vT", [P, L], F32)
    V = [att(f"V{i}", [P, KC, P], F32) for i in range(2)]
    Wsl = att("Wsl", [P, 3, 2, DC, P], FR)
    bcol = att("bcol", [P, 4], F32)
    mx = att("mx", [P, 16, 2], F32)
    nm = att("nm", [P, 16], F32)
    mrow = att("mrow", [16, P], FR)
    rden = att("rden", [P, HALF], F32)
    attn_sb = [att(f"attn_sb{i}", [P, HALF], F32) for i in range(2)]
    overlay = att.at
    Qs.append(att("Qs1", [P, HG, L], FR))
    Ks.append(att("Ks1", [P, HG, L], FR))
    prob = [att(f"prob{i}", [P, 2, HALF], F32) for i in range(4)]

    stp = Arena(nc, overlay, att.at)
    w_raw = [stp(f"w_raw{i}", [P, DC, D], F32) for i in range(2)]
    xin = [stp(f"xin{i}", [P, D], F32) for i in range(4)]
    w_stage = [[stp(f"w_stage{i}{s}", [P, D], FR) for s in ("hi", "lo")] for i in range(2)]
    lora_a = stp("lora_a", [P, 4, DC, RANK], F32)
    lora_b = stp("lora_b", [P, D], F32)
    lora_at = stp("lora_at", [P, D], F32)

    ffn = Arena(nc, region, nc.sbuf_usable_end)
    rows = ffn("rows", [P, NT, D], F32)
    raw13 = [ffn(f"raw13_{i}", [P, 2, DC, P], F32) for i in range(2)]
    raw2 = [ffn(f"raw2_{i}", [P, D], F32) for i in range(2)]
    r3 = {n: ffn(f"r3_{n}", [P, NT, E], F32) for n in ("lg", "d", "ex", "c", "oh", "s0", "s1", "io")}
    r2 = {n: ffn(f"r2_{n}", [P, NT], F32) for n in ("mx", "sm", "gate", "em", "ps", "keep", "flat", "t", "u", "gk")}
    oh_bf = ffn("oh_bf", [P, NT, E], BF16)
    sidx = ffn("sidx", [P, NT], U32)
    gidx = ffn("gidx", [P, NT], U32)
    st6 = ffn("st6", [P, 4, 6], F32)
    mv = ffn("mv", [P, 4, 2], F32)
    ln_v, ln_s, ln_r, ln_t = (ffn(f"ln_{n}", [P, 4], F32) for n in "vsrt")
    w2_at = ffn.at
    w2 = [ffn(f"w2{s}", [P, FC, D], FR) for s in ("hi", "lo")]
    w13_at = ffn.at
    w13 = [ffn(f"w13{s}", [P, 2 * FC - 1, DC, P], FR) for s in ("hi", "lo")]
    sa = [ffn(f"sa{i}", [P, 512], F32) for i in range(2)]
    hid = [[ffn(f"hid{i}{s}", [P, 512], FR) for s in ("hi", "lo")] for i in range(2)]
    oe_sb = [ffn(f"oe_sb{i}", [P, D], F32) for i in range(2)]
    xdi = sa

    prj = Arena(nc, w2_at, w13_at)
    wo = [prj(f"wo{s}", [P, DC, D], FR) for s in ("hi", "lo")]
    bo_bc = prj("bo_bc", [P, D], F32)
    xr = [prj(f"xr{i}", [P, D], F32) for i in range(2)]
    prj2 = Arena(nc, w13_at, ffn.at)
    at_in = [prj2(f"at_in{i}", [P, DC, P], F32) for i in range(2)]
    at = [[prj2(f"at{i}{s}", [P, DC, P], FR) for s in ("hi", "lo")] for i in range(2)]
    x1b = [prj2(f"x1b{i}", [P, D], F32) for i in range(4)]
    wgp = [prj2(f"wgp{s}", [P, DC, P], FR) for s in ("hi", "lo")]
    yb = [prj2(f"yb{i}", [P, D], F32) for i in range(4)]
    lgT = prj2("lgT", [E, T], F32)
    cmb = Arena(nc, w2_at, w13_at)
    got = [cmb(f"got{i}", [P, D], F32) for i in range(8)]

    block = ctx.enter_context(nc.Block())

    def f32(ap):
        return ap.bitcast(F32)

    def cols(i, j):
        return bass.ds(i * 512 + j * P, P)

    def up_cols(wd, c):
        return wd.rearrange("(c p) h -> p c h", p=P)[:, :, c * P:min((c + 1) * P, F)]

    @block.sync
    def _(sp):
        def value(e):
            return e if isinstance(e, int) else sp.snap(e)

        def load_w(m):
            if m >= 2:
                sp.wait_ge(sem("w_mm"), DC * (m - 1))
            sp.dma_start(w_raw[m % 2][:], W[m].rearrange("(c p) d -> p c d", p=P)).then_inc(sem(f"w_ld{m % 2}"), 16)

        for m in range(4):
            sp.dma_start(lora_b[32 * m:32 * m + RANK, :], Bm[m]).then_inc(sem("lora_ld"), 16)
            sp.dma_start(lora_a[:, m], Am[m].rearrange("(c p) r -> p c r", p=P)).then_inc(sem("lora_ld"), 16)
        load_w(0)
        load_w(1)
        for j in range(4):
            sp.dma_start(xin[j][:], x_rows[j * P:(j + 1) * P, :]).then_inc(sem(f"x_ld{j}"), 16)
        load_w(2)
        with sp.Fori(1, 4) as i:
            for j in range(4):
                r, need = value(i * 512 + j * P), value(i * 4 + (j - 3))
                sp.wait_ge(sem("x_t"), need)
                sp.dma_start(xin[j][:], x_rows[bass.ds(r, P), :]).then_inc(sem(f"x_ld{j}"), 16)
        load_w(3)
        sp.dma_start(wg_raw[:], Wg.rearrange("(c p) e -> p c e", p=P)).then_inc(sem("wg_ld"), 16)

        def load_slot(c):
            for m in range(3):
                for s in range(2):
                    sp.dma_start(f32(Wsl[:, m, s]), wt_d[m, s][:, :, bass.ds(c, P)]).then_inc(sem("slot_ld"), 16)
                sp.dma_start(bcol[:, m:m + 1],
                             bias[m][bass.ds(c, P)].rearrange("(p o) -> p o", o=1)).then_inc(sem("slot_ld"), 16)

        def stack(b, base, q_use, k_use):
            q_need, k_need = value(base + (q_use + 3)), value(base + (k_use + 3))
            for m, dst, need, parts in ((0, Qs[b], q_need, (0, 1, 0)), (1, Ks[b], k_need, (0, 0, 1))):
                sp.wait_ge(sem("wk_done"), need)
                for hh in range(HG):
                    for r, s in enumerate(parts):
                        sp.dma_start(f32(dst[32 * r:32 * r + 32, hh, :]),
                                     f32(plane[m][s][32 * hh:32 * hh + 32, :])).then_inc(sem("qk"[m] + "_stack"), 16)

        def put_mrow(b, hf, need):
            need = value(need)
            sp.wait_ge(sem("wk_done"), need)
            for hh in range(HG):
                sp.dma_start(f32(Qs[b][96:97, hh, hf * HALF:(hf + 1) * HALF]),
                             f32(mrow[4 * hh:4 * hh + 4, :])).then_inc(sem("mrow_ld"), 16)

        for i in range(2):
            for s in range(2):
                sp.wait_ge(sem(f"w_st{i}_{s}"), 16 * 6)
        load_slot(0)
        stack(0, 0, 1, 3)
        put_mrow(0, 0, len(PRO_USES) + 2)
        for i in range(2):
            for s in range(2):
                sp.wait_ge(sem(f"w_st{i}_{s}"), 16 * 8)

        def group(g, last):
            where = numbered(last)[0]
            base = g * G_USES + len(PRO_USES)
            for slot in range(4):
                b, hf = slot // 2, slot % 2
                if slot == 1 and not last:
                    c, need = value((g + 1) * P), value(base + (where[0, ("vturn", 1)] + 3))
                    sp.wait_ge(sem("wk_done"), need)
                    load_slot(c)
                if (slot, ("proj", 0, 0)) in where:
                    stack(1 - b, base, where[slot, ("proj", 0, 1)], where[slot, ("proj", 1, 1)])
                if (slot, ("mrow",)) in where:
                    nb, nhf = (slot + 1) % 4 // 2, (slot + 1) % 2
                    put_mrow(nb, nhf, base + (where[slot, ("mrow",)] + 3))
                r, need = value(g * P), value(g * 4 + (slot + 2))
                sp.wait_ge(sem("at_done"), need)
                sp.dma_start(attn_d[bass.ds(r, P), b * L + hf * HALF:b * L + (hf + 1) * HALF],
                             attn_sb[hf][:]).then_inc(sem(f"at_st{hf}"), 16)

        with sp.Fori(0, NG - 1) as g:
            group(g, False)
        group(NG - 1, True)

        sp.wait_ge(sem("at_st0"), 16 * (2 * NG + 1))
        sp.wait_ge(sem("at_st1"), 16 * (2 * NG + 1))
        for s in range(2):
            sp.dma_start(f32(wo[s][:]), wt_d[3, s]).then_inc(sem("wo_ld"), 16)
        sp.dma_start(bo_bc[:], bo.rearrange("(o d) -> o d", o=1).to_broadcast([P, D])).then_inc(sem("bo_ld"), 16)
        with sp.Fori(0, 4) as i:
            for j in range(4):
                r, need = value(i * 512 + j * P), value(i * 4 + (j + 1))
                sp.wait_ge(sem("at_lo"), need)
                sp.dma_start(at_in[j % 2][:], attn_cols[:, :, bass.ds(r, P)]).then_inc(sem(f"at_ld{j % 2}"), 16)
                sp.wait_ge(sem("y_done"), need)
                sp.dma_start(xr[j % 2][:], x_rows[bass.ds(r, P), :]).then_inc(sem(f"xr_ld{j % 2}"), 16)

        def load13(wa, wb, c):
            if c < FC - 1:
                da, db = raw13[c % 2][:, 0], raw13[c % 2][:, 1]
            else:
                da, db = raw13[c % 2][:, 0, :, 0:FTAIL], raw13[c % 2][:, 0, :, FTAIL:P]
            sp.dma_start(da, up_cols(wa, c)).then_inc(sem(f"raw13_ld{c % 2}"), 16)
            sp.dma_start(db, up_cols(wb, c)).then_inc(sem(f"raw13_ld{c % 2}"), 16)

        def load2(wc, c):
            sp.dma_start(raw2[c % 2][tail(c):P, :], wc[c * P:min((c + 1) * P, F), :]).then_inc(sem(f"raw2_ld{c % 2}"), 16)

        def load_set(wa, wb, wc, done, chunks):
            for kind, c in chunks:
                name = "conv13" if kind == 13 else "conv2"
                if not (isinstance(done, int) and done + c < 2):
                    need = value(done + (c - 1))
                    sp.wait_ge(sem(name), need)
                if kind == 13:
                    load13(wa, wb, c)
                else:
                    load2(wc, c)

        in_set = [kc for c in range(1, FC) for kc in CONV_BEFORE[c]]
        own = [kc for c in (0, 1) for kc in CONV_OWN[c]]
        load_set(sw1, sw3, sw2, 0, in_set + own)
        load_set(W1[0], W3[0], W2[0], FC, in_set)
        sp.wait_ge(sem("scat"), 16 * NT)
        sp.wait_ge(sem("hid_lo"), 24 + 2)
        with sp.Fori(0, NT // 2) as i:
            for j in range(2):
                r, need = value(i * 2 * P + j * P), value(i * 2 + (j + 1))
                sp.wait_ge(sem("xd_t"), need)
                sp.dma_start(xdi[j][:], xd_d[bass.ds(r, P), :]).then_inc(sem(f"xd_ld{j}"), 16)
        load_set(W1[0], W3[0], W2[0], FC, own)
        with sp.Fori(1, E) as e:
            ee = value(e)
            w1e, w3e, w2e = (w[bass.ds(ee, 1)].rearrange("o a b -> (o a) b") for w in (W1, W3, W2))
            load_set(w1e, w3e, w2e, e * FC + FC, in_set + own)

        for t in range(NT):
            sp.wait_ge(sem("out_rdy"), t + 1)
            sp.dma_start(out_rows[t * P:(t + 1) * P, :], rows[:, t]).then_inc(sem("out_st"), 16)
        sp.wait_ge(sem("out_st"), 16 * NT)

    @block.gpsimd
    def _(po):
        po.memset(ident[:], 0.0).then_inc(sem("blank"), 1)
        po.memset(tri[:], 1.0).then_inc(sem("blank"), 1)
        po.memset(allone[:], 1.0).then_inc(sem("const"), 1)
        po.memset(ones32[:], 1.0).then_inc(sem("const"), 1)
        po.memset(zeros[:], 0.0).then_inc(sem("const"), 1)
        po.wait_ge(sem("blank"), 2)
        po.affine_select(out=ident[:], in_=ident[:], compare_op=ALU.not_equal, fill=1.0, base=0,
                         pattern=[[-1, P]], channel_multiplier=1).then_inc(sem("const"), 1)
        po.affine_select(out=tri[:], in_=tri[:], compare_op=ALU.is_ge, fill=0.0, base=0,
                         pattern=[[1, P]], channel_multiplier=-1).then_inc(sem("const"), 1)

        for k in range(4 * DC):
            po.wait_ge(sem("w_lo"), k + 1)
            for s in range(2):
                po.dma_start(wt_d[k // DC, s][:, k % DC, :], f32(w_stage[k % 2][s][:])).then_inc(sem(f"w_st{k % 2}_{s}"), 16)
        for i in range(2):
            for s in range(2):
                po.wait_ge(sem(f"w_st{i}_{s}"), 16 * 8)
        po.wait_ge(sem("x_lo"), NT)
        for i in range(2):
            po.memset(f32(Ks[i][96:97, :, :]), 1.0).then_inc(sem("ks_ones"), 1)
        po.wait_ge(sem("const"), 5)
        with po.Fori(0, E * CAP // P) as i:
            po.dma_start(xd_d[bass.ds(i * P, P), :], zeros[:]).then_inc(sem("xd_zero"), 16)

        po.sem_inc(sem("x1_put"), 4)
        po.wait_ge(sem("at_st0"), 16 * (2 * NG + 1))
        po.wait_ge(sem("at_st1"), 16 * (2 * NG + 1))
        for s in range(2):
            po.memset(f32(wgp[s][:]), 0.0).then_inc(sem("wgp_zero"), 1)
        po.iota(r3["io"][:], pattern=[[0, NT], [1, E]], base=-E, channel_multiplier=0,
                allow_small_or_imprecise_dtypes=True).then_inc(sem("iota"), 1)
        po.wait_ge(sem("bo_ld"), 16)
        with po.Fori(0, 4) as i:
            for j in range(4):
                po.wait_ge(sem(f"xr_ld{j % 2}"), i * 32 + 16 * (j // 2 + 1))
                po.tensor_tensor(xr[j % 2][:], xr[j % 2][:], bo_bc[:], ALU.add).then_inc(sem("xb_rdy"), 1)
            for j in range(4):
                po.wait_ge(sem("x1_rdy"), i * 4 + (j + 1))
                po.tensor_copy(rows[:, bass.ds(i * 4 + j, 1), :].rearrange("p o d -> p (o d)"),
                               x1b[j][:]).then_inc(sem("x1_put"), 1)

        po.wait_ge(sem("xd_zero"), 16 * E * CAP // P)
        po.wait_ge(sem("x1_put"), NT + 4)
        po.wait_ge(sem("routed"), 1)
        for t in range(NT):
            po.indirect_dma_start(out=xd_d, out_offset=bass.IndirectOffsetOnAxis(ap=sidx[:, t:t + 1], axis=0),
                                  in_=rows[:, t, :], in_offset=None, bounds_check=E * CAP - 1,
                                  oob_is_err=False).then_inc(sem("scat"), 16)

        with po.Fori(0, E) as e:
            for i in range(2):
                po.wait_ge(sem("oe_rdy"), e * 2 + (i + 3))
                po.dma_start(oe_d[bass.ds(e * CAP + i * P, P), :], oe_sb[i][:]).then_inc(sem(f"oe_st{i}"), 16)

        for i in range(2):
            po.wait_ge(sem(f"oe_st{i}"), 16 * E)
        for t in range(NT):
            if t >= 8:
                po.wait_ge(sem("z_done"), t - 7)
            po.indirect_dma_start(out=got[t % 8][:], out_offset=None, in_=oe_d,
                                  in_offset=bass.IndirectOffsetOnAxis(ap=gidx[:, t:t + 1], axis=0),
                                  bounds_check=E * CAP - 1, oob_is_err=False).then_inc(sem(f"gath{t % 8}"), 16)

    @block.tensor
    def _(pe):
        def split3(dst, lhs, rhs):
            for dc in range(DC):
                for k, (a, b) in enumerate(SPLIT):
                    mm = nc.tensor.matmul(dst, lhs(a, dc), rhs(b, dc), start=dc == 0 and k == 0,
                                          stop=dc == DC - 1 and k == 2)
            return mm

        def turn(dst, src):
            for c in range(DC):
                mm = nc.tensor.transpose(dst[:, c * P:(c + 1) * P], src[:, c * P:(c + 1) * P], ident[:])
            return mm

        pe.sem_inc(sem("st_full"), 1)
        pe.sem_inc(sem("pv_done"), 2)
        pe.sem_inc(sem("o_full"), 2)
        pe.sem_inc(sem("used2"), 2)
        pe.sem_inc(sem("xd_t"), 2)

        pe.wait_ge(sem("const"), 5)
        pe.wait_ge(sem("lora_ld"), 16 * 8)
        for m in range(4):
            for oc in range(DC):
                mm = nc.tensor.transpose(bank[m][0:RANK, oc * P:(oc + 1) * P], lora_a[:, m, oc, :], ident[:])
            mm.then_inc(sem("a_t"), 1)

        def weights(m):
            pe.wait_ge(sem("a_ev"), m + 1)
            pe.wait_ge(sem(f"w_ld{m % 2}"), 16 * (m // 2 + 1))
            for dc in range(DC):
                k = m * DC + dc
                dst = bank[4 + k % 4]
                if k >= 4:
                    pe.wait_ge(sem("w_lo"), k - 3)
                nc.tensor.matmul(dst, lora_b[32 * m:32 * m + RANK, dc * P:(dc + 1) * P],
                                 lora_at[32 * m:32 * m + RANK, :], start=True, stop=False)
                for oc in range(DC):
                    mm = nc.tensor.matmul(dst[:, oc * P:(oc + 1) * P], w_raw[m % 2][:, oc, dc * P:(dc + 1) * P],
                                          ident[:], start=False, stop=oc == DC - 1)
                mm.then_inc(sem("w_mm"), 1)

        def turn_x(i):
            for j in range(4):
                pe.wait_ge(sem(f"x_ld{j}"), i * 16 + 16)
                if not isinstance(i, int):
                    pe.wait_ge(sem("x_lo"), i * 4 + (j - 3))
                turn(bank[j], xin[j]).then_inc(sem("x_t"), 1)

        weights(0)
        weights(1)
        pe.wait_ge(sem("a_ev"), 4)
        turn_x(0)
        weights(2)
        with pe.Fori(1, 4) as i:
            turn_x(i)
        weights(3)

        def use(kind, dst, n, b, hf, need):
            pe.wait_ge(sem("wk_done"), n + 1)
            if kind[0] == "proj":
                _, m, ph = kind
                pe.wait_ge(sem("slot_ld"), need)
                c0 = b * L + ph * HALF
                mm = split3(dst, lambda a, dc: Wsl[:, m, a, dc, :], lambda p, dc: xT[p][:, dc, c0:c0 + HALF])
            elif kind[0] == "vturn":
                pe.wait_ge(sem("wk_done"), need)
                for c in range(4):
                    kc = kind[1] * 4 + c
                    mm = nc.tensor.transpose(dst[:, c * P:(c + 1) * P], vT[:, kc * P:(kc + 1) * P], ident[:])
            elif kind[0] == "smax":
                _, hh, qt, part = kind
                q0 = hf * HALF + qt * P
                mm = nc.tensor.matmul(dst, Qs[b][0:96, hh, q0:q0 + P], Ks[b][0:96, hh, part * 512:part * 512 + 512],
                                      start=True, stop=True)
            else:
                pe.wait_ge(sem("nm_rdy"), need)
                mm = nc.tensor.transpose(dst[0:16, 0:P], nm[:], ident[:])
            mm.then_inc(sem("wk_full"), 1)

        pe.wait_ge(sem("x_lo"), NT)
        pe.wait_ge(sem("w_lo"), 16)
        for n, kind in enumerate(PRO_USES):
            if kind == ("smax", 0, 0, 0):
                pe.wait_ge(sem("q_stack"), 192)
                pe.wait_ge(sem("k_stack"), 192)
            need = {"proj": 144, "vturn": PRO_USES.index(("proj", 2, 1)) + 3, "smax": 0, "mrow": 1}[kind[0]]
            use(kind, bank[n % 2], n, 0, 0, need)
        pe.wait_ge(sem("ks_ones"), 2)

        def score(b, hf, steps, kc, p):
            pe.wait_ge(sem("exp_done"), steps + (2 * kc + p + 1))
            for i in range(2):
                hh = 2 * p + i
                mm = nc.tensor.matmul(pair[p][:, i], Ks[b][0:97, hh, kc * P:(kc + 1) * P],
                                      Qs[b][0:97, hh, hf * HALF:(hf + 1) * HALF], start=True, stop=True)
            mm.then_inc(sem("st_full"), 1)

        def values(b, steps, kc):
            pe.wait_ge(sem("exp_done"), steps + (2 * kc + 4))
            for dst, sums in ((ov, False), (dn, True)):
                for hh in range(HG):
                    w = ones32[:] if sums else V[b][:, kc, hh * HD:(hh + 1) * HD]
                    mm = nc.tensor.matmul(dst[hh * HD:(hh + 1) * HD, :], w, prob[2 * (kc % 2) + hh // 2][:, hh % 2, :],
                                          start=kc == 0, stop=kc == KC - 1)
            mm.then_inc(sem("pv_done"), 1)

        def group(g, last):
            where = numbered(last)[0]
            base = g * G_USES + len(PRO_USES)
            k = 0
            for slot in range(4):
                b, hf = slot // 2, slot % 2
                nb, nhf = (slot + 1) % 4 // 2, (slot + 1) % 2
                steps = g * 64 + 16 * slot
                needs = {"proj": g * 144 + (144 if slot == 0 else 288), "smax": 0, "mrow": g * 4 + (slot + 2)}
                if (slot, ("vturn", 0)) in where:
                    needs["vturn"] = base + (where[slot, ("proj", 2, 1)] + 3)
                pe.wait_ge(sem("mrow_ld"), g * 256 + 64 * (slot + 1))
                for kc, (before, after) in enumerate(slot_uses(slot, last)):
                    for step, uses in ((0, before), (1, after)):
                        score(b, hf, steps, kc, step)
                        if step == 1 and kc:
                            if kc == 1:
                                pe.wait_ge(sem("at_done"), g * 4 + (slot + 1))
                            values(b, steps, kc - 1)
                        for kind in uses:
                            if kind == ("smax", 0, 0, 0) and nhf == 0:
                                unit = g * 384 + (384 if slot == 1 else 576)
                                pe.wait_ge(sem("q_stack"), unit)
                                pe.wait_ge(sem("k_stack"), unit)
                            use(kind, bank[(len(PRO_USES) + k) % 2], base + k, 1 - b if kind[0] == "proj" else nb, nhf,
                                needs[kind[0]])
                            k += 1
                values(b, steps, KC - 1)

        with pe.Fori(0, NG - 1) as g:
            group(g, False)
        group(NG - 1, True)

        pe.wait_ge(sem("wk_done"), (NG - 1) * G_USES + len(PRO_USES) + numbered(True)[1] + 2)
        pe.wait_ge(sem("exp_done"), 64 * NG + 2)
        pe.wait_ge(sem("at_done"), 4 * NG + 1)
        pe.wait_ge(sem("wo_ld"), 32)
        pe.wait_ge(sem("wgp_lo"), 1)

        def project(i):
            for j in range(4):
                pe.wait_ge(sem("at_lo"), i * 4 + (j + 3))
                pe.wait_ge(sem("y_done"), i * 4 + (j + 1))
                split3(bank[j % 2], lambda a, dc: at[j % 2][a][:, dc, :],
                       lambda p, dc: wo[p][:, dc, :]).then_inc(sem("o_full"), 1)

        def turn_x1(i):
            for j in range(4):
                pe.wait_ge(sem("x1_rdy"), i * 4 + (j + 1))
                pe.wait_ge(sem("x1_lo"), i * 4 + (j + 1))
                turn(bank[2 + j], x1b[j]).then_inc(sem("x1_t"), 1)
            pe.wait_ge(sem("x1_lo"), i * 4 + 8)
            pe.wait_ge(sem("lg_ev"), i + 1)
            split3(bank[6], lambda a, dc: wgp[a][:, dc, :],
                   lambda p, dc: xT[p][:, dc, bass.ds(i * 512, 512)]).then_inc(sem("lg_full"), 1)

        project(0)
        with pe.Fori(1, 4) as i:
            project(i)
            turn_x1(i - 1)
        turn_x1(3)

        pe.wait_ge(sem("lg_ev"), 5)
        for t in range(NT):
            mm = nc.tensor.transpose(bank[7][:, t * E:(t + 1) * E], lgT[:, t * P:(t + 1) * P], ident[0:E, 0:E])
        mm.then_inc(sem("rt_mm"), 1)
        pe.wait_ge(sem("oh_rdy"), 1)
        nc.tensor.matmul(bank[0][:, 0:P], tri[:], oh_bf[:].rearrange("p t e -> p (t e)"), start=True, stop=True)
        nc.tensor.matmul(bank[1][:, 0:P], allone[:], oh_bf[:].rearrange("p t e -> p (t e)"), start=True,
                         stop=True).then_inc(sem("rt_mm"), 1)

        def ff(q, sets, width, rhs):
            def down(c):
                pe.wait_ge(sem("hid_lo"), q + (c + 3))
                pe.wait_ge(sem("conv2"), sets + (c + 1))
                p0 = tail(c)
                for i in range(width // P):
                    for k, (a, p) in enumerate(SPLIT):
                        mm = nc.tensor.matmul(bank[4 + i], hid[c % 2][a][p0:P, i * P:(i + 1) * P], w2[p][p0:P, c, :],
                                              start=c == 0 and k == 0, stop=c == FC - 1 and k == 2)
                mm.then_inc(sem("used2"), 1)

            for c in range(FC):
                pe.wait_ge(sem("conv13"), sets + (c + 1))
                pe.wait_ge(sem("h_done"), q + (c + 1))
                mm = split3(bank[2 * (c % 2)][:, 0:width], lambda a, dc: w13[a][:, 2 * c, dc, :], rhs)
                if c < FC - 1:
                    mm = split3(bank[2 * (c % 2) + 1][:, 0:width], lambda a, dc: w13[a][:, 2 * c + 1, dc, :], rhs)
                mm.then_inc(sem("ab_full"), 1)
                if c:
                    down(c - 1)
            down(FC - 1)

        pe.wait_ge(sem("pos_rdy"), 1)
        with pe.Fori(0, 4) as i:
            pe.wait_ge(sem("acc_done"), i * 4 + 1)
            ff(i * FC, 0, 512, lambda p, dc: xT[p][:, dc, bass.ds(i * 512, 512)])
        pe.wait_ge(sem("h_done"), 4 * FC + 2)
        pe.wait_ge(sem("acc_done"), NT + 1)
        with pe.Fori(0, NT // 4) as i:
            for j in range(4):
                pe.wait_ge(sem(f"xd_ld{j % 2}"), i * 32 + 16 * (j // 2 + 1))
                pe.wait_ge(sem("xd_lo"), i * 4 + (j + 1))
                turn(bank[j], xdi[j % 2]).then_inc(sem("xd_t"), 1)
        pe.wait_ge(sem("xd_lo"), NT + 4)
        with pe.Fori(0, E) as e:
            pe.wait_ge(sem("oe_rdy"), e * 2 + 2)
            ff(e * FC + 4 * FC, e * FC + FC, CAP, lambda p, dc: xT[p][:, dc, bass.ds(e * CAP, CAP)])

    @block.scalar
    def _(ac):
        ACTV = nc.scalar.activation
        ac.sem_inc(sem("exp_done"), 2)
        ac.sem_inc(sem("lg_ev"), 1)
        ac.sem_inc(sem("oe_rdy"), 2)

        def turned(i, j, src, full, done):
            ac.wait_ge(sem(full[0]), i * 4 + (j + 1 + full[1]))
            ACTV(xT[0][:, :, cols(i, j)], src.rearrange("p (c n) -> p c n", c=DC), ACT.Identity).then_inc(sem(done), 1)

        for m in range(4):
            ac.wait_ge(sem("a_t"), m + 1)
            ACTV(lora_at[32 * m:32 * m + RANK, :], bank[m][0:RANK, :], ACT.Copy, scale=LORA).then_inc(sem("a_ev"), 1)

        def weights(m):
            for dc in range(DC):
                k = m * DC + dc
                ac.wait_ge(sem("w_mm"), k + 1)
                if k >= 2:
                    ac.wait_ge(sem(f"w_st{k % 2}_0"), 16 * (k // 2))
                ACTV(w_stage[k % 2][0][:], bank[4 + k % 4], ACT.Identity).then_inc(sem("w_hi"), 1)

        weights(0)
        weights(1)
        for j in range(4):
            turned(0, j, bank[j], ("x_t", 0), "x_hi")
        weights(2)
        with ac.Fori(1, 4) as i:
            for j in range(4):
                turned(i, j, bank[j], ("x_t", 0), "x_hi")
        weights(3)

        def plane_hi(kind, src, n, slot_need, stack_need):
            _, m, ph = kind
            ac.wait_ge(sem("wk_full"), n + 1)
            ac.wait_ge(sem("slot_ld"), slot_need)
            if stack_need is not None:
                ac.wait_ge(sem("qk"[m] + "_stack"), stack_need)
            ACTV(plane[m][0][:, ph * HALF:(ph + 1) * HALF], src, ACT.Identity,
                 bias=bcol[:, m:m + 1]).then_inc(sem("pl_hi"), 1)

        for n, kind in enumerate(PRO_USES):
            if kind[0] == "proj" and kind[1] < 2:
                plane_hi(kind, bank[n % 2], n, 144, None)

        def group(g, last):
            base = g * G_USES + len(PRO_USES)
            k = 0
            for slot in range(4):
                for kc, parts in enumerate(slot_uses(slot, last)):
                    for step in range(2):
                        ac.wait_ge(sem("st_full"), g * 64 + (16 * slot + 2 * kc + step + 2))
                        ac.wait_ge(sem("pv_done"), g * 32 + (8 * slot + kc + 1))
                        ACTV(prob[2 * (kc % 2) + step][:], pair[step][:], ACT.Exp, scale=SCALE).then_inc(sem("exp_done"), 1)
                        for kind in parts[step]:
                            if kind[0] == "proj" and kind[1] < 2:
                                plane_hi(kind, bank[(len(PRO_USES) + k) % 2], base + k,
                                         g * 144 + (144 if slot == 0 else 288), g * 384 + (192 if slot == 0 else 384))
                            k += 1

        with ac.Fori(0, NG - 1) as g:
            group(g, False)
        group(NG - 1, True)

        ac.wait_ge(sem("wgp_zero"), 2)
        ac.wait_ge(sem("wg_ld"), 16)
        ACTV(wgp[0][:, :, 0:E], wg_raw[:], ACT.Identity).then_inc(sem("wgp_hi"), 1)

        def at_hi(i):
            for j in range(4):
                ac.wait_ge(sem(f"at_ld{j % 2}"), i * 32 + 16 * (j // 2 + 1))
                ac.wait_ge(sem("o_full"), i * 4 + (j + 1))
                ACTV(at[j % 2][0][:], at_in[j % 2][:], ACT.Identity).then_inc(sem("at_hi"), 1)

        def x1_hi(i):
            for j in range(4):
                turned(i, j, bank[2 + j], ("x1_t", 0), "x1_hi")
            ac.wait_ge(sem("lg_full"), i + 1)
            ACTV(lgT[:, bass.ds(i * 512, 512)], bank[6][0:E, :], ACT.Copy).then_inc(sem("lg_ev"), 1)

        def root(k, name):
            ac.wait_ge(sem(name + "_var"), k)
            ACTV(ln_s[:], ln_v[:], ACT.Sqrt).then_inc(sem(name + "_root"), 1)

        at_hi(0)
        root(1, "ln1")
        with ac.Fori(1, 4) as i:
            at_hi(i)
            x1_hi(i - 1)
            root(i + 1, "ln1")
        x1_hi(3)
        ac.wait_ge(sem("rt_d"), 1)
        ACTV(r3["ex"][:], r3["d"][:], ACT.Exp).then_inc(sem("rt_ex"), 1)

        def conv(kind, c, sets, need):
            if kind == 13:
                ac.wait_ge(sem(f"raw13_ld{c % 2}"), sets * 96 + 32 * (c // 2 + 1))
                if need is not None:
                    ac.wait_ge(sem("ab_full"), need + (c + 1))
                s0, s1 = 2 * c, min(2 * c + 2, 2 * FC - 1)
                ACTV(w13[0][:, s0:s1], raw13[c % 2][:, 0:s1 - s0], ACT.Identity).then_inc(sem("conv13_hi"), 1)
            else:
                ac.wait_ge(sem(f"raw2_ld{c % 2}"), sets * 48 + 16 * (c // 2 + 1))
                if need is not None:
                    ac.wait_ge(sem("used2"), need + (c + 3))
                ACTV(w2[0][tail(c):P, c], raw2[c % 2][tail(c):P, :], ACT.Identity).then_inc(sem("conv2_hi"), 1)

        def steps(q, width, own, ahead):
            for c in range(FC):
                r, p0 = c % 2, tail(c)
                ac.wait_ge(sem("ab_full"), q + (c + 1))
                ac.wait_ge(sem("hid_lo"), q + (c + 1))
                ACTV(sa[r][p0:P, 0:width], bank[2 * r][0:P - p0, 0:width], ACT.Silu).then_inc(sem("sa_rdy"), 1)
                for kind, cc in CONV_OWN.get(c, ()) if own else ():
                    conv(kind, cc, *own)
                for kind, cc in CONV_BEFORE.get(c, ()) if ahead else ():
                    conv(kind, cc, *ahead)
                ac.wait_ge(sem("h_done"), q + (c + 3))
                ac.wait_ge(sem("used2"), q + (c + 1))
                ACTV(hid[r][0][p0:P, 0:width], sa[r][p0:P, 0:width], ACT.Identity).then_inc(sem("hid_hi"), 1)

        ac.wait_ge(sem("lg_read"), 1)
        ac.wait_ge(sem("x1_put"), NT + 4)
        for c in range(1, FC):
            for kind, cc in CONV_BEFORE[c]:
                conv(kind, cc, 0, None)
        for c in range(2):
            for kind, cc in CONV_OWN[c]:
                conv(kind, cc, 0, None)
        with ac.Fori(0, 3) as i:
            steps(i * FC, 512, None, None)
        steps(3 * FC, 512, None, (1, 3 * FC))
        with ac.Fori(0, NT // 4) as i:
            for j in range(4):
                turned(i, j, bank[j], ("xd_t", 2), "xd_hi")

        def expert(e, first=False, last=False):
            steps(e * FC + 4 * FC, CAP, (e + 1, e * FC + 3 * FC), None if last else (e + 2, e * FC + 4 * FC))
            ac.wait_ge(sem("used2"), e * FC + (5 * FC + 2))
            for i in range(2):
                if not first:
                    ac.wait_ge(sem(f"oe_st{i}"), e * 16)
                ACTV(oe_sb[i][:], bank[4 + i], ACT.Copy).then_inc(sem("oe_rdy"), 1)

        expert(0, first=True)
        with ac.Fori(1, E - 1) as e:
            expert(e)
        expert(E - 1, last=True)
        for k in range(4):
            root(k + 1, "ln2")

    @block.vector
    def _(ve):
        TT, TS, RED = nc.vector.tensor_tensor, nc.vector.tensor_scalar, nc.vector.tensor_reduce
        ve.sem_inc(sem("wk_done"), 2)
        ve.sem_inc(sem("at_done"), 1)
        ve.sem_inc(sem("y_done"), 2)
        ve.sem_inc(sem("at_lo"), 2)
        ve.sem_inc(sem("x1_lo"), 4)
        ve.sem_inc(sem("xd_lo"), 4)
        ve.sem_inc(sem("h_done"), 2)
        ve.sem_inc(sem("hid_lo"), 2)
        ve.sem_inc(sem("acc_done"), 1)
        for i in range(2):
            ve.sem_inc(sem(f"at_st{i}"), 16)

        def turned(i, j, src, hi, lo):
            ve.wait_ge(sem(hi), i * 4 + (j + 1))
            TT(xT[1][:, :, cols(i, j)], src.rearrange("p (c n) -> p c n", c=DC), f32(xT[0][:, :, cols(i, j)]),
               ALU.subtract).then_inc(sem(lo), 1)

        def weights(m):
            for dc in range(DC):
                k = m * DC + dc
                ve.wait_ge(sem("w_hi"), k + 1)
                if k >= 2:
                    ve.wait_ge(sem(f"w_st{k % 2}_1"), 16 * (k // 2))
                TT(w_stage[k % 2][1][:], bank[4 + k % 4], f32(w_stage[k % 2][0][:]), ALU.subtract).then_inc(sem("w_lo"), 1)

        weights(0)
        weights(1)
        for j in range(4):
            turned(0, j, bank[j], "x_hi", "x_lo")
        weights(2)
        with ve.Fori(1, 4) as i:
            for j in range(4):
                turned(i, j, bank[j], "x_hi", "x_lo")
        weights(3)

        def use(kind, src, n, b, hi_need, slot_need, stack_need, half):
            ve.wait_ge(sem("wk_full"), n + 1)
            if kind[0] == "proj":
                _, m, ph = kind
                part = slice(ph * HALF, (ph + 1) * HALF)
                if m < 2:
                    ve.wait_ge(sem("pl_hi"), hi_need)
                    ins = nc.vector.scalar_tensor_tensor(out=plane[m][1][:, part], in0=src, scalar=bcol[:, m:m + 1],
                                                         in1=f32(plane[m][0][:, part]), op0=ALU.add, op1=ALU.subtract)
                else:
                    ve.wait_ge(sem("slot_ld"), slot_need)
                    ins = TS(vT[:, part], src, bcol[:, m:m + 1], None, ALU.add)
            elif kind[0] == "vturn":
                ins = nc.vector.tensor_copy(V[b][:, 4 * kind[1]:4 * kind[1] + 4, :],
                                            src.rearrange("p (c n) -> p c n", c=4))
            elif kind[0] == "smax":
                _, hh, qt, part = kind
                ins = RED(mx[:, 4 * hh + qt, part:part + 1], src, AX.X, ALU.max)
            else:
                if stack_need is not None:
                    ve.wait_ge(sem("mrow_ld"), stack_need)
                ins = nc.vector.tensor_copy(mrow[:], src[0:16, 0:P])
            ins.then_inc(sem("wk_done"), 1)
            if kind == LAST_SMAX:
                ve.wait_ge(sem("wk_done"), n + 3)
                RED(nm[:], mx[:], AX.X, ALU.max, negate=True).then_inc(sem("nm_rdy"), 1)

        his = 0
        for n, kind in enumerate(PRO_USES):
            his += kind[0] == "proj" and kind[1] < 2
            use(kind, bank[n % 2], n, 0, his, 144, None, 1)

        def group(g, last):
            base = g * G_USES + len(PRO_USES)
            k, his = 0, 0
            for slot in range(4):
                b, hf = slot // 2, slot % 2
                for parts in slot_uses(slot, last):
                    for part in parts:
                        for kind in part:
                            his += kind[0] == "proj" and kind[1] < 2
                            use(kind, bank[(len(PRO_USES) + k) % 2], base + k, 1 - b, g * 8 + (4 + his),
                                g * 144 + (144 if slot == 0 else 288), g * 256 + 64 * (slot + 1), None)
                            k += 1
                ve.wait_ge(sem("pv_done"), g * 32 + (8 * slot + 10))
                nc.vector.reciprocal(rden[:], dn[:]).then_inc(sem("rden"), 1)
                ve.wait_ge(sem("rden"), g * 4 + (slot + 1))
                ve.wait_ge(sem(f"at_st{hf}"), g * 32 + (16 * b + 16))
                TT(attn_sb[hf][:], ov[:], rden[:], ALU.mult).then_inc(sem("at_done"), 1)

        with ve.Fori(0, NG - 1) as g:
            group(g, False)
        group(NG - 1, True)

        ve.wait_ge(sem("wgp_hi"), 1)
        TT(wgp[1][:, :, 0:E], wg_raw[:], f32(wgp[0][:, :, 0:E]), ALU.subtract).then_inc(sem("wgp_lo"), 1)

        def row(t):
            return rows[:, bass.ds(t, 1), :].rearrange("p o d -> p (o d)")

        def at_rest(i, j):
            ve.wait_ge(sem("at_hi"), i * 4 + (j + 1))
            TT(at[j % 2][1][:], at_in[j % 2][:], f32(at[j % 2][0][:]), ALU.subtract).then_inc(sem("at_lo"), 1)

        def scale_of(link, k, name):
            for j in range(4):
                ins = nc.vector.bn_aggr(mv[:, j], st6[:, j])
            link(ins)
            TS(ln_v[:], mv[:, :, 1], EPS, None, ALU.add).then_inc(sem(name + "_var"), 1)
            ve.wait_ge(sem(name + "_root"), k)
            link(nc.vector.reciprocal(ln_r[:], ln_s[:]))
            link(TT(ln_t[:], ln_r[:], ln_r[:], ALU.mult))
            link(TT(ln_t[:], ln_t[:], ln_v[:], ALU.mult))
            link(TS(ln_t[:], ln_t[:], -0.5, 1.5, ALU.mult, ALU.add))
            link(TT(ln_r[:], ln_r[:], ln_t[:], ALU.mult))

        def tiles(i, link):
            at_rest(i, 0)
            at_rest(i, 1)
            for j in range(4):
                ve.wait_ge(sem("o_full"), i * 4 + (j + 3))
                ve.wait_ge(sem("xb_rdy"), i * 4 + (j + 1))
                TT(yb[j][:], bank[j % 2], xr[j % 2][:], ALU.add).then_inc(sem("y_done"), 1)
                if j < 2:
                    at_rest(i, j + 2)
                ve.wait_ge(sem("y_done"), i * 4 + (j + 3))
                link(nc.vector.bn_stats(st6[:, j], yb[j][:]))

        def norm(i, link):
            scale_of(link, i + 1, "ln1")
            for j in range(4):
                ve.wait_ge(sem("x1_put"), i * 4 + (j + 1))
                TS(x1b[j][:], yb[j][:], mv[:, j, 0:1], ln_r[:, j:j + 1], ALU.subtract, ALU.mult).then_inc(sem("x1_rdy"), 1)

        def x1_rest(i):
            for j in range(4):
                turned(i, j, bank[2 + j], "x1_hi", "x1_lo")

        link = Chain(ve, sem("ln1_chain"))
        tiles(0, link)
        norm(0, link)
        per_block = link.k
        with ve.Fori(1, 4) as i:
            link = Chain(ve, sem("ln1_chain"), i * per_block)
            tiles(i, link)
            x1_rest(i - 1)
            norm(i, link)
            assert link.k == per_block
        x1_rest(3)

        def over_e(t):
            return t[:].unsqueeze(2).to_broadcast([P, NT, E])

        def by_t(b):
            return b[:, 0:P].rearrange("p (t e) -> p t e", e=E)

        link = Chain(ve, sem("rt_chain"))
        ve.wait_ge(sem("rt_mm"), 1)
        nc.vector.tensor_copy(r3["lg"][:], by_t(bank[7])).then_inc(sem("lg_read"), 1)
        ve.wait_ge(sem("lg_read"), 1)
        link(RED(r2["mx"][:], r3["lg"][:], AX.X, ALU.max))
        TT(r3["d"][:], r3["lg"][:], over_e(r2["mx"]), ALU.subtract).then_inc(sem("rt_d"), 1)
        ve.wait_ge(sem("rt_d"), 1)
        ve.wait_ge(sem("iota"), 1)
        link(nc.vector.scalar_tensor_tensor(out=r3["c"][:], in0=r3["d"][:], scalar=0.0, in1=r3["io"][:],
                                            op0=ALU.is_equal, op1=ALU.mult))
        link(RED(r2["em"][:], r3["c"][:], AX.X, ALU.min))
        link(TT(r3["oh"][:], r3["io"][:], over_e(r2["em"]), ALU.is_equal))
        nc.vector.tensor_copy(oh_bf[:], r3["oh"][:]).then_inc(sem("oh_rdy"), 1)
        ve.wait_ge(sem("rt_ex"), 1)
        link(RED(r2["sm"][:], r3["ex"][:], AX.X, ALU.add))
        link(nc.vector.reciprocal(r2["gate"][:], r2["sm"][:]))
        ve.wait_ge(sem("rt_mm"), 2)
        link(nc.vector.memset(r3["s0"][:, 0:1, :], 0.0))
        link(nc.vector.tensor_copy(r3["s0"][:, 1:NT, :], by_t(bank[1])[:, 0:NT - 1, :]))
        a, b = "s0", "s1"
        for k in (1, 2, 4, 8):
            nc.vector.tensor_copy(r3[b][:, 0:k, :], r3[a][:, 0:k, :])
            link(TT(r3[b][:, k:NT, :], r3[a][:, k:NT, :], r3[a][:, 0:NT - k, :], ALU.add))
            a, b = b, a
        TT(r3["c"][:], by_t(bank[0]), r3[a][:], ALU.add).then_inc(sem("pos_rdy"), 1)
        ve.wait_ge(sem("pos_rdy"), 1)
        link(TT(r3["c"][:], r3["c"][:], r3["oh"][:], ALU.mult))
        link(RED(r2["ps"][:], r3["c"][:], AX.X, ALU.add))
        link(TS(r2["keep"][:], r2["ps"][:], float(CAP), None, ALU.is_le))
        link(nc.vector.scalar_tensor_tensor(out=r2["flat"][:], in0=r2["em"][:], scalar=float(CAP), in1=r2["ps"][:],
                                            op0=ALU.mult, op1=ALU.add))
        link(TS(r2["t"][:], r2["keep"][:], -2.0 * E * CAP, 3.0 * E * CAP - 1.0, ALU.mult, ALU.add))
        link(TT(r2["t"][:], r2["t"][:], r2["flat"][:], ALU.add))
        link(nc.vector.tensor_copy(sidx[:], r2["t"][:]))
        link(TS(r2["u"][:], r2["t"][:], E * CAP - 1.0, None, ALU.min))
        link(nc.vector.tensor_copy(gidx[:], r2["u"][:]))
        TT(r2["gk"][:], r2["gate"][:], r2["keep"][:], ALU.mult).then_inc(sem("routed"), 1)

        def conv(kind, c, sets):
            if kind == 13:
                ve.wait_ge(sem("conv13_hi"), sets * FC + (c + 1))
                s0, s1 = 2 * c, min(2 * c + 2, 2 * FC - 1)
                TT(w13[1][:, s0:s1], raw13[c % 2][:, 0:s1 - s0], f32(w13[0][:, s0:s1]), ALU.subtract).then_inc(sem("conv13"), 1)
            else:
                ve.wait_ge(sem("conv2_hi"), sets * FC + (c + 1))
                p0 = tail(c)
                TT(w2[1][p0:P, c], raw2[c % 2][p0:P, :], f32(w2[0][p0:P, c]), ALU.subtract).then_inc(sem("conv2"), 1)

        def steps(q, width, own, ahead):
            for c in range(FC):
                r, p0 = c % 2, tail(c)
                gated = bank[2 * r + 1] if c < FC - 1 else bank[2 * r]
                ve.wait_ge(sem("sa_rdy"), q + (c + 1))
                TT(sa[r][p0:P, 0:width], gated[p0:P, 0:width], sa[r][p0:P, 0:width], ALU.mult).then_inc(sem("h_done"), 1)
                for kind, cc in CONV_OWN.get(c, ()) if own is not None else ():
                    conv(kind, cc, own)
                for kind, cc in CONV_BEFORE.get(c, ()) if ahead is not None else ():
                    conv(kind, cc, ahead)
                ve.wait_ge(sem("hid_hi"), q + (c + 1))
                TT(hid[r][1][p0:P, 0:width], sa[r][p0:P, 0:width], f32(hid[r][0][p0:P, 0:width]),
                   ALU.subtract).then_inc(sem("hid_lo"), 1)

        def add_shared(i):
            ve.wait_ge(sem("used2"), i * FC + (FC + 2))
            for j in range(4):
                TT(row(i * 4 + j), bank[4 + j], row(i * 4 + j), ALU.add).then_inc(sem("acc_done"), 1)

        for c in range(1, FC):
            for kind, cc in CONV_BEFORE[c]:
                conv(kind, cc, 0)
        for c in range(2):
            for kind, cc in CONV_OWN[c]:
                conv(kind, cc, 0)
        steps(0, 512, None, None)
        ve.wait_ge(sem("scat"), 16 * NT)
        add_shared(0)
        with ve.Fori(1, 3) as i:
            steps(i * FC, 512, None, None)
            add_shared(i)
        steps(3 * FC, 512, None, 1)
        add_shared(3)
        with ve.Fori(0, NT // 4) as i:
            for j in range(4):
                turned(i, j, bank[j], "xd_hi", "xd_lo")
        with ve.Fori(0, E - 1) as e:
            steps(e * FC + 4 * FC, CAP, e + 1, e + 2)
        steps((E + 3) * FC, CAP, E, None)

        link = Chain(ve, sem("ln2_chain"))
        for k in range(4):
            for j in range(4):
                t = 4 * k + j
                ve.wait_ge(sem(f"gath{t % 8}"), 16 * (t // 8 + 1))
                nc.vector.scalar_tensor_tensor(out=rows[:, t], in0=got[t % 8][:], scalar=r2["gk"][:, t:t + 1],
                                               in1=rows[:, t], op0=ALU.mult, op1=ALU.add).then_inc(sem("z_done"), 1)
                ve.wait_ge(sem("z_done"), t + 1)
                link(nc.vector.bn_stats(st6[:, j], rows[:, t]))
            scale_of(link, k + 1, "ln2")
            for j in range(4):
                t = 4 * k + j
                TS(rows[:, t], rows[:, t], mv[:, j, 0:1], ln_r[:, j:j + 1], ALU.subtract, ALU.mult).then_inc(sem("out_rdy"), 1)


_INS = ["L0_attn_x"] + [f"L0_attn_{k}{m}" for m in "qkvo" for k in "WbBA"] + [
    "L0_ffn_Wg", "L0_ffn_W1", "L0_ffn_W3", "L0_ffn_W2", "L0_ffn_sw1", "L0_ffn_sw3", "L0_ffn_sw2"]
_OUTS = [((B, L, D), "float32")]


def build(nc, args):
    by_name = dict(zip(_INS + ["out"], args))
    per = {k: [by_name[f"L0_attn_{k}{m}"] for m in "qkvo"] for k in "WbBA"}
    ff = [by_name[f"L0_ffn_{n}"] for n in ("Wg", "W1", "W3", "W2", "sw1", "sw3", "sw2")]
    with ExitStack() as ctx:
        emit(nc, ctx, by_name["L0_attn_x"], per["W"], per["b"][:3], per["b"][3], per["B"], per["A"], *ff, by_name["out"])


def kernel(**inputs):
    import numpy as _np
    import concourse.bacc as _bacc
    from concourse import mybir as _mybir
    from concourse.bass_utils import run_bass_kernel_spmd as _run

    nc = _bacc.Bacc("TRN2", target_bir_lowering=False, num_devices=1)
    arrays, args = {}, []
    for name in _INS:
        a = _np.ascontiguousarray(inputs[name])
        arrays[f"in_{name}_dram"] = a
        args.append(nc.dram_tensor(f"in_{name}_dram", a.shape, _mybir.dt.from_np(a.dtype), kind="ExternalInput").ap())
    for i, (shape, dtype) in enumerate(_OUTS):
        dt = _mybir.dt.from_np(_np.dtype(dtype))
        args.append(nc.dram_tensor(f"out_{i}_dram", shape, dt, kind="ExternalOutput").ap())
    build(nc, args)
    r = _run(nc, [arrays], core_ids=[0])
    return r.results[0]["out_0_dram"]
```

```python
from contextlib import ExitStack

import concourse.bass as bass
from concourse import mybir

F32 = mybir.dt.float32
FR = mybir.dt.float32r
BF16 = mybir.dt.bfloat16
U32 = mybir.dt.uint32
ACT = mybir.ActivationFunctionType
ALU = mybir.AluOpType
AX = mybir.AxisListType

P = 128
B, L, D = 2, 1024, 512
T = B * L
NT = T // P
DC = D // P
HEADS = 16
HD = D // HEADS
HG = P // HD
NG = HEADS // HG
RANK = 16
LORA = 8.0 / RANK
SCALE = float(HD) ** -0.5
HALF = 512
KC = L // P
E = 8
CAP = T // E
F = 704
FC = 6
FTAIL = F - 5 * P
EPS = 1e-5
W_ORDER = (2, 0, 1, 3)
SPLIT = ((0, 0), (0, 1), (1, 0))


class Arena:

    def __init__(self, nc, start, end):
        self.nc, self.at, self.end = nc, start, end

    def __call__(self, name, shape, dt):
        size = mybir.dt.size(dt)
        for n in shape[1:]:
            size *= n
        t = self.nc.alloc_sbuf_tensor_at(name, shape, dt, offset=self.at)
        self.at += (size + 31) // 32 * 32
        assert self.at <= self.end, (name, self.at, self.end)
        return t


class Chain:

    def __init__(self, eng, sem, base=0):
        self.eng, self.sem, self.base, self.k = eng, sem, base, 0

    def __call__(self, ins):
        ins.then_inc(self.sem, 1)
        self.k += 1
        self.eng.wait_ge(self.sem, self.base + self.k)


SUMS_AT = 1
SUMS = 6
ADDS = 2 * (SUMS - 1)
RING = 4
WORK, SCORE = 3, 2


def smax_uses(ahead, start=0, stop=HG * HALF // P * 2):
    return [("smax", ahead, hh, qt, n) for hh in range(HG) for qt in range(HALF // P) for n in range(2)][start:stop]


EARLY = (16, 12)
LAST_SMAX = smax_uses(1)[-1]
PRO_USES = smax_uses(1) + [("mrow",)] + smax_uses(2, 0, EARLY[0])
PRO_PLACE = [10, 18, 26]
PRO_PROJ = [(1, 0), (1, 1), (0, 0), (0, 1), (1, 0), (1, 1), (0, 0)]


def half_uses(slot, last):
    odd = slot % 2
    plan = [[] for _ in range(KC)]
    if not (last and slot == 3):
        uses = smax_uses(1, EARLY[odd])
        for kc, n in enumerate((3, 3, 5, 5, 4) if odd else (5, 5, 3, 3)):
            plan[kc] += [uses.pop(0) for _ in range(n)]
        plan[5 if odd else 4].append(("mrow",))
    if not (last and slot >= 2):
        uses = smax_uses(2, 0, EARLY[1 - odd])
        for kc, n in zip(range(KC - 4, KC), (1, 5, 5, 5) if odd else (3, 3, 3, 3)):
            plan[kc] += [uses.pop(0) for _ in range(n)]
    return plan


def half_proj(slot):
    return {2: (1, 0), 4: (1, 1), 6: (0, 0)} if slot % 2 else {0: (0, 1)}


class Half:

    def __init__(self, g, h, last=False):
        self.g, self.h, self.slot, self.last = g, h, h % 4, last
        self.b, self.hf = self.slot // 2, h % 2
        self.first = isinstance(g, int) and g == 0 and h == 0
        self.plan, self.proj = half_uses(self.slot, last), {} if last else half_proj(self.slot)
        self.uses = [u for kc in self.plan for u in kc]
        self.start = len(PRO_USES) + sum(n_uses(i, last) for i in range(h))
        before = len(PRO_USES) if self.first else n_uses(h + 3, last and h > 0)
        self.before = before

    def halves(self, per, plus=0):
        return self.g * (4 * per) + (self.h * per + plus)

    def units(self, per, plus=0):
        return self.g * (2 * per) + (self.h // 2 * per + plus)

    def number(self, j):
        return self.g * GROUP_USES + (self.start + j)

    def bank_before(self, j):
        if j >= WORK:
            return j - WORK
        return max(k for k in range(self.before) if k % WORK == j) - self.before

    def projected(self, plus=0):
        return self.units(4, len(PRO_PROJ) + self.h % 2 + plus)

    def piece(self, kc, hh):
        places = ((kc // 2 * 2, 2), (kc // 2 * 2, 3), (kc // 2 * 2 + 1, 1), (kc // 2 * 2 + 1, 2))
        if (kc, hh) in places and kc // 2 * 2 in self.proj:
            return self.proj[kc // 2 * 2], places.index((kc, hh))
        return None, 0

    def after(self, kc, hh):
        n = len(self.plan[kc])
        return self.plan[kc][(n * hh + HG - 1) // HG:(n * (hh + 1) + HG - 1) // HG]

    def find(self, use):
        return self.uses.index(use)


def n_uses(h, last):
    return sum(len(kc) for kc in half_uses(h % 4, last))


GROUP_USES = sum(n_uses(i, False) for i in range(4))


def all_halves(eng, half, end):
    half(Half(0, 0))
    with eng.Fori(0, NG - 1) as g:
        for h in range(1, 5):
            half(Half(g, h))
    for h in range(1, 4):
        half(Half(NG - 1, h, True))
    end(Half(NG - 1, 4, True))


CONV_BEFORE = {1: ((13, 0),), 2: ((13, 1), (2, 0)), 3: ((13, 2), (2, 1)), 4: ((13, 3), (2, 2)), 5: ((13, 4), (2, 3))}
CONV_OWN = {0: ((13, 5), (2, 4)), 1: ((2, 5),)}


def tail(c):
    return 0 if c < FC - 1 else P - FTAIL


def emit(nc, ctx, x, W, bias, bo, Bm, Am, Wg, W1, W3, W2, sw1, sw3, sw2, out):
    sems = {}

    def sem(name):
        if name not in sems:
            sems[name] = ctx.enter_context(nc.semaphore(name))
        return sems[name]

    bank = [ctx.enter_context(nc.psum_tensor(f"bank{i}", [P, 512], F32))[:] for i in range(8)]
    work, score_bank = bank[0:WORK], bank[WORK:WORK + SCORE]
    pj, ov, dn = bank[5:8]

    wt_d = nc.dram_tensor("wt_d", [4, 2, P, DC, D], F32).ap()
    v_d = nc.dram_tensor("v_d", [T, D], F32).ap()
    attn_d = nc.dram_tensor("attn_d", [D, T], F32).ap()
    xd_d = nc.dram_tensor("xd_d", [E * CAP, D], F32).ap()
    oe_d = nc.dram_tensor("oe_d", [E * CAP, D], F32).ap()
    x_rows = x.rearrange("b l d -> (b l) d")
    out_rows = out.rearrange("b l d -> (b l) d")
    v_rows = v_d.rearrange("(t p) d -> p t d", p=P)
    attn_cols = attn_d.rearrange("(c p) t -> p c t", p=P)

    keep = Arena(nc, (nc.sbuf_base + 31) // 32 * 32, nc.sbuf_usable_end)
    xT = [keep(f"xT{s}", [P, DC, T], FR) for s in ("hi", "lo")]
    ident = keep("ident", [P, P], F32)
    ones32 = keep("ones32", [P, HD], F32)
    wg_raw = keep("wg_raw", [P, DC, E], F32)
    region = keep.at

    att = Arena(nc, region, nc.sbuf_usable_end)
    Qs = [att("Qs0", [P, HG, L], FR)]
    Ks = [att("Ks0", [P, HG, L], FR)]
    plane = [[att(f"plane_{m}{s}", [P, L], FR) for s in ("hi", "lo")] for m in "qk"]
    V = [att(f"V{i}", [P, KC, P], F32) for i in range(2)]
    Wsl = att("Wsl", [P, 2, 2, DC, P], FR)
    bcol = att("bcol", [P, 2], F32)
    mx = [att(f"mx{i}", [P, 16, 2], F32) for i in range(2)]
    nm = att("nm", [P, 16], F32)
    mrow = att("mrow", [16, P], FR)
    rden = att("rden", [P, HALF], F32)
    attn_sb = [att(f"attn_sb{i}", [P, HALF], F32) for i in range(2)]
    overlay = att.at
    Qs.append(att("Qs1", [P, HG, L], FR))
    Ks.append(att("Ks1", [P, HG, L], FR))
    prob = [att(f"prob{i}", [P, HG, HALF], F32) for i in range(RING)]
    psum = att("psum", [P, HG, HALF], F32)

    stp = Arena(nc, overlay, att.at)
    w_raw = [stp(f"w_raw{i}", [P, DC, D], F32) for i in range(2)]
    xin = [stp(f"xin{i}", [P, D], F32) for i in range(4)]
    w_stage = [[stp(f"w_stage{i}{s}", [P, D], FR) for s in ("hi", "lo")] for i in range(2)]
    wv = [stp(f"wv{s}", [P, DC, D], FR) for s in ("hi", "lo")]
    bv_bc = stp("bv_bc", [P, D], F32)
    v_sb = [stp(f"v_sb{i}", [P, D], F32) for i in range(2)]
    lora_a = stp("lora_a", [P, 4, DC, RANK], F32)
    lora_b = stp("lora_b", [P, D], F32)
    lora_at = stp("lora_at", [P, D], F32)

    ffn = Arena(nc, region, nc.sbuf_usable_end)
    rows = ffn("rows", [P, NT, D], F32)
    raw13 = [ffn(f"raw13_{i}", [P, 2, DC, P], F32) for i in range(2)]
    raw2 = [ffn(f"raw2_{i}", [P, D], F32) for i in range(2)]
    r3 = {n: ffn(f"r3_{n}", [P, NT, E], F32) for n in ("lg", "d", "ex", "c", "oh", "s0", "s1", "io")}
    r2 = {n: ffn(f"r2_{n}", [P, NT], F32) for n in ("mx", "sm", "gate", "em", "ps", "keep", "flat", "t", "u", "gk")}
    tri = ffn("tri", [P, P], BF16)
    allone = ffn("allone", [P, P], BF16)
    oh_bf = ffn("oh_bf", [P, NT, E], BF16)
    sidx = ffn("sidx", [P, NT], U32)
    gidx = ffn("gidx", [P, NT], U32)
    st6 = ffn("st6", [P, 4, 6], F32)
    mv = ffn("mv", [P, 4, 2], F32)
    ln_v, ln_s, ln_r, ln_t = (ffn(f"ln_{n}", [P, 4], F32) for n in "vsrt")
    w2_at = ffn.at
    w2 = [ffn(f"w2{s}", [P, FC, D], FR) for s in ("hi", "lo")]
    w13_at = ffn.at
    w13 = [ffn(f"w13{s}", [P, 2 * FC - 1, DC, P], FR) for s in ("hi", "lo")]
    sa = [ffn(f"sa{i}", [P, 512], F32) for i in range(2)]
    hid = [[ffn(f"hid{i}{s}", [P, 512], FR) for s in ("hi", "lo")] for i in range(2)]
    oe_sb = [ffn(f"oe_sb{i}", [P, D], F32) for i in range(2)]
    xdi = sa

    prj = Arena(nc, w2_at, w13_at)
    wo = [prj(f"wo{s}", [P, DC, D], FR) for s in ("hi", "lo")]
    bo_bc = prj("bo_bc", [P, D], F32)
    xr = [prj(f"xr{i}", [P, D], F32) for i in range(2)]
    prj2 = Arena(nc, w13_at, ffn.at)
    at_in = [prj2(f"at_in{i}", [P, DC, P], F32) for i in range(2)]
    at = [[prj2(f"at{i}{s}", [P, DC, P], FR) for s in ("hi", "lo")] for i in range(2)]
    x1b = [prj2(f"x1b{i}", [P, D], F32) for i in range(4)]
    wgp = [prj2(f"wgp{s}", [P, DC, P], FR) for s in ("hi", "lo")]
    yb = [prj2(f"yb{i}", [P, D], F32) for i in range(4)]
    zeros = prj2("zeros", [P, D], F32)
    lgT = prj2("lgT", [E, T], F32)
    cmb = Arena(nc, w2_at, w13_at)
    got = [cmb(f"got{i}", [P, D], F32) for i in range(8)]

    block = ctx.enter_context(nc.Block())

    def f32(ap):
        return ap.bitcast(F32)

    def w_bank(k):
        return bank[(4 if k < 3 * DC else WORK) + k % 2]

    def cols(i, j):
        return bass.ds(i * 512 + j * P, P)

    def up_cols(wd, c):
        return wd.rearrange("(c p) h -> p c h", p=P)[:, :, c * P:min((c + 1) * P, F)]

    @block.sync
    def _(sp):
        def value(e):
            return e if isinstance(e, int) else sp.snap(e)

        for m in range(4):
            sp.dma_start(lora_b[32 * m:32 * m + RANK, :], Bm[m]).then_inc(sem("lora_ld"), 16)
            sp.dma_start(lora_a[:, m], Am[m].rearrange("(c p) r -> p c r", p=P)).then_inc(sem("lora_ld"), 16)

        def load_w(n):
            if n >= 2:
                sp.wait_ge(sem("w_mm"), DC * (n - 1))
            sp.dma_start(w_raw[n % 2][:], W[W_ORDER[n]].rearrange("(c p) d -> p c d", p=P)).then_inc(sem(f"w_ld{n % 2}"), 16)

        def load_x(i):
            for j in range(4):
                if i:
                    sp.wait_ge(sem("x_t"), 4 * i + j - 3)
                sp.dma_start(xin[j][:], x_rows[(4 * i + j) * P:(4 * i + j + 1) * P, :]).then_inc(sem(f"x_ld{j}"), 16)

        load_w(0)
        load_x(0)
        load_w(1)
        sp.dma_start(bv_bc[:], bias[2].rearrange("(o d) -> o d", o=1).to_broadcast([P, D])).then_inc(sem("bv_ld"), 16)
        load_x(1)
        load_w(2)
        load_x(2)
        load_x(3)
        load_w(3)
        sp.dma_start(wg_raw[:], Wg.rearrange("(c p) e -> p c e", p=P)).then_inc(sem("wg_ld"), 16)

        def load_slot(c):
            for m in (1, 0):
                for s in range(2):
                    sp.dma_start(f32(Wsl[:, m, s]), wt_d[m, s][:, :, bass.ds(c, P)]).then_inc(sem("qk"[m] + "_ld"), 16)
                sp.dma_start(bcol[:, m:m + 1],
                             bias[m][bass.ds(c, P)].rearrange("(p o) -> p o", o=1)).then_inc(sem("qk"[m] + "_ld"), 16)

        def load_v(b, c):
            sp.dma_start(V[b][:], v_rows[:, b * KC:(b + 1) * KC, bass.ds(c, P)]).then_inc(sem(f"v_ld{b}"), 16)

        def stack(b, m, pair):
            dst, parts = ((Qs[b], (0, 1, 0)), (Ks[b], (0, 0, 1)))[m]
            for hh in (2 * pair, 2 * pair + 1):
                for r, s in enumerate(parts):
                    sp.dma_start(f32(dst[32 * r:32 * r + 32, hh, :]),
                                 f32(plane[m][s][32 * hh:32 * hh + 32, :])).then_inc(sem(f"{'qk'[m]}_stack_{pair}"), 16)

        def put_mrow(b, hf, need):
            sp.wait_ge(sem("wk_done"), need)
            for hh in range(HG):
                sp.dma_start(f32(Qs[b][96:97, hh, hf * HALF:(hf + 1) * HALF]),
                             f32(mrow[4 * hh:4 * hh + 4, :])).then_inc(sem("mrow_ld"), 16)

        def next_mrow(v):
            if ("mrow",) in v.uses:
                put_mrow((v.slot + 1) % 4 // 2, 1 - v.hf, value(v.number(v.find(("mrow",)) + 1)))

        def stack_unit(b, k_need, q_need, v=None):
            sp.wait_ge(sem("pj_done"), k_need)
            stack(b, 1, 0)
            sp.wait_ge(sem("pj_done"), q_need)
            stack(b, 0, 0)
            if v is not None:
                next_mrow(v)
            stack(b, 1, 1)
            stack(b, 0, 1)

        for i in range(2):
            for s in range(2):
                sp.wait_ge(sem(f"w_st{i}_{s}"), 16 * 4)
        load_slot(0)
        stack_unit(0, 3, 4)
        for i in range(2):
            sp.wait_ge(sem(f"v_st{i}"), 16 * NT // 2)
        load_v(0, 0)
        put_mrow(0, 0, PRO_USES.index(("mrow",)) + 1)
        for i in range(2):
            for s in range(2):
                sp.wait_ge(sem(f"w_st{i}_{s}"), 16 * 6)

        def half(v):
            if v.proj and v.slot % 2 == 0:
                stack_unit(1 - v.b, value(v.projected()), value(v.projected(1)), v)
                c, used = value(v.g * P + (v.h // 4 * P + v.b * P)), value(v.halves(KC))
                if not v.first:
                    sp.wait_ge(sem("pv_done"), used)
                load_v(1 - v.b, c)
            elif v.proj and v.slot == 1:
                c, need = value((v.g + 1) * P), value(v.projected())
                sp.wait_ge(sem("pj_done"), need)
                load_slot(c)
            if not v.proj or v.slot % 2:
                next_mrow(v)
            if not v.first:
                store(v)

        def store(v):
            b, hf = (v.slot + 3) % 4 // 2, 1 - v.hf
            r, need = value(v.g * P), value(v.halves(1, 1))
            sp.wait_ge(sem("at_done"), need)
            sp.dma_start(attn_d[bass.ds(r, P), b * L + hf * HALF:b * L + (hf + 1) * HALF],
                         attn_sb[hf][:]).then_inc(sem(f"at_st{hf}"), 16)

        all_halves(sp, half, store)

        sp.wait_ge(sem("at_st0"), 16 * (2 * NG + 1))
        sp.wait_ge(sem("at_st1"), 16 * (2 * NG + 1))
        for s in range(2):
            sp.dma_start(f32(wo[s][:]), wt_d[3, s]).then_inc(sem("wo_ld"), 16)
        sp.wait_ge(sem("zeros"), 1)
        sp.dma_start(xd_d.rearrange("(n p) d -> p n d", p=P),
                     zeros[:].unsqueeze(1).to_broadcast([P, E * CAP // P, D])).then_inc(sem("xd_zero"), 16)
        sp.dma_start(bo_bc[:], bo.rearrange("(o d) -> o d", o=1).to_broadcast([P, D])).then_inc(sem("bo_ld"), 16)
        with sp.Fori(0, 4) as i:
            for j in range(4):
                r, need = value(i * 512 + j * P), value(i * 4 + (j + 1))
                sp.wait_ge(sem("at_lo"), need)
                sp.dma_start(at_in[j % 2][:], attn_cols[:, :, bass.ds(r, P)]).then_inc(sem(f"at_ld{j % 2}"), 16)
                sp.wait_ge(sem("y_done"), need)
                sp.dma_start(xr[j % 2][:], x_rows[bass.ds(r, P), :]).then_inc(sem(f"xr_ld{j % 2}"), 16)

        def load13(wa, wb, c):
            if c < FC - 1:
                da, db = raw13[c % 2][:, 0], raw13[c % 2][:, 1]
            else:
                da, db = raw13[c % 2][:, 0, :, 0:FTAIL], raw13[c % 2][:, 0, :, FTAIL:P]
            sp.dma_start(da, up_cols(wa, c)).then_inc(sem(f"raw13_ld{c % 2}"), 16)
            sp.dma_start(db, up_cols(wb, c)).then_inc(sem(f"raw13_ld{c % 2}"), 16)

        def load2(wc, c):
            sp.dma_start(raw2[c % 2][tail(c):P, :], wc[c * P:min((c + 1) * P, F), :]).then_inc(sem(f"raw2_ld{c % 2}"), 16)

        def load_set(wa, wb, wc, done, chunks):
            for kind, c in chunks:
                name = "conv13" if kind == 13 else "conv2"
                if not (isinstance(done, int) and done + c < 2):
                    need = value(done + (c - 1))
                    sp.wait_ge(sem(name), need)
                if kind == 13:
                    load13(wa, wb, c)
                else:
                    load2(wc, c)

        in_set = [kc for c in range(1, FC) for kc in CONV_BEFORE[c]]
        own = [kc for c in (0, 1) for kc in CONV_OWN[c]]
        load_set(sw1, sw3, sw2, 0, in_set + own)
        load_set(W1[0], W3[0], W2[0], FC, in_set)
        sp.wait_ge(sem("scat"), 16 * NT)
        sp.wait_ge(sem("hid_lo"), 24 + 2)
        with sp.Fori(0, NT // 2) as i:
            for j in range(2):
                r, need = value(i * 2 * P + j * P), value(i * 2 + (j + 1))
                sp.wait_ge(sem("xd_t"), need)
                sp.dma_start(xdi[j][:], xd_d[bass.ds(r, P), :]).then_inc(sem(f"xd_ld{j}"), 16)
        load_set(W1[0], W3[0], W2[0], FC, own)
        with sp.Fori(1, E) as e:
            ee = value(e)
            w1e, w3e, w2e = (w[bass.ds(ee, 1)].rearrange("o a b -> (o a) b") for w in (W1, W3, W2))
            load_set(w1e, w3e, w2e, e * FC + FC, in_set + own)

        for t in range(NT):
            sp.wait_ge(sem("out_rdy"), t + 1)
            sp.dma_start(out_rows[t * P:(t + 1) * P, :], rows[:, t]).then_inc(sem("out_st"), 16)
        sp.wait_ge(sem("out_st"), 16 * NT)

    @block.gpsimd
    def _(po):
        po.memset(ident[:], 0.0).then_inc(sem("blank"), 1)
        po.memset(ones32[:], 1.0).then_inc(sem("const"), 1)
        po.wait_ge(sem("blank"), 1)
        po.affine_select(out=ident[:], in_=ident[:], compare_op=ALU.not_equal, fill=1.0, base=0,
                         pattern=[[-1, P]], channel_multiplier=1).then_inc(sem("const"), 1)

        def store_w(n):
            m = W_ORDER[n]
            for dc in range(DC):
                k = (n - 1) * DC + dc
                po.wait_ge(sem("w_lo"), k + DC + 1)
                for s in range(2):
                    po.dma_start(wt_d[m, s][:, dc, :], f32(w_stage[k % 2][s][:])).then_inc(sem(f"w_st{k % 2}_{s}"), 16)

        def store_v(i):
            for t in range(4 * i, 4 * i + 4):
                po.wait_ge(sem("v_done"), t + 1)
                po.dma_start(v_d[t * P:(t + 1) * P, :], v_sb[t % 2][:]).then_inc(sem(f"v_st{t % 2}"), 16)

        store_w(1)
        store_v(0)
        store_w(2)
        for i in range(1, 4):
            store_v(i)
        store_w(3)
        for i in range(2):
            for s in range(2):
                po.wait_ge(sem(f"w_st{i}_{s}"), 16 * 6)
            po.wait_ge(sem(f"v_st{i}"), 16 * NT // 2)
        po.wait_ge(sem("x_lo"), NT)
        for i in range(2):
            po.memset(f32(Ks[i][96:97, :, :]), 1.0).then_inc(sem("ks_ones"), 1)

        def sums(v, first):
            if not first:
                po.wait_ge(sem("den_done"), v)
            for kc in range(1, SUMS):
                for p in range(2):
                    pr = slice(2 * p, 2 * p + 2)
                    po.wait_ge(sem("exp_done"), v * (HG * KC) + (HG * kc + 2 * p + 2))
                    if kc > 1:
                        po.wait_ge(sem("sum_done"), v * ADDS + (2 * (kc - 2) + p + 1))
                    po.tensor_tensor(psum[:, pr], (prob[0] if kc == 1 else psum)[:, pr], prob[kc % RING][:, pr],
                                     ALU.add).then_inc(sem("sum_done"), 1)

        sums(0, True)
        with po.Fori(1, 4 * NG) as v:
            sums(v, False)

        po.wait_ge(sem("at_st0"), 16 * (2 * NG + 1))
        po.wait_ge(sem("at_st1"), 16 * (2 * NG + 1))
        po.memset(zeros[:], 0.0).then_inc(sem("zeros"), 1)
        po.memset(tri[:], 1.0).then_inc(sem("blank"), 1)
        po.memset(allone[:], 1.0).then_inc(sem("rt_const"), 1)
        for s in range(2):
            po.memset(f32(wgp[s][:]), 0.0).then_inc(sem("wgp_zero"), 1)
        po.wait_ge(sem("blank"), 2)
        po.affine_select(out=tri[:], in_=tri[:], compare_op=ALU.is_ge, fill=0.0, base=0,
                         pattern=[[1, P]], channel_multiplier=-1).then_inc(sem("rt_const"), 1)
        po.iota(r3["io"][:], pattern=[[0, NT], [1, E]], base=-E, channel_multiplier=0,
                allow_small_or_imprecise_dtypes=True).then_inc(sem("iota"), 1)
        po.wait_ge(sem("bo_ld"), 16)
        with po.Fori(0, 4) as i:
            for j in range(4):
                po.wait_ge(sem(f"xr_ld{j % 2}"), i * 32 + 16 * (j // 2 + 1))
                po.tensor_tensor(xr[j % 2][:], xr[j % 2][:], bo_bc[:], ALU.add).then_inc(sem("xb_rdy"), 1)

        po.wait_ge(sem("xd_zero"), 16)
        po.wait_ge(sem("x1_put"), NT + 4)
        po.wait_ge(sem("routed"), 1)
        for t in range(NT):
            po.indirect_dma_start(out=xd_d, out_offset=bass.IndirectOffsetOnAxis(ap=sidx[:, t:t + 1], axis=0),
                                  in_=rows[:, t, :], in_offset=None, bounds_check=E * CAP - 1,
                                  oob_is_err=False).then_inc(sem("scat"), 16)

        with po.Fori(0, E) as e:
            for i in range(2):
                po.wait_ge(sem("oe_rdy"), e * 2 + (i + 3))
                po.dma_start(oe_d[bass.ds(e * CAP + i * P, P), :], oe_sb[i][:]).then_inc(sem(f"oe_st{i}"), 16)

        for i in range(2):
            po.wait_ge(sem(f"oe_st{i}"), 16 * E)
        for t in range(NT):
            if t >= 8:
                po.wait_ge(sem("z_done"), t - 7)
            po.indirect_dma_start(out=got[t % 8][:], out_offset=None, in_=oe_d,
                                  in_offset=bass.IndirectOffsetOnAxis(ap=gidx[:, t:t + 1], axis=0),
                                  bounds_check=E * CAP - 1, oob_is_err=False).then_inc(sem(f"gath{t % 8}"), 16)

    @block.tensor
    def _(pe):
        def split3(dst, lhs, rhs):
            for dc in range(DC):
                for k, (a, b) in enumerate(SPLIT):
                    mm = nc.tensor.matmul(dst, lhs(a, dc), rhs(b, dc), start=dc == 0 and k == 0,
                                          stop=dc == DC - 1 and k == 2)
            return mm

        def turn(dst, src):
            for c in range(DC):
                mm = nc.tensor.transpose(dst[:, c * P:(c + 1) * P], src[:, c * P:(c + 1) * P], ident[:])
            return mm

        pe.sem_inc(sem("o_full"), 2)
        pe.sem_inc(sem("used2"), 2)
        pe.sem_inc(sem("xd_t"), 2)

        pe.wait_ge(sem("const"), 2)
        pe.wait_ge(sem("lora_ld"), 16 * 8)
        for n, m in enumerate(W_ORDER):
            for oc in range(DC):
                mm = nc.tensor.transpose(bank[n][0:RANK, oc * P:(oc + 1) * P], lora_a[:, m, oc, :], ident[:])
            mm.then_inc(sem("a_t"), 1)

        def weights(n, start=0, stop=DC):
            m = W_ORDER[n]
            pe.wait_ge(sem("a_ev"), n + 1)
            pe.wait_ge(sem(f"w_ld{n % 2}"), 16 * (n // 2 + 1))
            for dc in range(start, stop):
                k = n * DC + dc
                dst = w_bank(k)
                if k >= 2:
                    pe.wait_ge(sem("w_lo"), k - 1)
                nc.tensor.matmul(dst, lora_b[32 * m:32 * m + RANK, dc * P:(dc + 1) * P],
                                 lora_at[32 * m:32 * m + RANK, :], start=True, stop=False)
                for oc in range(DC):
                    mm = nc.tensor.matmul(dst[:, oc * P:(oc + 1) * P], w_raw[n % 2][:, oc, dc * P:(dc + 1) * P],
                                          ident[:], start=False, stop=oc == DC - 1)
                mm.then_inc(sem("w_mm"), 1)

        def turn_x(i):
            for j in range(4):
                pe.wait_ge(sem(f"x_ld{j}"), i * 16 + 16)
                if i:
                    pe.wait_ge(sem("x_lo"), i * 4 + (j - 3))
                turn(bank[j], xin[j]).then_inc(sem("x_t"), 1)

        def make_v(i):
            pe.wait_ge(sem("w_lo"), DC)
            for t in range(4 * i, 4 * i + 4):
                pe.wait_ge(sem("x_lo"), t + 1)
                if t >= 2:
                    pe.wait_ge(sem("v_done"), t - 1)
                split3(bank[6 + t % 2], lambda a, dc: xT[a][:, dc, t * P:(t + 1) * P],
                       lambda p, dc: wv[p][:, dc, :]).then_inc(sem("v_mm"), 1)

        weights(0)
        pe.wait_ge(sem("a_ev"), 4)
        turn_x(0)
        weights(1)
        make_v(0)
        turn_x(1)
        weights(2)
        make_v(1)
        for i in (2, 3):
            turn_x(i)
            make_v(i)

        def project_unit(m, ph, b, quarters, n, ld_need):
            if 0 in quarters:
                pe.wait_ge(sem("qk"[m] + "_ld"), ld_need)
                if n is not None:
                    pe.wait_ge(sem("pj_done"), n)
            cols = slice(b * L + ph * HALF, b * L + (ph + 1) * HALF)
            for dc in quarters:
                for k, (a, p) in enumerate(SPLIT):
                    mm = nc.tensor.matmul(pj, Wsl[:, m, a, dc, :], xT[p][:, dc, cols], start=dc == 0 and k == 0,
                                          stop=dc == DC - 1 and k == 2)
            if DC - 1 in quarters:
                mm.then_inc(sem("pj_full"), 1)

        def use(j, kind, slot, nm_need):
            dst = work[j % WORK]
            if kind[0] == "smax":
                _, ahead, hh, qt, part = kind
                b, hf = (slot + ahead) % 4 // 2, (slot + ahead) % 2
                q0 = hf * HALF + qt * P
                mm = nc.tensor.matmul(dst, Qs[b][0:96, hh, q0:q0 + P], Ks[b][0:96, hh, part * 512:part * 512 + 512],
                                      start=True, stop=True)
            else:
                pe.wait_ge(sem("nm_rdy"), nm_need)
                mm = nc.tensor.transpose(dst[0:16, 0:P], nm[:], ident[:])
            mm.then_inc(sem("wk_full"), 1)

        pe.wait_ge(sem("x_lo"), NT)
        for n, (m, ph) in enumerate(PRO_PROJ[:4]):
            project_unit(m, ph, 0, range(DC), n or None, 48)
            weights(3, n, n + 1)
        for n, kind in enumerate(PRO_USES):
            if kind[0] == "smax" and kind[1] == 1 and kind[2] in (0, 2) and kind[3:] == (0, 0):
                pe.wait_ge(sem(f"k_stack_{kind[2] // 2}"), 96)
                pe.wait_ge(sem(f"q_stack_{kind[2] // 2}"), 96)
            if n >= WORK:
                pe.wait_ge(sem("wk_done"), n - WORK + 1)
            use(n, kind, 3, 1)
            if n in PRO_PLACE:
                i = 4 + PRO_PLACE.index(n)
                project_unit(*PRO_PROJ[i], 1, range(DC), i, 48)
        pe.wait_ge(sem("ks_ones"), 2)
        pe.wait_ge(sem("w_lo"), 4 * DC)
        pe.wait_ge(sem("v_done"), NT)

        def score(v, i):
            kc, hh = i // HG, i % HG
            if i >= SCORE:
                pe.wait_ge(sem("exp_done"), v.halves(HG * KC, i - SCORE + 1))
            elif not v.first:
                held = max(k for k in range(HG * KC) if k % SCORE == i)
                pe.wait_ge(sem("exp_done"), v.halves(HG * KC, held + 1 - HG * KC))
            nc.tensor.matmul(score_bank[i % SCORE], Ks[v.b][0:97, hh, kc * P:(kc + 1) * P],
                             Qs[v.b][0:97, hh, v.hf * HALF:(v.hf + 1) * HALF], start=True,
                             stop=True).then_inc(sem("st_full"), 1)

        def values(v, kc):
            pe.wait_ge(sem("exp_done"), v.halves(HG * KC, HG * (kc + 1)))
            b = v.b if kc >= 0 else (v.slot + 3) % 4 // 2
            if kc == 0:
                pe.wait_ge(sem(f"v_ld{b}"), v.g * 16 + (v.h // 4 * 16 + 16))
                if not v.first:
                    pe.wait_ge(sem("ov_read"), v.halves(1))
            for hh in range(HG):
                mm = nc.tensor.matmul(ov[hh * HD:(hh + 1) * HD, :], V[b][:, kc % KC, hh * HD:(hh + 1) * HD],
                                      prob[kc % RING][:, hh, :], start=kc == 0, stop=kc == -1 or kc == KC - 1)
            mm.then_inc(sem("pv_done"), 1)

        def sums(v, parts, first, last):
            for k, part in enumerate(parts):
                for hh in range(HG):
                    mm = nc.tensor.matmul(dn[hh * HD:(hh + 1) * HD, :], ones32[:], part[:, hh, :],
                                          start=first and k == 0, stop=last and k == len(parts) - 1)
            return mm

        def late_sums(v):
            pe.wait_ge(sem("at_done"), v.halves(1))
            sums(v, [prob[kc % RING] for kc in range(SUMS, KC)], True, False).then_inc(sem("late_done"), 1)

        def early_sums(v):
            pe.wait_ge(sem("sum_done"), v.halves(ADDS))
            sums(v, [psum], False, True).then_inc(sem("den_done"), 1)

        def half(v):
            pe.wait_ge(sem("mrow_ld"), v.halves(64, 64))
            j = 0
            for kc in range(KC):
                for i in range(HG):
                    score(v, HG * kc + i)
                    if i == 2 and (kc or not v.first):
                        values(v, kc - 1)
                    if i == 3 and kc == 0 and not v.first:
                        late_sums(v)
                    if i == 3 and kc == SUMS_AT and not v.first:
                        early_sums(v)
                    proj, quarter = v.piece(kc, i)
                    if proj:
                        m, ph = proj
                        project_unit(m, ph, (1 + v.b + v.h) % 2, (quarter,), v.projected(ph + 2 * (1 - m) if v.hf else 0),
                                     v.g * 48 + (96 if v.h else 48))
                    for kind in v.after(kc, i):
                        if kind[0] == "smax" and kind[2] in (0, 2) and kind[3:] == (0, 0):
                            unit = v.g * 192 + ((v.h + kind[1]) // 2 * 96 + 96)
                            pe.wait_ge(sem(f"k_stack_{kind[2] // 2}"), unit)
                            pe.wait_ge(sem(f"q_stack_{kind[2] // 2}"), unit)
                        pe.wait_ge(sem("wk_done"), v.number(v.bank_before(j) + 1))
                        use(j, kind, v.slot, v.halves(1, 2))
                        j += 1

        def end(v):
            values(v, -1)
            late_sums(v)
            early_sums(v)

        all_halves(pe, half, end)

        pe.wait_ge(sem("wk_done"), Half(NG - 1, 4, True).number(0))
        pe.wait_ge(sem("ov_read"), 4 * NG)
        pe.wait_ge(sem("at_done"), 4 * NG + 1)
        pe.wait_ge(sem("wo_ld"), 32)
        pe.wait_ge(sem("wgp_lo"), 1)

        def project(i):
            for j in range(4):
                pe.wait_ge(sem("at_lo"), i * 4 + (j + 3))
                if not isinstance(i, int):
                    pe.wait_ge(sem("y_done"), i * 4 + (j - 1))
                split3(bank[(0, 1, 4, 5)[j]], lambda a, dc: at[j % 2][a][:, dc, :],
                       lambda p, dc: wo[p][:, dc, :]).then_inc(sem("o_full"), 1)

        def turn_x1(i):
            for j in range(4):
                pe.wait_ge(sem("x1_rdy"), i * 4 + (j + 1))
                pe.wait_ge(sem("x1_lo"), i * 4 + (j + 3))
                turn(bank[2 + j % 2], x1b[j]).then_inc(sem("x1_t"), 1)
            pe.wait_ge(sem("x1_lo"), i * 4 + 8)
            pe.wait_ge(sem("lg_ev"), i + 1)
            split3(bank[6], lambda a, dc: wgp[a][:, dc, :],
                   lambda p, dc: xT[p][:, dc, bass.ds(i * 512, 512)]).then_inc(sem("lg_full"), 1)

        project(0)
        with pe.Fori(1, 4) as i:
            project(i)
            turn_x1(i - 1)
        turn_x1(3)

        pe.wait_ge(sem("lg_ev"), 5)
        for t in range(NT):
            mm = nc.tensor.transpose(bank[7][:, t * E:(t + 1) * E], lgT[:, t * P:(t + 1) * P], ident[0:E, 0:E])
        mm.then_inc(sem("rt_mm"), 1)
        pe.wait_ge(sem("rt_const"), 2)
        pe.wait_ge(sem("oh_rdy"), 1)
        nc.tensor.matmul(bank[0][:, 0:P], tri[:], oh_bf[:].rearrange("p t e -> p (t e)"), start=True, stop=True)
        nc.tensor.matmul(bank[1][:, 0:P], allone[:], oh_bf[:].rearrange("p t e -> p (t e)"), start=True,
                         stop=True).then_inc(sem("rt_mm"), 1)

        def ff(q, sets, width, rhs, banks_read):
            def down(c):
                if c == 0:
                    pe.wait_ge(*banks_read)
                pe.wait_ge(sem("hid_lo"), q + (c + 3))
                pe.wait_ge(sem("conv2"), sets + (c + 1))
                p0 = tail(c)
                for i in range(width // P):
                    for k, (a, p) in enumerate(SPLIT):
                        mm = nc.tensor.matmul(bank[4 + i], hid[c % 2][a][p0:P, i * P:(i + 1) * P], w2[p][p0:P, c, :],
                                              start=c == 0 and k == 0, stop=c == FC - 1 and k == 2)
                mm.then_inc(sem("used2"), 1)

            for c in range(FC):
                pe.wait_ge(sem("conv13"), sets + (c + 1))
                pe.wait_ge(sem("h_done"), q + (c + 1))
                mm = split3(bank[2 * (c % 2)][:, 0:width], lambda a, dc: w13[a][:, 2 * c, dc, :], rhs)
                if c < FC - 1:
                    mm = split3(bank[2 * (c % 2) + 1][:, 0:width], lambda a, dc: w13[a][:, 2 * c + 1, dc, :], rhs)
                mm.then_inc(sem("ab_full"), 1)
                if c:
                    down(c - 1)
            down(FC - 1)

        pe.wait_ge(sem("pos_rdy"), 1)
        with pe.Fori(0, 4) as i:
            ff(i * FC, 0, 512, lambda p, dc: xT[p][:, dc, bass.ds(i * 512, 512)],
               (sem("acc_done"), i * 4 + 1))
        pe.wait_ge(sem("h_done"), 4 * FC + 2)
        pe.wait_ge(sem("acc_done"), NT + 1)
        with pe.Fori(0, NT // 4) as i:
            for j in range(4):
                pe.wait_ge(sem(f"xd_ld{j % 2}"), i * 32 + 16 * (j // 2 + 1))
                pe.wait_ge(sem("xd_lo"), i * 4 + (j + 1))
                turn(bank[j], xdi[j % 2]).then_inc(sem("xd_t"), 1)
        pe.wait_ge(sem("xd_lo"), NT + 4)
        with pe.Fori(0, E) as e:
            ff(e * FC + 4 * FC, e * FC + FC, CAP, lambda p, dc: xT[p][:, dc, bass.ds(e * CAP, CAP)],
               (sem("oe_rdy"), e * 2 + 2))

    @block.scalar
    def _(ac):
        ACTV = nc.scalar.activation
        ac.sem_inc(sem("lg_ev"), 1)
        ac.sem_inc(sem("x1_put"), 4)
        ac.sem_inc(sem("oe_rdy"), 2)

        def turned(i, j, src, full, done):
            ac.wait_ge(sem(full[0]), i * 4 + (j + 1 + full[1]))
            ACTV(xT[0][:, :, cols(i, j)], src.rearrange("p (c n) -> p c n", c=DC), ACT.Identity).then_inc(sem(done), 1)

        for n, m in enumerate(W_ORDER):
            ac.wait_ge(sem("a_t"), n + 1)
            ACTV(lora_at[32 * m:32 * m + RANK, :], bank[n][0:RANK, :], ACT.Copy, scale=LORA).then_inc(sem("a_ev"), 1)

        def weights(n, start=0, stop=DC):
            for dc in range(start, stop):
                k = n * DC + dc
                ac.wait_ge(sem("w_mm"), k + 1)
                if k >= DC + 2:
                    ac.wait_ge(sem(f"w_st{k % 2}_0"), 16 * ((k - DC) // 2))
                ACTV(wv[0][:, dc, :] if n == 0 else w_stage[k % 2][0][:], w_bank(k),
                     ACT.Identity).then_inc(sem("w_hi"), 1)

        def turned_x(i):
            for j in range(4):
                turned(i, j, bank[j], ("x_t", 0), "x_hi")

        weights(0)
        turned_x(0)
        weights(1)
        turned_x(1)
        weights(2)
        turned_x(2)
        turned_x(3)

        def plane_hi(m, ph, n, slot_need, stack_need):
            ac.wait_ge(sem("pj_full"), n)
            ac.wait_ge(sem("qk"[m] + "_ld"), slot_need)
            if stack_need is not None:
                for pair in range(HG // 2):
                    ac.wait_ge(sem(f"{'qk'[m]}_stack_{pair}"), stack_need)
            ACTV(plane[m][0][:, ph * HALF:(ph + 1) * HALF], pj, ACT.Identity,
                 bias=bcol[:, m:m + 1]).then_inc(sem("pl_hi"), 1)

        for n, (m, ph) in enumerate(PRO_PROJ[:4]):
            plane_hi(m, ph, n + 1, 48, None)
            weights(3, n, n + 1)
        for i in range(2):
            for s in range(2):
                ac.wait_ge(sem(f"w_st{i}_{s}"), 16 * 6)
            ac.wait_ge(sem(f"v_st{i}"), 16 * NT // 2)
        for n, (m, ph) in enumerate(PRO_PROJ[4:]):
            plane_hi(m, ph, n + 5, 48, 96)

        def half(v):
            for kc in range(KC):
                if kc >= RING or not v.first:
                    ac.wait_ge(sem("pv_done"), v.halves(KC, kc - RING + 1))
                if kc >= RING:
                    ac.wait_ge(sem("sum_done"), v.halves(ADDS, max(2, 2 * (kc - RING))))
                elif not v.first:
                    held = KC - RING + kc
                    if held < SUMS:
                        ac.wait_ge(sem("sum_done"), v.halves(ADDS, 2 * held - ADDS))
                    else:
                        ac.wait_ge(sem("late_done"), v.halves(1))
                for hh in range(HG):
                    i = HG * kc + hh
                    ac.wait_ge(sem("st_full"), v.halves(HG * KC, i + 1))
                    ACTV(prob[kc % RING][:, hh, :], score_bank[i % SCORE], ACT.Exp, scale=SCALE).then_inc(sem("exp_done"), 1)
                    if kc == 0 and hh == HG - 1 and not v.first:
                        take_ov(v)
                    if hh == 2 and kc - 1 in v.proj:
                        m, ph = v.proj[kc - 1]
                        plane_hi(m, ph, v.projected(1 + (ph + 2 * (1 - m) if v.hf else 0)), v.g * 48 + (96 if v.h else 48),
                                 v.units(96, 96 * (1 + v.hf)))

        def take_ov(v):
            hf = 1 - v.hf
            ac.wait_ge(sem("pv_done"), v.halves(KC))
            ac.wait_ge(sem(f"at_st{hf}"), v.g * 32 + (16 * ((v.h - 1) // 2) + 16))
            ACTV(attn_sb[hf][:], ov, ACT.Copy).then_inc(sem("ov_read"), 1)

        all_halves(ac, half, take_ov)

        ac.wait_ge(sem("wgp_zero"), 2)
        ac.wait_ge(sem("wg_ld"), 16)
        ACTV(wgp[0][:, :, 0:E], wg_raw[:], ACT.Identity).then_inc(sem("wgp_hi"), 1)

        def at_hi(i):
            for j in range(4):
                ac.wait_ge(sem(f"at_ld{j % 2}"), i * 32 + 16 * (j // 2 + 1))
                ac.wait_ge(sem("o_full"), i * 4 + (j + 1))
                ACTV(at[j % 2][0][:], at_in[j % 2][:], ACT.Identity).then_inc(sem("at_hi"), 1)

        def x1_hi(i):
            for j in range(4):
                turned(i, j, bank[2 + j % 2], ("x1_t", 0), "x1_hi")
                ACTV(rows[:, bass.ds(i * 4 + j, 1), :].rearrange("p o d -> p (o d)"), x1b[j][:],
                     ACT.Copy).then_inc(sem("x1_put"), 1)
            ac.wait_ge(sem("lg_full"), i + 1)
            ACTV(lgT[:, bass.ds(i * 512, 512)], bank[6][0:E, :], ACT.Copy).then_inc(sem("lg_ev"), 1)

        def root(k, name):
            ac.wait_ge(sem(name + "_var"), k)
            ACTV(ln_s[:], ln_v[:], ACT.Sqrt).then_inc(sem(name + "_root"), 1)

        at_hi(0)
        root(1, "ln1")
        with ac.Fori(1, 4) as i:
            at_hi(i)
            x1_hi(i - 1)
            root(i + 1, "ln1")
        x1_hi(3)
        ac.wait_ge(sem("rt_d"), 1)
        ACTV(r3["ex"][:], r3["d"][:], ACT.Exp).then_inc(sem("rt_ex"), 1)

        def conv(kind, c, sets, need):
            if kind == 13:
                ac.wait_ge(sem(f"raw13_ld{c % 2}"), sets * 96 + 32 * (c // 2 + 1))
                if need is not None:
                    ac.wait_ge(sem("ab_full"), need + (c + 1))
                s0, s1 = 2 * c, min(2 * c + 2, 2 * FC - 1)
                ACTV(w13[0][:, s0:s1], raw13[c % 2][:, 0:s1 - s0], ACT.Identity).then_inc(sem("conv13_hi"), 1)
            else:
                ac.wait_ge(sem(f"raw2_ld{c % 2}"), sets * 48 + 16 * (c // 2 + 1))
                if need is not None:
                    ac.wait_ge(sem("used2"), need + (c + 3))
                ACTV(w2[0][tail(c):P, c], raw2[c % 2][tail(c):P, :], ACT.Identity).then_inc(sem("conv2_hi"), 1)

        def steps(q, width, own, ahead):
            for c in range(FC):
                r, p0 = c % 2, tail(c)
                ac.wait_ge(sem("ab_full"), q + (c + 1))
                ac.wait_ge(sem("hid_lo"), q + (c + 1))
                ACTV(sa[r][p0:P, 0:width], bank[2 * r][0:P - p0, 0:width], ACT.Silu).then_inc(sem("sa_rdy"), 1)
                ac.wait_ge(sem("h_done"), q + (c + 3))
                ac.wait_ge(sem("used2"), q + (c + 1))
                ACTV(hid[r][0][p0:P, 0:width], sa[r][p0:P, 0:width], ACT.Identity).then_inc(sem("hid_hi"), 1)
                for kind, cc in CONV_OWN.get(c, ()) if own else ():
                    conv(kind, cc, *own)
                for kind, cc in CONV_BEFORE.get(c, ()) if ahead else ():
                    conv(kind, cc, *ahead)

        ac.wait_ge(sem("lg_read"), 1)
        ac.wait_ge(sem("x1_put"), NT + 4)
        ac.wait_ge(sem("xd_zero"), 16)
        for c in range(1, FC):
            for kind, cc in CONV_BEFORE[c]:
                conv(kind, cc, 0, None)
        for c in range(2):
            for kind, cc in CONV_OWN[c]:
                conv(kind, cc, 0, None)
        with ac.Fori(0, 3) as i:
            steps(i * FC, 512, None, None)
        steps(3 * FC, 512, None, (1, 3 * FC))
        with ac.Fori(0, NT // 4) as i:
            for j in range(4):
                turned(i, j, bank[j], ("xd_t", 2), "xd_hi")

        def expert(e, first=False, last=False):
            steps(e * FC + 4 * FC, CAP, (e + 1, e * FC + 3 * FC), None if last else (e + 2, e * FC + 4 * FC))
            ac.wait_ge(sem("used2"), e * FC + (5 * FC + 2))
            for i in range(2):
                if not first:
                    ac.wait_ge(sem(f"oe_st{i}"), e * 16)
                ACTV(oe_sb[i][:], bank[4 + i], ACT.Copy).then_inc(sem("oe_rdy"), 1)

        expert(0, first=True)
        with ac.Fori(1, E - 1) as e:
            expert(e)
        expert(E - 1, last=True)
        for k in range(4):
            root(k + 1, "ln2")

    @block.vector
    def _(ve):
        TT, TS, RED = nc.vector.tensor_tensor, nc.vector.tensor_scalar, nc.vector.tensor_reduce
        ve.sem_inc(sem("at_done"), 1)
        ve.sem_inc(sem("y_done"), 2)
        ve.sem_inc(sem("at_lo"), 2)
        ve.sem_inc(sem("x1_lo"), 4)
        ve.sem_inc(sem("xd_lo"), 4)
        ve.sem_inc(sem("h_done"), 2)
        ve.sem_inc(sem("hid_lo"), 2)
        ve.sem_inc(sem("acc_done"), 1)
        for i in range(2):
            ve.sem_inc(sem(f"at_st{i}"), 16)

        def turned(i, j, src, hi, lo):
            ve.wait_ge(sem(hi), i * 4 + (j + 1))
            TT(xT[1][:, :, cols(i, j)], src.rearrange("p (c n) -> p c n", c=DC), f32(xT[0][:, :, cols(i, j)]),
               ALU.subtract).then_inc(sem(lo), 1)

        def weights(n, start=0, stop=DC):
            for dc in range(start, stop):
                k = n * DC + dc
                hi, lo = (wv[s][:, dc, :] if n == 0 else w_stage[k % 2][s][:] for s in range(2))
                ve.wait_ge(sem("w_hi"), k + 1)
                if k >= DC + 2:
                    ve.wait_ge(sem(f"w_st{k % 2}_1"), 16 * ((k - DC) // 2))
                TT(lo, w_bank(k), f32(hi), ALU.subtract).then_inc(sem("w_lo"), 1)

        def turned_x(i):
            for j in range(4):
                turned(i, j, bank[j], "x_hi", "x_lo")

        def make_v(i):
            for t in range(4 * i, 4 * i + 4):
                ve.wait_ge(sem("v_mm"), t + 1)
                if t >= 2:
                    ve.wait_ge(sem(f"v_st{t % 2}"), 16 * (t // 2))
                TT(v_sb[t % 2][:], bank[6 + t % 2], bv_bc[:], ALU.add).then_inc(sem("v_done"), 1)

        weights(0)
        turned_x(0)
        weights(1)
        ve.wait_ge(sem("bv_ld"), 16)
        make_v(0)
        turned_x(1)
        weights(2)
        make_v(1)
        for i in (2, 3):
            turned_x(i)
            make_v(i)

        def plane_lo(m, ph, n):
            part = slice(ph * HALF, (ph + 1) * HALF)
            ve.wait_ge(sem("pl_hi"), n)
            nc.vector.scalar_tensor_tensor(out=plane[m][1][:, part], in0=pj, scalar=bcol[:, m:m + 1],
                                           in1=f32(plane[m][0][:, part]), op0=ALU.add,
                                           op1=ALU.subtract).then_inc(sem("pj_done"), 1)

        def use(kind, j, n, hf, stack_need):
            src = work[j % WORK]
            ve.wait_ge(sem("wk_full"), n)
            if kind[0] == "smax":
                _, ahead, hh, qt, part = kind
                ins = RED(mx[(hf + ahead) % 2][:, 4 * hh + qt, part:part + 1], src, AX.X, ALU.max)
            else:
                if stack_need is not None:
                    ve.wait_ge(sem("mrow_ld"), stack_need)
                ins = nc.vector.tensor_copy(mrow[:], src[0:16, 0:P])
            ins.then_inc(sem("wk_done"), 1)
            if kind == LAST_SMAX:
                ve.wait_ge(sem("wk_done"), n)
                RED(nm[:], mx[1 - hf][:], AX.X, ALU.max, negate=True).then_inc(sem("nm_rdy"), 1)

        for n, (m, ph) in enumerate(PRO_PROJ[:4]):
            plane_lo(m, ph, n + 1)
            weights(3, n, n + 1)
        for n, kind in enumerate(PRO_USES):
            use(kind, n, n + 1, 1, None)
            if n - 1 in PRO_PLACE:
                i = 4 + PRO_PLACE.index(n - 1)
                plane_lo(*PRO_PROJ[i], i + 1)

        def half(v):
            j = 0
            for kc, uses in enumerate(v.plan):
                for kind in uses:
                    use(kind, j, v.number(j + 1), v.hf, v.halves(64, 64))
                    j += 1
                if kc - 1 in v.proj:
                    m, ph = v.proj[kc - 1]
                    plane_lo(m, ph, v.projected(1 + (ph + 2 * (1 - m) if v.hf else 0)))
                if 3 <= kc < 7 and not v.first:
                    invert(v, kc - 3, kc - 2)
                    if kc == 6:
                        norm_out(v)

        def invert(v, start, stop):
            if start == 0:
                ve.wait_ge(sem("den_done"), v.halves(1))
            for q in range(start, stop):
                nc.vector.reciprocal(rden[:, q * P:(q + 1) * P], dn[:, q * P:(q + 1) * P]).then_inc(sem("rden"), 1)

        def norm_out(v):
            hf = 1 - v.hf
            ve.wait_ge(sem("rden"), v.halves(4))
            ve.wait_ge(sem("ov_read"), v.halves(1))
            TT(attn_sb[hf][:], attn_sb[hf][:], rden[:], ALU.mult).then_inc(sem("at_done"), 1)

        def end(v):
            invert(v, 0, 4)
            norm_out(v)

        all_halves(ve, half, end)

        ve.wait_ge(sem("wgp_hi"), 1)
        TT(wgp[1][:, :, 0:E], wg_raw[:], f32(wgp[0][:, :, 0:E]), ALU.subtract).then_inc(sem("wgp_lo"), 1)

        def row(t):
            return rows[:, bass.ds(t, 1), :].rearrange("p o d -> p (o d)")

        def at_rest(i, j):
            ve.wait_ge(sem("at_hi"), i * 4 + (j + 1))
            TT(at[j % 2][1][:], at_in[j % 2][:], f32(at[j % 2][0][:]), ALU.subtract).then_inc(sem("at_lo"), 1)

        def scale_of(link, k, name):
            for j in range(4):
                ins = nc.vector.bn_aggr(mv[:, j], st6[:, j])
            link(ins)
            TS(ln_v[:], mv[:, :, 1], EPS, None, ALU.add).then_inc(sem(name + "_var"), 1)
            ve.wait_ge(sem(name + "_root"), k)
            link(nc.vector.reciprocal(ln_r[:], ln_s[:]))
            link(TT(ln_t[:], ln_r[:], ln_r[:], ALU.mult))
            link(TT(ln_t[:], ln_t[:], ln_v[:], ALU.mult))
            link(TS(ln_t[:], ln_t[:], -0.5, 1.5, ALU.mult, ALU.add))
            link(TT(ln_r[:], ln_r[:], ln_t[:], ALU.mult))

        def tiles(i, link):
            at_rest(i, 0)
            at_rest(i, 1)
            for j in range(4):
                ve.wait_ge(sem("o_full"), i * 4 + (j + 3))
                ve.wait_ge(sem("xb_rdy"), i * 4 + (j + 1))
                TT(yb[j][:], bank[(0, 1, 4, 5)[j]], xr[j % 2][:], ALU.add).then_inc(sem("y_done"), 1)
                if j < 2:
                    at_rest(i, j + 2)
                ve.wait_ge(sem("y_done"), i * 4 + (j + 3))
                link(nc.vector.bn_stats(st6[:, j], yb[j][:]))

        def norm(i, link):
            scale_of(link, i + 1, "ln1")
            for j in range(4):
                ve.wait_ge(sem("x1_put"), i * 4 + (j + 1))
                TS(x1b[j][:], yb[j][:], mv[:, j, 0:1], ln_r[:, j:j + 1], ALU.subtract, ALU.mult).then_inc(sem("x1_rdy"), 1)

        def x1_rest(i):
            for j in range(4):
                turned(i, j, bank[2 + j % 2], "x1_hi", "x1_lo")

        link = Chain(ve, sem("ln1_chain"))
        tiles(0, link)
        norm(0, link)
        per_block = link.k
        with ve.Fori(1, 4) as i:
            link = Chain(ve, sem("ln1_chain"), i * per_block)
            tiles(i, link)
            x1_rest(i - 1)
            norm(i, link)
            assert link.k == per_block
        x1_rest(3)

        def over_e(t):
            return t[:].unsqueeze(2).to_broadcast([P, NT, E])

        def by_t(b):
            return b[:, 0:P].rearrange("p (t e) -> p t e", e=E)

        link = Chain(ve, sem("rt_chain"))
        ve.wait_ge(sem("rt_mm"), 1)
        nc.vector.tensor_copy(r3["lg"][:], by_t(bank[7])).then_inc(sem("lg_read"), 1)
        ve.wait_ge(sem("lg_read"), 1)
        link(RED(r2["mx"][:], r3["lg"][:], AX.X, ALU.max))
        TT(r3["d"][:], r3["lg"][:], over_e(r2["mx"]), ALU.subtract).then_inc(sem("rt_d"), 1)
        ve.wait_ge(sem("rt_d"), 1)
        ve.wait_ge(sem("iota"), 1)
        link(nc.vector.scalar_tensor_tensor(out=r3["c"][:], in0=r3["d"][:], scalar=0.0, in1=r3["io"][:],
                                            op0=ALU.is_equal, op1=ALU.mult))
        link(RED(r2["em"][:], r3["c"][:], AX.X, ALU.min))
        link(TT(r3["oh"][:], r3["io"][:], over_e(r2["em"]), ALU.is_equal))
        nc.vector.tensor_copy(oh_bf[:], r3["oh"][:]).then_inc(sem("oh_rdy"), 1)
        ve.wait_ge(sem("rt_ex"), 1)
        link(RED(r2["sm"][:], r3["ex"][:], AX.X, ALU.add))
        link(nc.vector.reciprocal(r2["gate"][:], r2["sm"][:]))
        ve.wait_ge(sem("rt_mm"), 2)
        link(nc.vector.memset(r3["s0"][:, 0:1, :], 0.0))
        link(nc.vector.tensor_copy(r3["s0"][:, 1:NT, :], by_t(bank[1])[:, 0:NT - 1, :]))
        a, b = "s0", "s1"
        for k in (1, 2, 4, 8):
            nc.vector.tensor_copy(r3[b][:, 0:k, :], r3[a][:, 0:k, :])
            link(TT(r3[b][:, k:NT, :], r3[a][:, k:NT, :], r3[a][:, 0:NT - k, :], ALU.add))
            a, b = b, a
        TT(r3["c"][:], by_t(bank[0]), r3[a][:], ALU.add).then_inc(sem("pos_rdy"), 1)
        ve.wait_ge(sem("pos_rdy"), 1)
        link(TT(r3["c"][:], r3["c"][:], r3["oh"][:], ALU.mult))
        link(RED(r2["ps"][:], r3["c"][:], AX.X, ALU.add))
        link(TS(r2["keep"][:], r2["ps"][:], float(CAP), None, ALU.is_le))
        link(nc.vector.scalar_tensor_tensor(out=r2["flat"][:], in0=r2["em"][:], scalar=float(CAP), in1=r2["ps"][:],
                                            op0=ALU.mult, op1=ALU.add))
        link(TS(r2["t"][:], r2["keep"][:], -2.0 * E * CAP, 3.0 * E * CAP - 1.0, ALU.mult, ALU.add))
        link(TT(r2["t"][:], r2["t"][:], r2["flat"][:], ALU.add))
        link(nc.vector.tensor_copy(sidx[:], r2["t"][:]))
        link(TS(r2["u"][:], r2["t"][:], E * CAP - 1.0, None, ALU.min))
        link(nc.vector.tensor_copy(gidx[:], r2["u"][:]))
        TT(r2["gk"][:], r2["gate"][:], r2["keep"][:], ALU.mult).then_inc(sem("routed"), 1)

        def conv(kind, c, sets):
            if kind == 13:
                ve.wait_ge(sem("conv13_hi"), sets * FC + (c + 1))
                s0, s1 = 2 * c, min(2 * c + 2, 2 * FC - 1)
                TT(w13[1][:, s0:s1], raw13[c % 2][:, 0:s1 - s0], f32(w13[0][:, s0:s1]), ALU.subtract).then_inc(sem("conv13"), 1)
            else:
                ve.wait_ge(sem("conv2_hi"), sets * FC + (c + 1))
                p0 = tail(c)
                TT(w2[1][p0:P, c], raw2[c % 2][p0:P, :], f32(w2[0][p0:P, c]), ALU.subtract).then_inc(sem("conv2"), 1)

        def steps(q, width, own, ahead):
            for c in range(FC):
                r, p0 = c % 2, tail(c)
                gated = bank[2 * r + 1] if c < FC - 1 else bank[2 * r]
                ve.wait_ge(sem("sa_rdy"), q + (c + 1))
                TT(sa[r][p0:P, 0:width], gated[p0:P, 0:width], sa[r][p0:P, 0:width], ALU.mult).then_inc(sem("h_done"), 1)
                ve.wait_ge(sem("hid_hi"), q + (c + 1))
                TT(hid[r][1][p0:P, 0:width], sa[r][p0:P, 0:width], f32(hid[r][0][p0:P, 0:width]),
                   ALU.subtract).then_inc(sem("hid_lo"), 1)
                for kind, cc in CONV_OWN.get(c, ()) if own is not None else ():
                    conv(kind, cc, own)
                for kind, cc in CONV_BEFORE.get(c, ()) if ahead is not None else ():
                    conv(kind, cc, ahead)

        def add_shared(i):
            ve.wait_ge(sem("used2"), i * FC + (FC + 2))
            for j in range(4):
                TT(row(i * 4 + j), bank[4 + j], row(i * 4 + j), ALU.add).then_inc(sem("acc_done"), 1)

        for c in range(1, FC):
            for kind, cc in CONV_BEFORE[c]:
                conv(kind, cc, 0)
        for c in range(2):
            for kind, cc in CONV_OWN[c]:
                conv(kind, cc, 0)
        steps(0, 512, None, None)
        ve.wait_ge(sem("scat"), 16 * NT)
        add_shared(0)
        with ve.Fori(1, 3) as i:
            steps(i * FC, 512, None, None)
            add_shared(i)
        steps(3 * FC, 512, None, 1)
        add_shared(3)
        with ve.Fori(0, NT // 4) as i:
            for j in range(4):
                turned(i, j, bank[j], "xd_hi", "xd_lo")
        with ve.Fori(0, E - 1) as e:
            steps(e * FC + 4 * FC, CAP, e + 1, e + 2)
        steps((E + 3) * FC, CAP, E, None)

        link = Chain(ve, sem("ln2_chain"))
        for k in range(4):
            for j in range(4):
                t = 4 * k + j
                ve.wait_ge(sem(f"gath{t % 8}"), 16 * (t // 8 + 1))
                nc.vector.scalar_tensor_tensor(out=rows[:, t], in0=got[t % 8][:], scalar=r2["gk"][:, t:t + 1],
                                               in1=rows[:, t], op0=ALU.mult, op1=ALU.add).then_inc(sem("z_done"), 1)
                ve.wait_ge(sem("z_done"), t + 1)
                link(nc.vector.bn_stats(st6[:, j], rows[:, t]))
            scale_of(link, k + 1, "ln2")
            for j in range(4):
                t = 4 * k + j
                TS(rows[:, t], rows[:, t], mv[:, j, 0:1], ln_r[:, j:j + 1], ALU.subtract, ALU.mult).then_inc(sem("out_rdy"), 1)


_INS = ["L0_attn_x"] + [f"L0_attn_{k}{m}" for m in "qkvo" for k in "WbBA"] + [
    "L0_ffn_Wg", "L0_ffn_W1", "L0_ffn_W3", "L0_ffn_W2", "L0_ffn_sw1", "L0_ffn_sw3", "L0_ffn_sw2"]
_OUTS = [((B, L, D), "float32")]


def build(nc, args):
    by_name = dict(zip(_INS + ["out"], args))
    per = {k: [by_name[f"L0_attn_{k}{m}"] for m in "qkvo"] for k in "WbBA"}
    ff = [by_name[f"L0_ffn_{n}"] for n in ("Wg", "W1", "W3", "W2", "sw1", "sw3", "sw2")]
    with ExitStack() as ctx:
        emit(nc, ctx, by_name["L0_attn_x"], per["W"], per["b"][:3], per["b"][3], per["B"], per["A"], *ff, by_name["out"])


def kernel(**inputs):
    import numpy as _np
    import concourse.bacc as _bacc
    from concourse import mybir as _mybir
    from concourse.bass_utils import run_bass_kernel_spmd as _run

    nc = _bacc.Bacc("TRN2", target_bir_lowering=False, num_devices=1)
    arrays, args = {}, []
    for name in _INS:
        a = _np.ascontiguousarray(inputs[name])
        arrays[f"in_{name}_dram"] = a
        args.append(nc.dram_tensor(f"in_{name}_dram", a.shape, _mybir.dt.from_np(a.dtype), kind="ExternalInput").ap())
    for i, (shape, dtype) in enumerate(_OUTS):
        dt = _mybir.dt.from_np(_np.dtype(dtype))
        args.append(nc.dram_tensor(f"out_{i}_dram", shape, dt, kind="ExternalOutput").ap())
    build(nc, args)
    r = _run(nc, [arrays], core_ids=[0])
    return r.results[0]["out_0_dram"]
```

```python
from contextlib import ExitStack

import concourse.bass as bass
from concourse import mybir

F32 = mybir.dt.float32
FR = mybir.dt.float32r
BF16 = mybir.dt.bfloat16
U32 = mybir.dt.uint32
ACT = mybir.ActivationFunctionType
ALU = mybir.AluOpType
AX = mybir.AxisListType

P = 128
B, L, D = 2, 1024, 512
T = B * L
NT = T // P
DC = D // P
HEADS = 16
HD = D // HEADS
HG = P // HD
NG = HEADS // HG
RANK = 16
LORA = 8.0 / RANK
SCALE = float(HD) ** -0.5
HALF = 512
KC = L // P
E = 8
CAP = T // E
F = 704
FC = 6
FTAIL = F - 5 * P
EPS = 1e-5
W_ORDER = (2, 0, 1, 3)
SPLIT = ((0, 0), (0, 1), (1, 0))


class Arena:

    def __init__(self, nc, start, end):
        self.nc, self.at, self.end = nc, start, end

    def __call__(self, name, shape, dt):
        size = mybir.dt.size(dt)
        for n in shape[1:]:
            size *= n
        t = self.nc.alloc_sbuf_tensor_at(name, shape, dt, offset=self.at)
        self.at += (size + 31) // 32 * 32
        assert self.at <= self.end, (name, self.at, self.end)
        return t


class Chain:

    def __init__(self, eng, sem, base=0):
        self.eng, self.sem, self.base, self.k = eng, sem, base, 0

    def __call__(self, ins):
        ins.then_inc(self.sem, 1)
        self.k += 1
        self.eng.wait_ge(self.sem, self.base + self.k)


SUMS_AT = 1
SUMS = 6
ADDS = 2 * (SUMS - 1)
RING = 4
WORK, SCORE = 3, 2


def smax_uses(ahead, start=0, stop=HG * HALF // P * 2):
    return [("smax", ahead, hh, qt, n) for hh in range(HG) for qt in range(HALF // P) for n in range(2)][start:stop]


EARLY = (12, 12)
LAST_SMAX = smax_uses(1)[-1]
PRO_USES = smax_uses(1) + [("mrow",)] + smax_uses(2, 0, EARLY[0])
PRO_PLACE = [10, 18, 26]
PRO_PROJ = [(1, 0), (1, 1), (0, 0), (0, 1), (1, 0), (1, 1), (0, 0)]


def half_uses(slot, last):
    odd = slot % 2
    plan = [[] for _ in range(KC)]
    if not (last and slot == 3):
        uses = smax_uses(1, EARLY[odd])
        for kc, n in enumerate((3, 4, 5, 4, 4) if odd else (6, 5, 5, 4)):
            plan[kc] += [uses.pop(0) for _ in range(n)]
        plan[5 if odd else 4].append(("mrow",))
    if not (last and slot >= 2):
        uses = smax_uses(2, 0, EARLY[1 - odd])
        for kc, n in zip(range(KC - 4, KC), (1, 3, 4, 4) if odd else (3, 3, 3, 3)):
            plan[kc] += [uses.pop(0) for _ in range(n)]
    return plan


def half_proj(slot):
    return {2: (1, 0), 4: (1, 1), 6: (0, 0)} if slot % 2 else {0: (0, 1)}


class Half:

    def __init__(self, g, h, last=False):
        self.g, self.h, self.slot, self.last = g, h, h % 4, last
        self.b, self.hf = self.slot // 2, h % 2
        self.first = isinstance(g, int) and g == 0 and h == 0
        self.plan, self.proj = half_uses(self.slot, last), {} if last else half_proj(self.slot)
        self.uses = [u for kc in self.plan for u in kc]
        self.start = len(PRO_USES) + sum(n_uses(i, last) for i in range(h))
        before = len(PRO_USES) if self.first else n_uses(h + 3, last and h > 0)
        self.before = before

    def halves(self, per, plus=0):
        return self.g * (4 * per) + (self.h * per + plus)

    def units(self, per, plus=0):
        return self.g * (2 * per) + (self.h // 2 * per + plus)

    def number(self, j):
        return self.g * GROUP_USES + (self.start + j)

    def bank_before(self, j):
        if j >= WORK:
            return j - WORK
        return max(k for k in range(self.before) if k % WORK == j) - self.before

    def projected(self, plus=0):
        return self.units(4, len(PRO_PROJ) + self.h % 2 + plus)

    def piece(self, kc, hh):
        places = ((kc // 2 * 2, 2), (kc // 2 * 2, 3), (kc // 2 * 2 + 1, 1), (kc // 2 * 2 + 1, 2))
        if (kc, hh) in places and kc // 2 * 2 in self.proj:
            return self.proj[kc // 2 * 2], places.index((kc, hh))
        return None, 0

    def after(self, kc, hh):
        n = len(self.plan[kc])
        return self.plan[kc][(n * hh + HG - 1) // HG:(n * (hh + 1) + HG - 1) // HG]

    def find(self, use):
        return self.uses.index(use)


def n_uses(h, last):
    return sum(len(kc) for kc in half_uses(h % 4, last))


GROUP_USES = sum(n_uses(i, False) for i in range(4))


def all_halves(eng, half, end):
    half(Half(0, 0))
    with eng.Fori(0, NG - 1) as g:
        for h in range(1, 5):
            half(Half(g, h))
    for h in range(1, 4):
        half(Half(NG - 1, h, True))
    end(Half(NG - 1, 4, True))


CONV_BEFORE = {1: ((13, 0),), 2: ((13, 1), (2, 0)), 3: ((13, 2), (2, 1)), 4: ((13, 3), (2, 2)), 5: ((13, 4), (2, 3))}
CONV_OWN = {0: ((13, 5), (2, 4)), 1: ((2, 5),)}

FIRST_PROJ = {1: 0, 2: 1, 3: 2}
FIRST = {0: ((13, 3), (2, 0), (2, 1)), 1: ((13, 4), (2, 2)), 2: ((13, 5), (2, 3)), 3: ((2, 4),), 4: ((2, 5),)}


def tail(c):
    return 0 if c < FC - 1 else P - FTAIL


def emit(nc, ctx, x, W, bias, bo, Bm, Am, Wg, W1, W3, W2, sw1, sw3, sw2, out):
    sems = {}

    def sem(name):
        if name not in sems:
            sems[name] = ctx.enter_context(nc.semaphore(name))
        return sems[name]

    bank = [ctx.enter_context(nc.psum_tensor(f"bank{i}", [P, 512], F32))[:] for i in range(8)]
    work, score_bank = bank[0:WORK], bank[WORK:WORK + SCORE]
    pj, ov, dn = bank[5:8]

    wt_d = nc.dram_tensor("wt_d", [4, 2, P, DC, D], F32).ap()
    v_d = nc.dram_tensor("v_d", [T, D], F32).ap()
    attn_d = nc.dram_tensor("attn_d", [D, T], F32).ap()
    xd_d = nc.dram_tensor("xd_d", [E * CAP, D], F32).ap()
    gate_d = nc.dram_tensor("gate_d", [E * CAP, 1], F32).ap()
    oe_d = nc.dram_tensor("oe_d", [E * CAP, D], F32).ap()
    x_rows = x.rearrange("b l d -> (b l) d")
    out_rows = out.rearrange("b l d -> (b l) d")
    v_rows = v_d.rearrange("(t p) d -> p t d", p=P)
    attn_cols = attn_d.rearrange("(c p) t -> p c t", p=P)

    keep = Arena(nc, (nc.sbuf_base + 31) // 32 * 32, nc.sbuf_usable_end)
    xT = [keep(f"xT{s}", [P, DC, T], FR) for s in ("hi", "lo")]
    ident = keep("ident", [P, P], F32)
    ones32 = keep("ones32", [P, HD], F32)
    zeros = keep("zeros", [P, D // 8], F32)
    region = keep.at
    V_BYTES = KC * P * 4

    att = Arena(nc, region, nc.sbuf_usable_end)
    Qs = [att("Qs0", [P, HG, L], FR)]
    Ks = [att("Ks0", [P, HG, L], FR)]
    plane = [[att(f"plane_{m}{s}", [P, L], FR) for s in ("hi", "lo")] for m in "qk"]
    Wsl = att("Wsl", [P, 2, 2, DC, P], FR)
    V = [att(f"V{i}", [P, KC, P], F32) for i in range(2)]
    small_at = att.at
    bcol = att("bcol", [P, 2], F32)
    mx = [att(f"mx{i}", [P, 16, 2], F32) for i in range(2)]
    nm = att("nm", [P, 16], F32)
    mrow = att("mrow", [16, P], FR)
    rden = att("rden", [P, HALF], F32)
    attn_sb = [att(f"attn_sb{i}", [P, HALF], F32) for i in range(2)]
    overlay = att.at
    Qs.append(att("Qs1", [P, HG, L], FR))
    Ks.append(att("Ks1", [P, HG, L], FR))
    prob = [att(f"prob{i}", [P, HG, HALF], F32) for i in range(RING)]
    sum_at = att.at - RING * HG * HALF * 4
    psum = att("psum", [P, HG, HALF], F32)

    stp = Arena(nc, overlay, att.at)
    w_raw = [stp(f"w_raw{i}", [P, DC, D], F32) for i in range(2)]
    xin = [stp(f"xin{i}", [P, D], F32) for i in range(4)]
    w_stage = [[stp(f"w_stage{i}{s}", [P, D], FR) for s in ("hi", "lo")] for i in range(2)]
    wv = [stp(f"wv{s}", [P, DC, D], FR) for s in ("hi", "lo")]
    bv_bc = stp("bv_bc", [P, D], F32)
    v_sb = [stp(f"v_sb{i}", [P, D], F32) for i in range(2)]
    lora_a = stp("lora_a", [P, 4, DC, RANK], F32)
    lora_b = stp("lora_b", [P, D], F32)
    lora_at = stp("lora_at", [P, D], F32)

    early = Arena(nc, region, small_at - V_BYTES)
    wo = [early(f"wo{s}", [P, DC, D], FR) for s in ("hi", "lo")]
    at_in = [early(f"at_in{i}", [P, DC, P], F32) for i in range(4)]
    xr = [early(f"xr{i}", [P, D], F32) for i in range(4)]
    at = [[early(f"at{i}{s}", [P, DC, P], FR) for s in ("hi", "lo")] for i in range(2)]
    bo_bc = early("bo_bc", [P, D], F32)
    early_end = early.at
    w13 = [[early(f"w13_{c}{s}", [P, 2, DC, P], FR) for s in ("hi", "lo")] for c in range(2)]
    wg_raw = early("wg_raw", [P, DC, E], F32)
    st6 = early("st6", [P, 4, 6], F32)
    mv = early("mv", [P, 4, 2], F32)
    ln_v, ln_s, ln_r, ln_t = (early(f"ln_{n}", [P, 4], F32) for n in "vsrt")
    mid = Arena(nc, small_at - V_BYTES, overlay)
    raw2 = [mid(f"raw2_{i}", [P, D], F32) for i in range(2)]
    r3 = {n: mid(f"r3_{n}", [P, NT, E], F32) for n in ("lg", "d", "ex", "c", "oh", "s0", "s1", "io")}
    r2 = {n: mid(f"r2_{n}", [P, NT], F32) for n in ("mx", "sm", "gate", "em", "ps", "keep", "flat", "t", "u")}
    ln_rb = [[mid(f"ln_{n}{i}", [P, 4], F32) for n in ("scale", "shift")] for i in range(2)]
    tri = mid("tri", [P, P], BF16)
    allone = mid("allone", [P, P], BF16)
    oh_bf = mid("oh_bf", [P, NT, E], BF16)
    sidx = mid("sidx", [P, NT], U32)
    lidx = mid("lidx", [P, NT], U32)
    gate_sb = mid("gate_sb", [P, E * CAP // P], F32)
    wide = Arena(nc, overlay, sum_at)
    rows = wide("rows", [P, NT, D], F32)
    late = Arena(nc, sum_at, nc.sbuf_usable_end)
    raw13 = [late(f"raw13_{i}", [P, 2, DC, P], F32) for i in range(2)]
    w13 += [[late(f"w13_{c}{s}", [P, 2, DC, P], FR) for s in ("hi", "lo")] for c in (2, 3)]
    xdi = [late(f"xdi{i}", [P, D], F32) for i in range(2)]
    late_at = late.at
    w13 += [[late(f"w13_{c}{s}", [P, 2 if c < FC - 1 else 1, DC, P], FR) for s in ("hi", "lo")] for c in (4, 5)]
    gate = Arena(nc, late_at, late.at)
    wgp = [gate(f"wgp{s}", [P, DC, P], FR) for s in ("hi", "lo")]
    lgT = gate("lgT", [E, T], F32)
    ffn = Arena(nc, region, early_end)
    w2 = [ffn(f"w2{s}", [P, FC, D], FR) for s in ("hi", "lo")]
    sa = [ffn(f"sa{i}", [P, 512], F32) for i in range(2)]
    hid = [[ffn(f"hid{i}{s}", [P, 512], FR) for s in ("hi", "lo")] for i in range(2)]
    oe_sb = [ffn(f"oe_sb{i}", [P, D], F32) for i in range(2)]
    xdi += oe_sb

    block = ctx.enter_context(nc.Block())

    def f32(ap):
        return ap.bitcast(F32)

    def w_bank(k):
        return bank[(4 if k < 3 * DC else WORK) + k % 2]

    def x1_bank(t):
        return bank[(2, 3)[t % 2]] if t < NT - 4 else bank[(4, 5)[t % 2]]

    def cols(i, j):
        return bass.ds(i * 512 + j * P, P)

    def up_cols(wd, c):
        return wd.rearrange("(c p) h -> p c h", p=P)[:, :, c * P:min((c + 1) * P, F)]

    @block.sync
    def _(sp):
        def value(e):
            return e if isinstance(e, int) else sp.snap(e)

        for m in range(4):
            sp.dma_start(lora_b[32 * m:32 * m + RANK, :], Bm[m]).then_inc(sem("lora_ld"), 16)
            sp.dma_start(lora_a[:, m], Am[m].rearrange("(c p) r -> p c r", p=P)).then_inc(sem("lora_ld"), 16)

        def load_w(n):
            if n >= 2:
                sp.wait_ge(sem("w_mm"), DC * (n - 1))
            sp.dma_start(w_raw[n % 2][:], W[W_ORDER[n]].rearrange("(c p) d -> p c d", p=P)).then_inc(sem(f"w_ld{n % 2}"), 16)

        def load_x(i):
            for j in range(4):
                if i:
                    sp.wait_ge(sem("x_t"), 4 * i + j - 3)
                sp.dma_start(xin[j][:], x_rows[(4 * i + j) * P:(4 * i + j + 1) * P, :]).then_inc(sem(f"x_ld{j}"), 16)

        load_w(0)
        load_x(0)
        load_w(1)
        sp.dma_start(bv_bc[:], bias[2].rearrange("(o d) -> o d", o=1).to_broadcast([P, D])).then_inc(sem("bv_ld"), 16)
        load_x(1)
        load_w(2)
        load_x(2)
        load_x(3)
        load_w(3)

        def load_slot(c):
            for m in (1, 0):
                for s in range(2):
                    sp.dma_start(f32(Wsl[:, m, s]), wt_d[m, s][:, :, bass.ds(c, P)]).then_inc(sem("qk"[m] + "_ld"), 16)
                sp.dma_start(bcol[:, m:m + 1],
                             bias[m][bass.ds(c, P)].rearrange("(p o) -> p o", o=1)).then_inc(sem("qk"[m] + "_ld"), 16)

        def load_v(b, c):
            sp.dma_start(V[b][:], v_rows[:, b * KC:(b + 1) * KC, bass.ds(c, P)]).then_inc(sem(f"v_ld{b}"), 16)

        def stack(b, m, pair):
            dst, parts = ((Qs[b], (0, 1, 0)), (Ks[b], (0, 0, 1)))[m]
            for hh in (2 * pair, 2 * pair + 1):
                for r, s in enumerate(parts):
                    sp.dma_start(f32(dst[32 * r:32 * r + 32, hh, :]),
                                 f32(plane[m][s][32 * hh:32 * hh + 32, :])).then_inc(sem(f"{'qk'[m]}_stack_{pair}"), 16)

        def put_mrow(b, hf, need):
            sp.wait_ge(sem("wk_done"), need)
            for hh in range(HG):
                sp.dma_start(f32(Qs[b][96:97, hh, hf * HALF:(hf + 1) * HALF]),
                             f32(mrow[4 * hh:4 * hh + 4, :])).then_inc(sem("mrow_ld"), 16)

        def next_mrow(v):
            if ("mrow",) in v.uses:
                put_mrow((v.slot + 1) % 4 // 2, 1 - v.hf, value(v.number(v.find(("mrow",)) + 1)))

        def stack_unit(b, k_need, q_need, v=None):
            sp.wait_ge(sem("pj_done"), k_need)
            stack(b, 1, 0)
            sp.wait_ge(sem("pj_done"), q_need)
            stack(b, 0, 0)
            if v is not None:
                next_mrow(v)
            stack(b, 1, 1)
            stack(b, 0, 1)

        for i in range(2):
            for s in range(2):
                sp.wait_ge(sem(f"w_st{i}_{s}"), 16 * 4)
        load_slot(0)
        stack_unit(0, 3, 4)
        for i in range(2):
            sp.wait_ge(sem(f"v_st{i}"), 16 * NT // 2)
        load_v(0, 0)
        put_mrow(0, 0, PRO_USES.index(("mrow",)) + 1)
        for i in range(2):
            for s in range(2):
                sp.wait_ge(sem(f"w_st{i}_{s}"), 16 * 6)

        def half(v):
            if v.proj and v.slot % 2 == 0:
                stack_unit(1 - v.b, value(v.projected()), value(v.projected(1)), v)
                c, used = value(v.g * P + (v.h // 4 * P + v.b * P)), value(v.halves(KC))
                if not v.first:
                    sp.wait_ge(sem("pv_done"), used)
                load_v(1 - v.b, c)
            elif v.proj and v.slot == 1:
                c, need = value((v.g + 1) * P), value(v.projected())
                sp.wait_ge(sem("pj_done"), need)
                load_slot(c)
            if v.last and v.slot == 2:
                load_wo(v)
            if not v.proj or v.slot % 2:
                next_mrow(v)
            if v.last and v.slot == 1:
                sp.wait_ge(sem("zeros"), 1)
                sp.dma_start(xd_d.rearrange("(p n) (a b) -> p (n a) b", p=P, a=8),
                             zeros[:].unsqueeze(1).to_broadcast([P, E * CAP // P * 8, D // 8])).then_inc(sem("xd_zero"), 16)
                sp.dma_start(gate_d.rearrange("(p n) o -> p (n o)", p=P), zeros[:, 0:E * CAP // P]).then_inc(sem("gate_zero"), 16)
            if v.last and v.slot == 3:
                for hf in range(2):
                    sp.wait_ge(sem(f"at_st{hf}"), 16 * 2 * NG)
                for t in range(4):
                    load_tile(t)
            if not v.first:
                store(v)

        def load_wo(v):
            sp.wait_ge(sem("st_full"), v.halves(HG * KC))
            for s in range(2):
                sp.dma_start(f32(wo[s][:]), wt_d[3, s]).then_inc(sem("wo_ld"), 16)
            sp.dma_start(bo_bc[:], bo.rearrange("(o d) -> o d", o=1).to_broadcast([P, D])).then_inc(sem("bo_ld"), 16)
            sp.dma_start(wg_raw[:], Wg.rearrange("(c p) e -> p c e", p=P)).then_inc(sem("wg_ld"), 16)

        def load_tile(t):
            if t >= 4:
                sp.wait_ge(sem("at_lo"), t - 3)
            sp.dma_start(at_in[t % 4][:], attn_cols[:, :, t * P:(t + 1) * P]).then_inc(sem(f"at_ld{t % 4}"), 16)
            if t >= 4:
                sp.wait_ge(sem("y_done"), t - 3)
            sp.dma_start(xr[t % 4][:], x_rows[t * P:(t + 1) * P, :]).then_inc(sem(f"xr_ld{t % 4}"), 16)

        def store(v):
            b, hf = (v.slot + 3) % 4 // 2, 1 - v.hf
            r, need = value(v.g * P), value(v.halves(1, 1))
            sp.wait_ge(sem("at_done"), need)
            sp.dma_start(attn_d[bass.ds(r, P), b * L + hf * HALF:b * L + (hf + 1) * HALF],
                         attn_sb[hf][:]).then_inc(sem(f"at_st{hf}"), 16)

        all_halves(sp, half, store)

        def load13(wa, wb, c):
            if c < FC - 1:
                da, db = raw13[c % 2][:, 0], raw13[c % 2][:, 1]
            else:
                da, db = raw13[c % 2][:, 0, :, 0:FTAIL], raw13[c % 2][:, 0, :, FTAIL:P]
            sp.dma_start(da, up_cols(wa, c)).then_inc(sem(f"raw13_ld{c % 2}"), 16)
            sp.dma_start(db, up_cols(wb, c)).then_inc(sem(f"raw13_ld{c % 2}"), 16)

        def load2(wc, c):
            sp.dma_start(raw2[c % 2][tail(c):P, :], wc[c * P:min((c + 1) * P, F), :]).then_inc(sem(f"raw2_ld{c % 2}"), 16)

        def load_set(wa, wb, wc, done, chunks):
            for kind, c in chunks:
                name = "conv13" if kind == 13 else "conv2"
                if not (isinstance(done, int) and done + c < 2):
                    need = value(done + (c - 1))
                    sp.wait_ge(sem(name), need)
                if kind == 13:
                    load13(wa, wb, c)
                else:
                    load2(wc, c)

        def load_shared(*chunks):
            load_set(sw1, sw3, sw2, 0, chunks)

        sp.wait_ge(sem("den_done"), 4 * NG)
        load_shared((13, 0), (13, 1), (2, 0), (2, 1))
        sp.wait_ge(sem("at_st0"), 16 * (2 * NG + 1))
        sp.wait_ge(sem("at_st1"), 16 * (2 * NG + 1))
        for i in range(1, 4):
            for j in range(4):
                load_tile(4 * i + j)
            if i >= 2:
                load_shared((13, i))
        load_shared((13, 4), (2, 2), (13, 5), (2, 3), (2, 4), (2, 5))
        in_set = [kc for c in range(1, FC) for kc in CONV_BEFORE[c]]
        own = [kc for c in (0, 1) for kc in CONV_OWN[c]]
        sp.wait_ge(sem("scat"), 16 * NT)
        for j in range(4):
            sp.dma_start(xdi[j][:], xd_d[j * P:(j + 1) * P, :]).then_inc(sem(f"xd_ld{j}"), 16)
        with sp.Fori(1, 4) as i:
            for j in range(4):
                r, need = value(i * 4 * P + j * P), value(i * 4 + (j - 3))
                sp.wait_ge(sem("xd_t"), need)
                sp.dma_start(xdi[j][:], xd_d[bass.ds(r, P), :]).then_inc(sem(f"xd_ld{j}"), 16)
        sp.wait_ge(sem("gate_put"), 16 * NT)
        sp.dma_start(gate_sb[:], gate_d.rearrange("(n p) o -> p (n o)", p=P),
                     allow_slow_non_contiguous=True).then_inc(sem("gate_ld"), 16)
        load_set(W1[0], W3[0], W2[0], FC, in_set)
        load_set(W1[0], W3[0], W2[0], FC, own)
        with sp.Fori(1, E) as e:
            ee = value(e)
            w1e, w3e, w2e = (w[bass.ds(ee, 1)].rearrange("o a b -> (o a) b") for w in (W1, W3, W2))
            load_set(w1e, w3e, w2e, e * FC + FC, in_set + own)

        for t in range(NT):
            sp.wait_ge(sem("out_rdy"), t + 1)
            sp.dma_start(out_rows[t * P:(t + 1) * P, :], rows[:, t]).then_inc(sem("out_st"), 16)
        sp.wait_ge(sem("out_st"), 16 * NT)

    @block.gpsimd
    def _(po):
        po.memset(ident[:], 0.0).then_inc(sem("blank"), 1)
        po.memset(ones32[:], 1.0).then_inc(sem("const"), 1)
        po.memset(zeros[:], 0.0).then_inc(sem("zeros"), 1)
        po.wait_ge(sem("blank"), 1)
        po.affine_select(out=ident[:], in_=ident[:], compare_op=ALU.not_equal, fill=1.0, base=0,
                         pattern=[[-1, P]], channel_multiplier=1).then_inc(sem("const"), 1)

        def store_w(n):
            m = W_ORDER[n]
            for dc in range(DC):
                k = (n - 1) * DC + dc
                po.wait_ge(sem("w_lo"), k + DC + 1)
                for s in range(2):
                    po.dma_start(wt_d[m, s][:, dc, :], f32(w_stage[k % 2][s][:])).then_inc(sem(f"w_st{k % 2}_{s}"), 16)

        def store_v(i):
            for t in range(4 * i, 4 * i + 4):
                po.wait_ge(sem("v_done"), t + 1)
                po.dma_start(v_d[t * P:(t + 1) * P, :], v_sb[t % 2][:]).then_inc(sem(f"v_st{t % 2}"), 16)

        store_w(1)
        store_v(0)
        store_w(2)
        for i in range(1, 4):
            store_v(i)
        store_w(3)
        for i in range(2):
            for s in range(2):
                po.wait_ge(sem(f"w_st{i}_{s}"), 16 * 6)
            po.wait_ge(sem(f"v_st{i}"), 16 * NT // 2)
        po.wait_ge(sem("x_lo"), NT)
        for i in range(2):
            po.memset(f32(Ks[i][96:97, :, :]), 1.0).then_inc(sem("ks_ones"), 1)

        def sums(v, first):
            if not first:
                po.wait_ge(sem("den_done"), v)
            for kc in range(1, SUMS):
                for p in range(2):
                    pr = slice(2 * p, 2 * p + 2)
                    po.wait_ge(sem("exp_done"), v * (HG * KC) + (HG * kc + 2 * p + 2))
                    if kc > 1:
                        po.wait_ge(sem("sum_done"), v * ADDS + (2 * (kc - 2) + p + 1))
                    po.tensor_tensor(psum[:, pr], (prob[0] if kc == 1 else psum)[:, pr], prob[kc % RING][:, pr],
                                     ALU.add).then_inc(sem("sum_done"), 1)

        sums(0, True)
        with po.Fori(1, 4 * NG) as v:
            sums(v, False)

        po.wait_ge(sem("den_done"), 4 * NG)
        for s in range(2):
            po.memset(f32(wgp[s][:]), 0.0).then_inc(sem("wgp_zero"), 1)
        po.wait_ge(sem("bo_ld"), 16)

        def residual(i):
            for j in range(4):
                po.wait_ge(sem(f"xr_ld{j}"), i * 16 + 16)
                po.tensor_tensor(xr[j][:], xr[j][:], bo_bc[:], ALU.add).then_inc(sem("xb_rdy"), 1)

        residual(0)
        po.wait_ge(sem("at_st0"), 16 * (2 * NG + 1))
        po.wait_ge(sem("at_st1"), 16 * (2 * NG + 1))
        po.memset(tri[:], 1.0).then_inc(sem("blank"), 1)
        po.memset(allone[:], 1.0).then_inc(sem("rt_const"), 1)
        po.iota(r3["io"][:], pattern=[[0, NT], [1, E]], base=-E, channel_multiplier=0,
                allow_small_or_imprecise_dtypes=True).then_inc(sem("iota"), 1)
        po.wait_ge(sem("blank"), 2)
        po.affine_select(out=tri[:], in_=tri[:], compare_op=ALU.is_ge, fill=0.0, base=0,
                         pattern=[[1, P]], channel_multiplier=-1).then_inc(sem("rt_const"), 1)
        with po.Fori(1, 4) as i:
            residual(i)

        po.wait_ge(sem("xd_zero"), 16)
        po.wait_ge(sem("routed"), 1)
        for t in range(NT):
            po.indirect_dma_start(out=xd_d, out_offset=bass.IndirectOffsetOnAxis(ap=sidx[:, t:t + 1], axis=0),
                                  in_=rows[:, t, :], in_offset=None, bounds_check=E * CAP - 1,
                                  oob_is_err=False).then_inc(sem("scat"), 16)

        po.wait_ge(sem("gate_zero"), 16)
        for t in range(NT):
            po.indirect_dma_start(out=gate_d, out_offset=bass.IndirectOffsetOnAxis(ap=sidx[:, t:t + 1], axis=0),
                                  in_=r2["gate"][:, t:t + 1], in_offset=None, bounds_check=E * CAP - 1,
                                  oob_is_err=False).then_inc(sem("gate_put"), 16)

        def store_oe(e):
            for i in range(2):
                po.wait_ge(sem("oe_rdy"), e * 2 + (i + 3))
                po.dma_start(oe_d[bass.ds(e * CAP + i * P, P), :], oe_sb[i][:]).then_inc(sem(f"oe_st{i}"), 16)

        with po.Fori(0, E - 1) as e:
            store_oe(e)

        def add_rows(t, idx, experts, done):
            po.indirect_dma_start(out=rows[:, t, :], out_offset=None, in_=oe_d[0:experts * CAP, :],
                                  in_offset=bass.IndirectOffsetOnAxis(ap=idx[:, t:t + 1], axis=0),
                                  bounds_check=experts * CAP - 1, oob_is_err=False,
                                  compute_op=ALU.add).then_inc(sem(done), 16)

        po.wait_ge(sem("acc_done"), NT)
        for i in range(2):
            po.wait_ge(sem(f"oe_st{i}"), 16 * (E - 1))
        for t in range(NT):
            add_rows(t, sidx, E - 1, "most_added")
        store_oe(E - 1)
        po.wait_ge(sem("most_added"), 16 * NT)
        for i in range(2):
            po.wait_ge(sem(f"oe_st{i}"), 16 * E)
        for t in range(NT):
            add_rows(t, lidx, E, f"all_added{t}")

    @block.tensor
    def _(pe):
        def split3(dst, lhs, rhs):
            for dc in range(DC):
                for k, (a, b) in enumerate(SPLIT):
                    mm = nc.tensor.matmul(dst, lhs(a, dc), rhs(b, dc), start=dc == 0 and k == 0,
                                          stop=dc == DC - 1 and k == 2)
            return mm

        def turn(dst, src):
            for c in range(DC):
                mm = nc.tensor.transpose(dst[:, c * P:(c + 1) * P], src[:, c * P:(c + 1) * P], ident[:])
            return mm

        pe.sem_inc(sem("used2"), 2)

        pe.wait_ge(sem("const"), 2)
        pe.wait_ge(sem("lora_ld"), 16 * 8)
        for n, m in enumerate(W_ORDER):
            for oc in range(DC):
                mm = nc.tensor.transpose(bank[n][0:RANK, oc * P:(oc + 1) * P], lora_a[:, m, oc, :], ident[:])
            mm.then_inc(sem("a_t"), 1)

        def weights(n, start=0, stop=DC):
            m = W_ORDER[n]
            pe.wait_ge(sem("a_ev"), n + 1)
            pe.wait_ge(sem(f"w_ld{n % 2}"), 16 * (n // 2 + 1))
            for dc in range(start, stop):
                k = n * DC + dc
                dst = w_bank(k)
                if k >= 2:
                    pe.wait_ge(sem("w_lo"), k - 1)
                nc.tensor.matmul(dst, lora_b[32 * m:32 * m + RANK, dc * P:(dc + 1) * P],
                                 lora_at[32 * m:32 * m + RANK, :], start=True, stop=False)
                for oc in range(DC):
                    mm = nc.tensor.matmul(dst[:, oc * P:(oc + 1) * P], w_raw[n % 2][:, oc, dc * P:(dc + 1) * P],
                                          ident[:], start=False, stop=oc == DC - 1)
                mm.then_inc(sem("w_mm"), 1)

        def turn_x(i):
            for j in range(4):
                pe.wait_ge(sem(f"x_ld{j}"), i * 16 + 16)
                if i:
                    pe.wait_ge(sem("x_lo"), i * 4 + (j - 3))
                turn(bank[j], xin[j]).then_inc(sem("x_t"), 1)

        def make_v(i):
            pe.wait_ge(sem("w_lo"), DC)
            for t in range(4 * i, 4 * i + 4):
                pe.wait_ge(sem("x_lo"), t + 1)
                if t >= 2:
                    pe.wait_ge(sem("v_done"), t - 1)
                split3(bank[6 + t % 2], lambda a, dc: xT[a][:, dc, t * P:(t + 1) * P],
                       lambda p, dc: wv[p][:, dc, :]).then_inc(sem("v_mm"), 1)

        weights(0)
        pe.wait_ge(sem("a_ev"), 4)
        turn_x(0)
        weights(1)
        make_v(0)
        turn_x(1)
        weights(2)
        make_v(1)
        for i in (2, 3):
            turn_x(i)
            make_v(i)

        def project_unit(m, ph, b, quarters, n, ld_need):
            if 0 in quarters:
                pe.wait_ge(sem("qk"[m] + "_ld"), ld_need)
                if n is not None:
                    pe.wait_ge(sem("pj_done"), n)
            cols = slice(b * L + ph * HALF, b * L + (ph + 1) * HALF)
            for dc in quarters:
                for k, (a, p) in enumerate(SPLIT):
                    mm = nc.tensor.matmul(pj, Wsl[:, m, a, dc, :], xT[p][:, dc, cols], start=dc == 0 and k == 0,
                                          stop=dc == DC - 1 and k == 2)
            if DC - 1 in quarters:
                mm.then_inc(sem("pj_full"), 1)

        def use(j, kind, slot, nm_need):
            dst = work[j % WORK]
            if kind[0] == "smax":
                _, ahead, hh, qt, part = kind
                b, hf = (slot + ahead) % 4 // 2, (slot + ahead) % 2
                q0 = hf * HALF + qt * P
                mm = nc.tensor.matmul(dst, Qs[b][0:96, hh, q0:q0 + P], Ks[b][0:96, hh, part * 512:part * 512 + 512],
                                      start=True, stop=True)
            else:
                pe.wait_ge(sem("nm_rdy"), nm_need)
                mm = nc.tensor.transpose(dst[0:16, 0:P], nm[:], ident[:])
            mm.then_inc(sem("wk_full"), 1)

        pe.wait_ge(sem("x_lo"), NT)
        for n, (m, ph) in enumerate(PRO_PROJ[:4]):
            project_unit(m, ph, 0, range(DC), n or None, 48)
            weights(3, n, n + 1)
        for n, kind in enumerate(PRO_USES):
            if kind[0] == "smax" and kind[1] == 1 and kind[2] in (0, 2) and kind[3:] == (0, 0):
                pe.wait_ge(sem(f"k_stack_{kind[2] // 2}"), 96)
                pe.wait_ge(sem(f"q_stack_{kind[2] // 2}"), 96)
            if n >= WORK:
                pe.wait_ge(sem("wk_done"), n - WORK + 1)
            use(n, kind, 3, 1)
            if n in PRO_PLACE:
                i = 4 + PRO_PLACE.index(n)
                project_unit(*PRO_PROJ[i], 1, range(DC), i, 48)
        pe.wait_ge(sem("ks_ones"), 2)
        pe.wait_ge(sem("w_lo"), 4 * DC)
        pe.wait_ge(sem("v_done"), NT)

        def score(v, i):
            kc, hh = i // HG, i % HG
            if i >= SCORE:
                pe.wait_ge(sem("exp_done"), v.halves(HG * KC, i - SCORE + 1))
            elif not v.first:
                held = max(k for k in range(HG * KC) if k % SCORE == i)
                pe.wait_ge(sem("exp_done"), v.halves(HG * KC, held + 1 - HG * KC))
            nc.tensor.matmul(score_bank[i % SCORE], Ks[v.b][0:97, hh, kc * P:(kc + 1) * P],
                             Qs[v.b][0:97, hh, v.hf * HALF:(v.hf + 1) * HALF], start=True,
                             stop=True).then_inc(sem("st_full"), 1)

        def values(v, kc):
            pe.wait_ge(sem("exp_done"), v.halves(HG * KC, HG * (kc + 1)))
            b = v.b if kc >= 0 else (v.slot + 3) % 4 // 2
            if kc == 0:
                pe.wait_ge(sem(f"v_ld{b}"), v.g * 16 + (v.h // 4 * 16 + 16))
                if not v.first:
                    pe.wait_ge(sem("ov_read"), v.halves(1))
            for hh in range(HG):
                mm = nc.tensor.matmul(ov[hh * HD:(hh + 1) * HD, :], V[b][:, kc % KC, hh * HD:(hh + 1) * HD],
                                      prob[kc % RING][:, hh, :], start=kc == 0, stop=kc == -1 or kc == KC - 1)
            mm.then_inc(sem("pv_done"), 1)

        def sums(v, parts, first, last):
            for k, part in enumerate(parts):
                for hh in range(HG):
                    mm = nc.tensor.matmul(dn[hh * HD:(hh + 1) * HD, :], ones32[:], part[:, hh, :],
                                          start=first and k == 0, stop=last and k == len(parts) - 1)
            return mm

        def late_sums(v):
            pe.wait_ge(sem("at_done"), v.halves(1))
            sums(v, [prob[kc % RING] for kc in range(SUMS, KC)], True, False).then_inc(sem("late_done"), 1)

        def early_sums(v):
            pe.wait_ge(sem("sum_done"), v.halves(ADDS))
            sums(v, [psum], False, True).then_inc(sem("den_done"), 1)

        def half(v):
            pe.wait_ge(sem("mrow_ld"), v.halves(64, 64))
            j = 0
            for kc in range(KC):
                for i in range(HG):
                    score(v, HG * kc + i)
                    if i == 1 and (kc or not v.first):
                        values(v, kc - 1)
                    if i == 3 and kc == 0 and not v.first:
                        late_sums(v)
                    if i == 3 and kc == SUMS_AT and not v.first:
                        early_sums(v)
                    proj, quarter = v.piece(kc, i)
                    if proj:
                        m, ph = proj
                        project_unit(m, ph, (1 + v.b + v.h) % 2, (quarter,), v.projected(ph + 2 * (1 - m) if v.hf else 0),
                                     v.g * 48 + (96 if v.h else 48))
                    for kind in v.after(kc, i):
                        if kind[0] == "smax" and kind[2] in (0, 2) and kind[3:] == (0, 0):
                            unit = v.g * 192 + ((v.h + kind[1]) // 2 * 96 + 96)
                            pe.wait_ge(sem(f"k_stack_{kind[2] // 2}"), unit)
                            pe.wait_ge(sem(f"q_stack_{kind[2] // 2}"), unit)
                        pe.wait_ge(sem("wk_done"), v.number(v.bank_before(j) + 1))
                        use(j, kind, v.slot, v.halves(1, 2))
                        j += 1

        def end(v):
            values(v, -1)
            late_sums(v)
            early_sums(v)

        all_halves(pe, half, end)

        pe.wait_ge(sem("wk_done"), Half(NG - 1, 4, True).number(0))
        pe.wait_ge(sem("exp_done"), 4 * NG * HG * KC)
        pe.wait_ge(sem("pj_done"), len(PRO_PROJ) + 4 * (2 * NG - 2))
        pe.wait_ge(sem("wo_ld"), 32)

        def project(i):
            for t in range(4 * i, 4 * i + 4):
                pe.wait_ge(sem("at_lo"), t + 1)
                if t >= 3:
                    pe.wait_ge(sem("y_done"), t - 2)
                split3(bank[(0, 1, 4)[t % 3]], lambda a, dc: at[t % 2][a][:, dc, :],
                       lambda p, dc: wo[p][:, dc, :]).then_inc(sem("o_full"), 1)

        def turn_x1(i):
            for t in range(4 * i, 4 * i + 4):
                pe.wait_ge(sem("x1_rdy"), t + 1)
                if t >= 2:
                    pe.wait_ge(sem("x1_lo"), t - 1)
                turn(x1_bank(t), rows[:, t]).then_inc(sem("x1_t"), 1)

        def logits(i):
            pe.wait_ge(sem("x1_lo"), 4 * i + 4)
            if i >= 2:
                pe.wait_ge(sem("lg_ev"), i - 1)
            split3(bank[6 + i % 2], lambda a, dc: wgp[a][:, dc, :],
                   lambda p, dc: xT[p][:, dc, i * 512:(i + 1) * 512]).then_inc(sem("lg_full"), 1)

        def up_half(c, half, width, rhs):
            return split3(bank[2 * (c % 2) + half][:, 0:width], lambda a, dc: w13[c][a][:, half, dc, :], rhs)

        def up(c, q, sets, width, rhs):
            pe.wait_ge(sem("conv13"), sets + (c + 1))
            pe.wait_ge(sem("h_done"), q + (c + 1))
            mm = up_half(c, 0, width, rhs)
            if c < FC - 1:
                mm = up_half(c, 1, width, rhs)
            mm.then_inc(sem("ab_full"), 1)

        def down(c, q, sets, width):
            pe.wait_ge(sem("hid_lo"), q + (c + 3))
            pe.wait_ge(sem("conv2"), sets + (c + 1))
            p0 = tail(c)
            for i in range(width // P):
                for k, (a, p) in enumerate(SPLIT):
                    mm = nc.tensor.matmul(bank[4 + i], hid[c % 2][a][p0:P, i * P:(i + 1) * P], w2[p][p0:P, c, :],
                                          start=c == 0 and k == 0, stop=c == FC - 1 and k == 2)
            mm.then_inc(sem("used2"), 1)

        def turn_slots(i):
            pe.wait_ge(sem("h_done"), i * FC + (FC + 2))
            for j in range(4):
                pe.wait_ge(sem(f"xd_ld{j}"), i * 16 + 16)
                turn(bank[j], xdi[j]).then_inc(sem("xd_t"), 1)

        def tokens(i):
            return lambda p, dc: xT[p][:, dc, i * 512:(i + 1) * 512] if isinstance(i, int) else xT[p][:, dc, bass.ds(i * 512, 512)]

        def shared_from(c0, i):
            for c in range(c0, FC):
                if c == 0:
                    pe.wait_ge(sem("xd_lo"), i * 4)
                up(c, i * FC, 0, 512, tokens(i))
                if c == 1:
                    pe.wait_ge(sem("acc_done"), i * 4)
                if c:
                    down(c - 1, i * FC, 0, 512)
            turn_slots(i)
            down(FC - 1, i * FC, 0, 512)

        for i in range(4):
            project(i)
            if i >= 2:
                logits(i - 2)
            if i:
                turn_x1(i - 1)
        turn_x1(3)
        pe.wait_ge(sem("y_done"), NT)
        up(0, 0, 0, 512, tokens(0))
        logits(2)
        logits(3)
        pe.wait_ge(sem("conv13"), 2)
        pe.wait_ge(sem("x1_lo"), NT)
        up_half(1, 0, 512, tokens(0))
        pe.wait_ge(sem("lg_ev"), 4)
        for t in range(NT):
            mm = nc.tensor.transpose(bank[6][:, t * E:(t + 1) * E], lgT[:, t * P:(t + 1) * P], ident[0:E, 0:E])
        mm.then_inc(sem("rt_mm"), 1)
        up_half(1, 1, 512, tokens(0)).then_inc(sem("ab_full"), 1)
        pe.wait_ge(sem("rt_const"), 2)
        pe.wait_ge(sem("oh_rdy"), 1)
        choices = oh_bf[:].rearrange("p t e -> p (t e)")
        nc.tensor.matmul(bank[7][:, 0:P], tri[:], choices, start=True, stop=True)
        nc.tensor.matmul(bank[7][:, P:2 * P], allone[:], choices, start=True, stop=True).then_inc(sem("rt_mm"), 1)
        up(2, 0, 0, 512, tokens(0))
        pe.wait_ge(sem("pos_rdy"), 1)
        down(0, 0, 0, 512)
        down(1, 0, 0, 512)
        for c in range(3, FC):
            up(c, 0, 0, 512, tokens(0))
            down(c - 1, 0, 0, 512)
        turn_slots(0)
        down(FC - 1, 0, 0, 512)
        with pe.Fori(1, 4) as i:
            shared_from(0, i)
        pe.wait_ge(sem("xd_lo"), NT)
        pe.wait_ge(sem("acc_done"), NT)

        def up_slots(c, e, plus=0):
            up(c, e * FC + (4 + plus) * FC, e * FC + (1 + plus) * FC, CAP,
               lambda p, dc: xT[p][:, dc, bass.ds(e * CAP + plus * CAP, CAP)])

        def expert(e, last=False):
            q, sets = e * FC + 4 * FC, e * FC + FC
            for c in range(1, FC):
                up_slots(c, e)
                if c == 1:
                    pe.wait_ge(sem("oe_rdy"), e * 2 + 2)
                down(c - 1, q, sets, CAP)
            if not last:
                up_slots(0, e, 1)
            down(FC - 1, q, sets, CAP)

        up_slots(0, 0)
        with pe.Fori(0, E - 1) as e:
            expert(e)
        expert(E - 1, last=True)

    @block.scalar
    def _(ac):
        ACTV = nc.scalar.activation
        ac.sem_inc(sem("oe_rdy"), 2)

        def turned(i, j, src, full, done):
            ac.wait_ge(sem(full[0]), i * 4 + (j + 1 + full[1]))
            ACTV(xT[0][:, :, cols(i, j)], src.rearrange("p (c n) -> p c n", c=DC), ACT.Identity).then_inc(sem(done), 1)

        for n, m in enumerate(W_ORDER):
            ac.wait_ge(sem("a_t"), n + 1)
            ACTV(lora_at[32 * m:32 * m + RANK, :], bank[n][0:RANK, :], ACT.Copy, scale=LORA).then_inc(sem("a_ev"), 1)

        def weights(n, start=0, stop=DC):
            for dc in range(start, stop):
                k = n * DC + dc
                ac.wait_ge(sem("w_mm"), k + 1)
                if k >= DC + 2:
                    ac.wait_ge(sem(f"w_st{k % 2}_0"), 16 * ((k - DC) // 2))
                ACTV(wv[0][:, dc, :] if n == 0 else w_stage[k % 2][0][:], w_bank(k),
                     ACT.Identity).then_inc(sem("w_hi"), 1)

        def turned_x(i):
            for j in range(4):
                turned(i, j, bank[j], ("x_t", 0), "x_hi")

        weights(0)
        turned_x(0)
        weights(1)
        turned_x(1)
        weights(2)
        turned_x(2)
        turned_x(3)

        def plane_hi(m, ph, n, slot_need, stack_need):
            ac.wait_ge(sem("pj_full"), n)
            ac.wait_ge(sem("qk"[m] + "_ld"), slot_need)
            if stack_need is not None:
                for pair in range(HG // 2):
                    ac.wait_ge(sem(f"{'qk'[m]}_stack_{pair}"), stack_need)
            ACTV(plane[m][0][:, ph * HALF:(ph + 1) * HALF], pj, ACT.Identity,
                 bias=bcol[:, m:m + 1]).then_inc(sem("pl_hi"), 1)

        for n, (m, ph) in enumerate(PRO_PROJ[:4]):
            plane_hi(m, ph, n + 1, 48, None)
            weights(3, n, n + 1)
        for i in range(2):
            for s in range(2):
                ac.wait_ge(sem(f"w_st{i}_{s}"), 16 * 6)
            ac.wait_ge(sem(f"v_st{i}"), 16 * NT // 2)
        for n, (m, ph) in enumerate(PRO_PROJ[4:]):
            plane_hi(m, ph, n + 5, 48, 96)

        def half(v):
            for kc in range(KC):
                if kc >= RING or not v.first:
                    ac.wait_ge(sem("pv_done"), v.halves(KC, kc - RING + 1))
                if kc >= RING:
                    ac.wait_ge(sem("sum_done"), v.halves(ADDS, max(2, 2 * (kc - RING))))
                elif not v.first:
                    held = KC - RING + kc
                    if held < SUMS:
                        ac.wait_ge(sem("sum_done"), v.halves(ADDS, 2 * held - ADDS))
                    else:
                        ac.wait_ge(sem("late_done"), v.halves(1))
                for hh in range(HG):
                    i = HG * kc + hh
                    ac.wait_ge(sem("st_full"), v.halves(HG * KC, i + 1))
                    ACTV(prob[kc % RING][:, hh, :], score_bank[i % SCORE], ACT.Exp, scale=SCALE).then_inc(sem("exp_done"), 1)
                    if kc == 0 and hh == HG - 1 and not v.first:
                        take_ov(v)
                    if hh == 2 and kc - 1 in v.proj:
                        m, ph = v.proj[kc - 1]
                        plane_hi(m, ph, v.projected(1 + (ph + 2 * (1 - m) if v.hf else 0)), v.g * 48 + (96 if v.h else 48),
                                 v.units(96, 96 * (1 + v.hf)))

        def take_ov(v):
            hf = 1 - v.hf
            ac.wait_ge(sem("pv_done"), v.halves(KC))
            ac.wait_ge(sem(f"at_st{hf}"), v.g * 32 + (16 * ((v.h - 1) // 2) + 16))
            ACTV(attn_sb[hf][:], ov, ACT.Copy).then_inc(sem("ov_read"), 1)

        def at_hi(t):
            ac.wait_ge(sem(f"at_ld{t % 4}"), t // 4 * 16 + 16)
            if t >= 2:
                ac.wait_ge(sem("o_full"), t - 1)
            ACTV(at[t % 2][0][:], at_in[t % 4][:], ACT.Identity).then_inc(sem("at_hi"), 1)

        def end(v):
            at_hi(0)
            at_hi(1)
            take_ov(v)

        all_halves(ac, half, end)

        ac.wait_ge(sem("wgp_zero"), 2)
        ac.wait_ge(sem("wg_ld"), 16)
        ACTV(wgp[0][:, :, 0:E], wg_raw[:], ACT.Identity).then_inc(sem("wgp_hi"), 1)

        def x1_hi(i):
            for j in range(4):
                turned(i, j, x1_bank(4 * i + j), ("x1_t", 0), "x1_hi")

        def take_logits(i):
            ac.wait_ge(sem("lg_full"), i + 1)
            ACTV(lgT[:, i * 512:(i + 1) * 512], bank[6 + i % 2][0:E, :], ACT.Copy).then_inc(sem("lg_ev"), 1)

        def root(k, name):
            ac.wait_ge(sem(name + "_var"), k)
            ACTV(ln_s[:], ln_v[:], ACT.Sqrt).then_inc(sem(name + "_root"), 1)

        def conv(kind, c, sets, need):
            if kind == 13:
                ac.wait_ge(sem(f"raw13_ld{c % 2}"), sets * 96 + 32 * (c // 2 + 1))
                if need is not None:
                    ac.wait_ge(sem("ab_full"), need + (c + 1))
                ACTV(w13[c][0][:], raw13[c % 2][:, 0:1 + (c < FC - 1)], ACT.Identity).then_inc(sem("conv13_hi"), 1)
            else:
                ac.wait_ge(sem(f"raw2_ld{c % 2}"), sets * 48 + 16 * (c // 2 + 1))
                if need is not None:
                    ac.wait_ge(sem("used2"), need + (c + 3))
                ACTV(w2[0][tail(c):P, c], raw2[c % 2][tail(c):P, :], ACT.Identity).then_inc(sem("conv2_hi"), 1)

        def step(c, q, width):
            r, p0 = c % 2, tail(c)
            ac.wait_ge(sem("ab_full"), q + (c + 1))
            ac.wait_ge(sem("hid_lo"), q + (c + 1))
            ACTV(sa[r][p0:P, 0:width], bank[2 * r][0:P - p0, 0:width], ACT.Silu).then_inc(sem("sa_rdy"), 1)
            ac.wait_ge(sem("h_done"), q + (c + 3))
            ac.wait_ge(sem("used2"), q + (c + 1))
            ACTV(hid[r][0][p0:P, 0:width], sa[r][p0:P, 0:width], ACT.Identity).then_inc(sem("hid_hi"), 1)

        def steps(q, width, own, ahead, between=None):
            for c in range(FC):
                step(c, q, width)
                if c == 0 and between is not None:
                    take_oe(between)
                for kind, cc in CONV_OWN.get(c, ()) if own else ():
                    conv(kind, cc, *own)
                for kind, cc in CONV_BEFORE.get(c, ()) if ahead else ():
                    conv(kind, cc, *ahead)

        def slots_hi(i):
            for j in range(4):
                turned(i, j, bank[j], ("xd_t", 0), "xd_hi")

        for i in range(4):
            for t in range(4 * i + 2, min(4 * i + 6, NT)):
                at_hi(t)
            if i >= 2:
                take_logits(i - 2)
            if i:
                x1_hi(i - 1)
            root(i + 1, "ln1")
            if i in FIRST_PROJ:
                conv(13, FIRST_PROJ[i], 0, None)
        x1_hi(3)
        step(0, 0, 512)
        take_logits(2)
        take_logits(3)
        ac.wait_ge(sem("rt_d"), 1)
        ACTV(r3["ex"][:], r3["d"][:], ACT.Exp).then_inc(sem("rt_ex"), 1)
        ac.wait_ge(sem("xd_zero"), 16)
        for c in range(FC):
            if c:
                step(c, 0, 512)
            for kind, cc in FIRST.get(c, ()):
                conv(kind, cc, 0, None)
        slots_hi(0)
        with ac.Fori(1, 3) as i:
            steps(i * FC, 512, None, None)
            slots_hi(i)
        steps(3 * FC, 512, None, (1, 3 * FC))
        slots_hi(3)

        def take_oe(after):
            ac.wait_ge(sem("used2"), after * FC + (4 * FC + 2))
            for i in range(2):
                if not (isinstance(after, int) and after == 1):
                    ac.wait_ge(sem(f"oe_st{i}"), after * 16 - 16)
                ACTV(oe_sb[i][:], bank[4 + i], ACT.Copy,
                     scale=gate_sb[:, bass.ds(after * 2 - 2 + i, 1)]).then_inc(sem("oe_rdy"), 1)

        def expert(e, first=False, last=False):
            steps(e * FC + 4 * FC, CAP, (e + 1, e * FC + 3 * FC), None if last else (e + 2, e * FC + 4 * FC),
                  None if first else e)

        ac.wait_ge(sem("gate_ld"), 16)
        expert(0, first=True)
        expert(1)
        with ac.Fori(2, E - 1) as e:
            expert(e)
        expert(E - 1, last=True)
        take_oe(E)
        for k in range(4):
            root(k + 1, "ln2")
            ac.wait_ge(sem("ln2_shift"), k + 1)
            for j in range(4):
                t, (scale, shift) = 4 * k + j, ln_rb[k % 2]
                ACTV(rows[:, t], rows[:, t], ACT.Identity, scale=scale[:, j:j + 1],
                     bias=shift[:, j:j + 1]).then_inc(sem("out_rdy"), 1)

    @block.vector
    def _(ve):
        TT, TS, RED = nc.vector.tensor_tensor, nc.vector.tensor_scalar, nc.vector.tensor_reduce
        ve.sem_inc(sem("at_done"), 1)
        ve.sem_inc(sem("h_done"), 2)
        ve.sem_inc(sem("hid_lo"), 2)
        for i in range(2):
            ve.sem_inc(sem(f"at_st{i}"), 16)

        def turned(i, j, src, hi, lo):
            ve.wait_ge(sem(hi), i * 4 + (j + 1))
            TT(xT[1][:, :, cols(i, j)], src.rearrange("p (c n) -> p c n", c=DC), f32(xT[0][:, :, cols(i, j)]),
               ALU.subtract).then_inc(sem(lo), 1)

        def weights(n, start=0, stop=DC):
            for dc in range(start, stop):
                k = n * DC + dc
                hi, lo = (wv[s][:, dc, :] if n == 0 else w_stage[k % 2][s][:] for s in range(2))
                ve.wait_ge(sem("w_hi"), k + 1)
                if k >= DC + 2:
                    ve.wait_ge(sem(f"w_st{k % 2}_1"), 16 * ((k - DC) // 2))
                TT(lo, w_bank(k), f32(hi), ALU.subtract).then_inc(sem("w_lo"), 1)

        def turned_x(i):
            for j in range(4):
                turned(i, j, bank[j], "x_hi", "x_lo")

        def make_v(i):
            for t in range(4 * i, 4 * i + 4):
                ve.wait_ge(sem("v_mm"), t + 1)
                if t >= 2:
                    ve.wait_ge(sem(f"v_st{t % 2}"), 16 * (t // 2))
                TT(v_sb[t % 2][:], bank[6 + t % 2], bv_bc[:], ALU.add).then_inc(sem("v_done"), 1)

        weights(0)
        turned_x(0)
        weights(1)
        ve.wait_ge(sem("bv_ld"), 16)
        make_v(0)
        turned_x(1)
        weights(2)
        make_v(1)
        for i in (2, 3):
            turned_x(i)
            make_v(i)

        def plane_lo(m, ph, n):
            part = slice(ph * HALF, (ph + 1) * HALF)
            ve.wait_ge(sem("pl_hi"), n)
            nc.vector.scalar_tensor_tensor(out=plane[m][1][:, part], in0=pj, scalar=bcol[:, m:m + 1],
                                           in1=f32(plane[m][0][:, part]), op0=ALU.add,
                                           op1=ALU.subtract).then_inc(sem("pj_done"), 1)

        def use(kind, j, n, hf, stack_need):
            src = work[j % WORK]
            ve.wait_ge(sem("wk_full"), n)
            if kind[0] == "smax":
                _, ahead, hh, qt, part = kind
                ins = RED(mx[(hf + ahead) % 2][:, 4 * hh + qt, part:part + 1], src, AX.X, ALU.max)
            else:
                if stack_need is not None:
                    ve.wait_ge(sem("mrow_ld"), stack_need)
                ins = nc.vector.tensor_copy(mrow[:], src[0:16, 0:P])
            ins.then_inc(sem("wk_done"), 1)
            if kind == LAST_SMAX:
                ve.wait_ge(sem("wk_done"), n)
                RED(nm[:], mx[1 - hf][:], AX.X, ALU.max, negate=True).then_inc(sem("nm_rdy"), 1)

        for n, (m, ph) in enumerate(PRO_PROJ[:4]):
            plane_lo(m, ph, n + 1)
            weights(3, n, n + 1)
        for n, kind in enumerate(PRO_USES):
            use(kind, n, n + 1, 1, None)
            if n - 1 in PRO_PLACE:
                i = 4 + PRO_PLACE.index(n - 1)
                plane_lo(*PRO_PROJ[i], i + 1)

        def half(v):
            j = 0
            for kc, uses in enumerate(v.plan):
                for kind in uses:
                    use(kind, j, v.number(j + 1), v.hf, v.halves(64, 64))
                    j += 1
                if kc - 1 in v.proj:
                    m, ph = v.proj[kc - 1]
                    plane_lo(m, ph, v.projected(1 + (ph + 2 * (1 - m) if v.hf else 0)))
                if 3 <= kc < 7 and not v.first:
                    invert(v, kc - 3, kc - 2)
                    if kc == 6:
                        norm_out(v)

        def invert(v, start, stop):
            if start == 0:
                ve.wait_ge(sem("den_done"), v.halves(1))
            for q in range(start, stop):
                nc.vector.reciprocal(rden[:, q * P:(q + 1) * P], dn[:, q * P:(q + 1) * P]).then_inc(sem("rden"), 1)

        def norm_out(v):
            hf = 1 - v.hf
            ve.wait_ge(sem("rden"), v.halves(4))
            ve.wait_ge(sem("ov_read"), v.halves(1))
            TT(attn_sb[hf][:], attn_sb[hf][:], rden[:], ALU.mult).then_inc(sem("at_done"), 1)

        def at_rest(t):
            ve.wait_ge(sem("at_hi"), t + 1)
            TT(at[t % 2][1][:], at_in[t % 4][:], f32(at[t % 2][0][:]), ALU.subtract).then_inc(sem("at_lo"), 1)

        def end(v):
            at_rest(0)
            at_rest(1)
            invert(v, 0, 4)
            norm_out(v)

        all_halves(ve, half, end)

        ve.wait_ge(sem("wgp_hi"), 1)
        TT(wgp[1][:, :, 0:E], wg_raw[:], f32(wgp[0][:, :, 0:E]), ALU.subtract).then_inc(sem("wgp_lo"), 1)

        def row(t):
            return rows[:, bass.ds(t, 1), :].rearrange("p o d -> p (o d)")

        def variances(link, name):
            for j in range(4):
                ins = nc.vector.bn_aggr(mv[:, j], st6[:, j])
            link(ins)
            TS(ln_v[:], mv[:, :, 1], EPS, None, ALU.add).then_inc(sem(name + "_var"), 1)

        def scales(link, k, name, out=ln_r):
            ve.wait_ge(sem(name + "_root"), k)
            link(nc.vector.reciprocal(ln_r[:], ln_s[:]))
            link(TT(ln_t[:], ln_r[:], ln_r[:], ALU.mult))
            link(TT(ln_t[:], ln_t[:], ln_v[:], ALU.mult))
            link(TS(ln_t[:], ln_t[:], -0.5, 1.5, ALU.mult, ALU.add))
            link(TT(out[:], ln_r[:], ln_t[:], ALU.mult))

        def tiles(i, link):
            for j in range(4):
                t = 4 * i + j
                ve.wait_ge(sem("o_full"), t + 1)
                ve.wait_ge(sem("xb_rdy"), t + 1)
                TT(rows[:, t], bank[(0, 1, 4)[t % 3]], xr[j][:], ALU.add).then_inc(sem("y_done"), 1)
                if t + 2 < NT:
                    at_rest(t + 2)
                ve.wait_ge(sem("y_done"), t + 1)
                link(nc.vector.bn_stats(st6[:, j], rows[:, t]))

        def x1_rest(i):
            for j in range(4):
                turned(i, j, x1_bank(4 * i + j), "x1_hi", "x1_lo")

        def conv(kind, c, sets):
            if kind == 13:
                ve.wait_ge(sem("conv13_hi"), sets * FC + (c + 1))
                TT(w13[c][1][:], raw13[c % 2][:, 0:1 + (c < FC - 1)], f32(w13[c][0][:]), ALU.subtract).then_inc(sem("conv13"), 1)
            else:
                ve.wait_ge(sem("conv2_hi"), sets * FC + (c + 1))
                p0 = tail(c)
                TT(w2[1][p0:P, c], raw2[c % 2][p0:P, :], f32(w2[0][p0:P, c]), ALU.subtract).then_inc(sem("conv2"), 1)

        def step(c, q, width):
            r, p0 = c % 2, tail(c)
            gated = bank[2 * r + 1] if c < FC - 1 else bank[2 * r]
            ve.wait_ge(sem("sa_rdy"), q + (c + 1))
            TT(sa[r][p0:P, 0:width], gated[p0:P, 0:width], sa[r][p0:P, 0:width], ALU.mult).then_inc(sem("h_done"), 1)
            ve.wait_ge(sem("hid_hi"), q + (c + 1))
            TT(hid[r][1][p0:P, 0:width], sa[r][p0:P, 0:width], f32(hid[r][0][p0:P, 0:width]),
               ALU.subtract).then_inc(sem("hid_lo"), 1)

        link = Chain(ve, sem("ln1_chain"))
        for i in range(4):
            tiles(i, link)
            variances(link, "ln1")
            if i:
                x1_rest(i - 1)
            scales(link, i + 1, "ln1")
            for j in range(4):
                t = 4 * i + j
                TS(rows[:, t], rows[:, t], mv[:, j, 0:1], ln_r[:, j:j + 1], ALU.subtract, ALU.mult).then_inc(sem("x1_rdy"), 1)
            if i in FIRST_PROJ:
                conv(13, FIRST_PROJ[i], 0)
        x1_rest(3)
        step(0, 0, 512)

        def over_e(t):
            return t[:].unsqueeze(2).to_broadcast([P, NT, E])

        def by_t(b, k=0):
            return b[:, k * P:(k + 1) * P].rearrange("p (t e) -> p t e", e=E)

        link = Chain(ve, sem("rt_chain"))
        ve.wait_ge(sem("rt_mm"), 1)
        nc.vector.tensor_copy(r3["lg"][:], by_t(bank[6])).then_inc(sem("lg_read"), 1)
        ve.wait_ge(sem("lg_read"), 1)
        link(RED(r2["mx"][:], r3["lg"][:], AX.X, ALU.max))
        TT(r3["d"][:], r3["lg"][:], over_e(r2["mx"]), ALU.subtract).then_inc(sem("rt_d"), 1)
        ve.wait_ge(sem("rt_d"), 1)
        ve.wait_ge(sem("iota"), 1)
        link(nc.vector.scalar_tensor_tensor(out=r3["c"][:], in0=r3["d"][:], scalar=0.0, in1=r3["io"][:],
                                            op0=ALU.is_equal, op1=ALU.mult))
        link(RED(r2["em"][:], r3["c"][:], AX.X, ALU.min))
        link(TT(r3["oh"][:], r3["io"][:], over_e(r2["em"]), ALU.is_equal))
        nc.vector.tensor_copy(oh_bf[:], r3["oh"][:]).then_inc(sem("oh_rdy"), 1)
        ve.wait_ge(sem("rt_ex"), 1)
        link(RED(r2["sm"][:], r3["ex"][:], AX.X, ALU.add))
        link(nc.vector.reciprocal(r2["gate"][:], r2["sm"][:]))
        ve.wait_ge(sem("rt_mm"), 2)
        link(nc.vector.memset(r3["s0"][:, 0:1, :], 0.0))
        link(nc.vector.tensor_copy(r3["s0"][:, 1:NT, :], by_t(bank[7], 1)[:, 0:NT - 1, :]))
        a, b = "s0", "s1"
        for k in (1, 2, 4, 8):
            nc.vector.tensor_copy(r3[b][:, 0:k, :], r3[a][:, 0:k, :])
            link(TT(r3[b][:, k:NT, :], r3[a][:, k:NT, :], r3[a][:, 0:NT - k, :], ALU.add))
            a, b = b, a
        TT(r3["c"][:], by_t(bank[7]), r3[a][:], ALU.add).then_inc(sem("pos_rdy"), 1)
        ve.wait_ge(sem("pos_rdy"), 1)
        link(TT(r3["c"][:], r3["c"][:], r3["oh"][:], ALU.mult))
        link(RED(r2["ps"][:], r3["c"][:], AX.X, ALU.add))
        link(TS(r2["keep"][:], r2["ps"][:], float(CAP), None, ALU.is_le))
        link(nc.vector.scalar_tensor_tensor(out=r2["flat"][:], in0=r2["em"][:], scalar=float(CAP), in1=r2["ps"][:],
                                            op0=ALU.mult, op1=ALU.add))
        link(TS(r2["t"][:], r2["keep"][:], -2.0 * E * CAP, 3.0 * E * CAP - 1.0, ALU.mult, ALU.add))
        link(TT(r2["t"][:], r2["t"][:], r2["flat"][:], ALU.add))
        link(nc.vector.tensor_copy(sidx[:], r2["t"][:]))
        link(TS(r2["u"][:], r2["t"][:], (E - 1.0) * CAP, 2.0 * E * CAP, ALU.is_lt, ALU.mult))
        link(TT(r2["u"][:], r2["u"][:], r2["t"][:], ALU.add))
        nc.vector.tensor_copy(lidx[:], r2["u"][:]).then_inc(sem("routed"), 1)

        def steps(q, width, own, ahead):
            for c in range(FC):
                step(c, q, width)
                for kind, cc in CONV_OWN.get(c, ()) if own is not None else ():
                    conv(kind, cc, own)
                for kind, cc in CONV_BEFORE.get(c, ()) if ahead is not None else ():
                    conv(kind, cc, ahead)

        def slots_lo(i):
            for j in range(4):
                turned(i, j, bank[j], "xd_hi", "xd_lo")

        def add_shared(i):
            ve.wait_ge(sem("used2"), i * FC + (FC + 2))
            for j in range(4):
                TT(row(i * 4 + j), bank[4 + j], row(i * 4 + j), ALU.add).then_inc(sem("acc_done"), 1)

        for c in range(FC):
            if c:
                step(c, 0, 512)
            for kind, cc in FIRST.get(c, ()):
                conv(kind, cc, 0)
        slots_lo(0)
        add_shared(0)
        with ve.Fori(1, 3) as i:
            steps(i * FC, 512, None, None)
            slots_lo(i)
            add_shared(i)
        steps(3 * FC, 512, None, 1)
        slots_lo(3)
        add_shared(3)
        with ve.Fori(0, E - 1) as e:
            steps(e * FC + 4 * FC, CAP, e + 1, e + 2)
        steps((E + 3) * FC, CAP, E, None)

        link = Chain(ve, sem("ln2_chain"))
        for k in range(4):
            for j in range(4):
                t = 4 * k + j
                ve.wait_ge(sem(f"all_added{t}"), 16)
                link(nc.vector.bn_stats(st6[:, j], rows[:, t]))
            variances(link, "ln2")
            scale, shift = ln_rb[k % 2]
            if k >= 2:
                ve.wait_ge(sem("out_rdy"), 4 * (k - 1))
            scales(link, k + 1, "ln2", scale)
            nc.vector.scalar_tensor_tensor(out=shift[:], in0=mv[:, :, 0], scalar=-1.0, in1=scale[:], op0=ALU.mult,
                                           op1=ALU.mult).then_inc(sem("ln2_shift"), 1)
            if k < 3:
                ve.wait_ge(sem("ln2_shift"), k + 1)


_INS = ["L0_attn_x"] + [f"L0_attn_{k}{m}" for m in "qkvo" for k in "WbBA"] + [
    "L0_ffn_Wg", "L0_ffn_W1", "L0_ffn_W3", "L0_ffn_W2", "L0_ffn_sw1", "L0_ffn_sw3", "L0_ffn_sw2"]
_OUTS = [((B, L, D), "float32")]


def build(nc, args):
    by_name = dict(zip(_INS + ["out"], args))
    per = {k: [by_name[f"L0_attn_{k}{m}"] for m in "qkvo"] for k in "WbBA"}
    ff = [by_name[f"L0_ffn_{n}"] for n in ("Wg", "W1", "W3", "W2", "sw1", "sw3", "sw2")]
    with ExitStack() as ctx:
        emit(nc, ctx, by_name["L0_attn_x"], per["W"], per["b"][:3], per["b"][3], per["B"], per["A"], *ff, by_name["out"])


def kernel(**inputs):
    import numpy as _np
    import concourse.bacc as _bacc
    from concourse import mybir as _mybir
    from concourse.bass_utils import run_bass_kernel_spmd as _run

    nc = _bacc.Bacc("TRN2", target_bir_lowering=False, num_devices=1)
    arrays, args = {}, []
    for name in _INS:
        a = _np.ascontiguousarray(inputs[name])
        arrays[f"in_{name}_dram"] = a
        args.append(nc.dram_tensor(f"in_{name}_dram", a.shape, _mybir.dt.from_np(a.dtype), kind="ExternalInput").ap())
    for i, (shape, dtype) in enumerate(_OUTS):
        dt = _mybir.dt.from_np(_np.dtype(dtype))
        args.append(nc.dram_tensor(f"out_{i}_dram", shape, dt, kind="ExternalOutput").ap())
    build(nc, args)
    r = _run(nc, [arrays], core_ids=[0])
    return r.results[0]["out_0_dram"]
```
